# Optimizing a Trainium2 kernel written in Bass

```python
import numpy as np
import jax
import jax.numpy as jnp

def _softmax(x, axis=-1):
    return jax.nn.softmax(x, axis=axis)

def _gelu(x):
    return jax.nn.gelu(x, approximate=True)

def _silu(x):
    return jax.nn.silu(x)

def _sigmoid(x):
    return jax.nn.sigmoid(x)

def _layernorm(x, axis=-1, eps=1e-05):
    m = jnp.mean(x, axis=axis, keepdims=True)
    v = jnp.var(x, axis=axis, keepdims=True)
    return (x - m) / jnp.sqrt(v + eps)

def _scatter_add(tgt, idx, src, axis=0):
    return tgt.at[idx].add(src)

def _segment_sum(src, seg, n):
    return jax.ops.segment_sum(src, seg, n)
kernel_name = 'mk_flamingo_gated_d2_seqx_r2_990571'

def setup_inputs(seed: int=0):
    np.random.seed(seed)
    _w = jnp.asarray

    def _rec_inputs():
        import jax
        import jax.numpy as jnp
        _rk = jax.random.key(seed)
        x = 0.002226 + 0.9996 * jax.random.normal(jax.random.fold_in(_rk, 1), (8, 100, 512), jnp.float32)
        _lenS = 100 - jax.random.randint(jax.random.fold_in(_rk, 7), (8,), 0, max(1, 100 // 4) + 1, jnp.int32)
        _lenS2 = 722 - jax.random.randint(jax.random.fold_in(_rk, 8), (8,), 0, max(1, 722 // 4) + 1, jnp.int32)
        _ctx_1024P = jax.random.normal(jax.random.fold_in(_rk, 11), (8, 16, 512), jnp.float32)
        _ctx_1024c = jax.random.dirichlet(jax.random.fold_in(_rk, 511), 0.3 * jnp.ones((16,), jnp.float32), (8, 722))
        _ctx_1024t = jnp.einsum('bsk,bkd->bsd', _ctx_1024c, _ctx_1024P)
        _ctx_1024t = _ctx_1024t * jax.lax.rsqrt(jnp.mean(jnp.square(_ctx_1024t)) + 1e-12) * 0.953939
        ctx_1024 = -0.000125008 + 0.999885 * (_ctx_1024t + 0.3 * jax.random.normal(jax.random.fold_in(_rk, 611), (8, 722, 512), jnp.float32))
        _validS = jnp.arange(100)[None, :] < _lenS[:, None]
        _validS2 = jnp.arange(722)[None, :] < _lenS2[:, None]
        _causal = jnp.tril(jnp.ones((100, 100), dtype=bool))
        mask_BxS2_bk0 = jnp.logical_not(jnp.broadcast_to(_validS2[:, :], (8, 722)))
        _g = jax.random.normal(jax.random.fold_in(_rk, 9001), (2, 2), jnp.float32)
        _g = jnp.sign(_g) * jnp.maximum(jnp.abs(_g), 1.0) + (_g == 0) * 1.0
        g_xattn = _g[0]
        g_ffn = _g[1]
        return (x, ctx_1024, mask_BxS2_bk0, g_xattn, g_ffn)
    x, ctx_1024, mask_BxS2_bk0, g_xattn, g_ffn = _rec_inputs()

    def _L0_xattn_setup():
        import jax, jax.numpy as jnp
        import numpy as np
        DIM = 512
        HEADS = 16
        DIM_HEAD = 64
        INNER = HEADS * DIM_HEAD
        EPS = 1e-05

        def layernorm(t, g, b):
            mu = jnp.mean(t, axis=-1, keepdims=True)
            var = jnp.var(t, axis=-1, keepdims=True)
            return (t - mu) * jax.lax.rsqrt(var + EPS) * g + b
        key = jax.random.key(seed)
        ks = jax.random.split(key, 8)
        b, n, m = (8, 2048, 64)
        x = jax.random.normal(ks[0], (b, n, DIM), dtype=jnp.float32)
        latents = jax.random.normal(ks[1], (b, m, DIM), dtype=jnp.float32)
        mask = jax.random.randint(ks[2], (b, n), 0, 2).astype(bool)
        s = 0.02
        Wq = jax.random.normal(ks[3], (DIM, INNER), dtype=jnp.float32) * s
        Wkv = jax.random.normal(ks[4], (DIM, 2 * INNER), dtype=jnp.float32) * s
        Wout = jax.random.normal(ks[5], (INNER, DIM), dtype=jnp.float32) * s
        ln_x_g = jnp.ones((DIM,), jnp.float32)
        ln_x_b = jnp.zeros((DIM,), jnp.float32)
        ln_l_g = jnp.ones((DIM,), jnp.float32)
        ln_l_b = jnp.zeros((DIM,), jnp.float32)
        ln_o_g = jnp.ones((DIM,), jnp.float32)
        ln_o_b = jnp.zeros((DIM,), jnp.float32)
        return {'x': x, 'latents': latents, 'mask': mask, 'ln_x_g': ln_x_g, 'ln_x_b': ln_x_b, 'ln_l_g': ln_l_g, 'ln_l_b': ln_l_b, 'Wq': Wq, 'Wkv': Wkv, 'Wout': Wout, 'ln_o_g': ln_o_g, 'ln_o_b': ln_o_b}
    _L0_xattn_all = _L0_xattn_setup()
    _L0_xattn_in = {k: v for k, v in _L0_xattn_all.items() if k in ('ln_x_g', 'ln_x_b', 'ln_l_g', 'ln_l_b', 'Wq', 'Wkv', 'Wout', 'ln_o_g', 'ln_o_b')}
    del _L0_xattn_all

    def _L0_ffn_setup():
        import jax, jax.numpy as jnp
        import numpy as np
        B, S, D, F, E, K = (4, 1024, 512, 2048, 4, 2)
        key = jax.random.key(seed)
        k = jax.random.split(key, 6)
        x = jax.random.normal(k[0], (B, S, D), jnp.float32)
        router_w = jax.random.normal(k[1], (D, E), jnp.float32) * D ** (-0.5)
        router_b = jnp.zeros((E,), jnp.float32)
        w1 = jax.random.normal(k[2], (E, D, F), jnp.float32) * 0.02
        w3 = jax.random.normal(k[3], (E, D, F), jnp.float32) * 0.02
        w2 = jax.random.normal(k[4], (E, F, D), jnp.float32) * 0.02
        return {'x': x, 'router_w': router_w, 'router_b': router_b, 'w1': w1, 'w3': w3, 'w2': w2}
    _L0_ffn_all = _L0_ffn_setup()
    _L0_ffn_in = {k: v for k, v in _L0_ffn_all.items() if k in ('router_w', 'router_b', 'w1', 'w3', 'w2')}
    del _L0_ffn_all

    def _L1_xattn_setup():
        import jax, jax.numpy as jnp
        import numpy as np
        E = 512
        H = 16
        D = E // H
        key = jax.random.key(seed)
        ks = jax.random.split(key, 12)
        B, Tq, Tk = (2, 512, 4096)
        s = 0.02
        return {'hidden_states': jax.random.normal(ks[0], (B, Tq, E), jnp.float32), 'key_value_states': jax.random.normal(ks[1], (B, Tk, E), jnp.float32), 'Wq': jax.random.normal(ks[2], (E, E), jnp.float32) * s, 'bq': jnp.zeros((E,), jnp.float32), 'Wk': jax.random.normal(ks[3], (E, E), jnp.float32) * s, 'bk': jnp.zeros((E,), jnp.float32), 'Wv': jax.random.normal(ks[4], (E, E), jnp.float32) * s, 'bv': jnp.zeros((E,), jnp.float32), 'Wo': jax.random.normal(ks[5], (E, E), jnp.float32) * s, 'bo': jnp.zeros((E,), jnp.float32), 'stride': 16}
    _L1_xattn_all = _L1_xattn_setup()
    _L1_xattn_in = {k: v for k, v in _L1_xattn_all.items() if k in ('Wq', 'bq', 'Wk', 'bk', 'Wv', 'bv', 'Wo', 'bo')}
    del _L1_xattn_all

    def _L1_ffn_setup():
        import jax, jax.numpy as jnp
        import numpy as np
        B, S, D = (4, 512, 512)
        E, K = (8, 2)
        H = 2 * D
        key = jax.random.key(seed)
        ks = jax.random.split(key, 5)
        x = jax.random.normal(ks[0], (B, S, D), dtype=jnp.float32)
        Wg = jax.random.normal(ks[1], (E, D), dtype=jnp.float32) * 0.02
        W1 = jax.random.normal(ks[2], (E, H, D), dtype=jnp.float32) * 0.02
        W2 = jax.random.normal(ks[3], (E, H, D), dtype=jnp.float32) * 0.02
        W3 = jax.random.normal(ks[4], (E, D, H), dtype=jnp.float32) * 0.02
        return {'x': x, 'Wg': Wg, 'W1': W1, 'W2': W2, 'W3': W3}
    _L1_ffn_all = _L1_ffn_setup()
    _L1_ffn_in = {k: v for k, v in _L1_ffn_all.items() if k in ('Wg', 'W1', 'W2', 'W3')}
    del _L1_ffn_all
    return {'x': x, 'ctx_1024': ctx_1024, 'mask_BxS2_bk0': mask_BxS2_bk0, 'g_xattn': g_xattn, 'g_ffn': g_ffn, 'L0_xattn_ln_x_g': _L0_xattn_in['ln_x_g'], 'L0_xattn_ln_x_b': _L0_xattn_in['ln_x_b'], 'L0_xattn_ln_l_g': _L0_xattn_in['ln_l_g'], 'L0_xattn_ln_l_b': _L0_xattn_in['ln_l_b'], 'L0_xattn_Wq': _L0_xattn_in['Wq'], 'L0_xattn_Wkv': _L0_xattn_in['Wkv'], 'L0_xattn_Wout': _L0_xattn_in['Wout'], 'L0_xattn_ln_o_g': _L0_xattn_in['ln_o_g'], 'L0_xattn_ln_o_b': _L0_xattn_in['ln_o_b'], 'L0_ffn_router_w': _L0_ffn_in['router_w'], 'L0_ffn_router_b': _L0_ffn_in['router_b'], 'L0_ffn_w1': _L0_ffn_in['w1'], 'L0_ffn_w3': _L0_ffn_in['w3'], 'L0_ffn_w2': _L0_ffn_in['w2'], 'L1_xattn_Wq': _L1_xattn_in['Wq'], 'L1_xattn_bq': _L1_xattn_in['bq'], 'L1_xattn_Wk': _L1_xattn_in['Wk'], 'L1_xattn_bk': _L1_xattn_in['bk'], 'L1_xattn_Wv': _L1_xattn_in['Wv'], 'L1_xattn_bv': _L1_xattn_in['bv'], 'L1_xattn_Wo': _L1_xattn_in['Wo'], 'L1_xattn_bo': _L1_xattn_in['bo'], 'L1_ffn_Wg': _L1_ffn_in['Wg'], 'L1_ffn_W1': _L1_ffn_in['W1'], 'L1_ffn_W2': _L1_ffn_in['W2'], 'L1_ffn_W3': _L1_ffn_in['W3']}

def reference(x, ctx_1024, mask_BxS2_bk0, g_xattn, g_ffn, L0_xattn_ln_x_g, L0_xattn_ln_x_b, L0_xattn_ln_l_g, L0_xattn_ln_l_b, L0_xattn_Wq, L0_xattn_Wkv, L0_xattn_Wout, L0_xattn_ln_o_g, L0_xattn_ln_o_b, L0_ffn_router_w, L0_ffn_router_b, L0_ffn_w1, L0_ffn_w3, L0_ffn_w2, L1_xattn_Wq, L1_xattn_bq, L1_xattn_Wk, L1_xattn_bk, L1_xattn_Wv, L1_xattn_bv, L1_xattn_Wo, L1_xattn_bo, L1_ffn_Wg, L1_ffn_W1, L1_ffn_W2, L1_ffn_W3):
    import jax
    import jax.numpy as jnp

    def _L0_xattn_ref(x, latents, mask, ln_x_g, ln_x_b, ln_l_g, ln_l_b, Wq, Wkv, Wout, ln_o_g, ln_o_b):
        import jax, jax.numpy as jnp
        import numpy as np
        DIM = 512
        HEADS = 16
        DIM_HEAD = 64
        INNER = HEADS * DIM_HEAD
        EPS = 1e-05

        def layernorm(t, g, b):
            mu = jnp.mean(t, axis=-1, keepdims=True)
            var = jnp.var(t, axis=-1, keepdims=True)
            return (t - mu) * jax.lax.rsqrt(var + EPS) * g + b
        b, n, _ = x.shape
        m = latents.shape[1]
        scale = DIM_HEAD ** (-0.5)
        xn = layernorm(x, ln_x_g, ln_x_b)
        ln = layernorm(latents, ln_l_g, ln_l_b)
        q = ln @ Wq
        kv_input = jnp.concatenate((xn, ln), axis=1)
        kv = kv_input @ Wkv
        k, v = jnp.split(kv, 2, axis=-1)

        def heads(t):
            return t.reshape(t.shape[0], t.shape[1], HEADS, DIM_HEAD).transpose(0, 2, 1, 3)
        q, k, v = (heads(q) * scale, heads(k), heads(v))
        sim = jnp.einsum('bhid,bhjd->bhij', q, k)
        mask_full = jnp.concatenate((mask, jnp.ones((b, m), dtype=bool)), axis=1)
        max_neg = -jnp.finfo(sim.dtype).max
        sim = jnp.where(mask_full[:, None, None, :], sim, max_neg)
        attn = jax.nn.softmax(sim.astype(jnp.float32), axis=-1).astype(sim.dtype)
        out = jnp.einsum('bhij,bhjd->bhid', attn, v)
        out = out.transpose(0, 2, 1, 3).reshape(b, m, INNER)
        out = out @ Wout
        return layernorm(out, ln_o_g, ln_o_b)

    def _L0_ffn_ref(x, router_w, router_b, w1, w3, w2):
        import jax, jax.numpy as jnp
        import numpy as np
        B, S, D, F, E, K = (4, 1024, 512, 2048, 4, 2)
        b, s, d = x.shape
        T = b * s
        e = router_w.shape[1]
        xf = x.reshape(T, d)
        logits = xf @ router_w + router_b
        probs = jax.nn.softmax(logits, axis=-1)
        top_p, top_i = jax.lax.top_k(probs, K)
        top_p = top_p / jnp.sum(top_p, axis=-1, keepdims=True)
        gates = jnp.zeros((T, e), xf.dtype).at[jnp.arange(T)[:, None], top_i].add(top_p)
        h = jax.nn.silu(jnp.einsum('td,edf->etf', xf, w1)) * jnp.einsum('td,edf->etf', xf, w3)
        expert_out = jnp.einsum('etf,efd->etd', h, w2)
        out = jnp.einsum('te,etd->td', gates, expert_out)
        return out.reshape(b, s, d)

    def _L1_xattn_ref(hidden_states, key_value_states, Wq, bq, Wk, bk, Wv, bv, Wo, bo, stride):
        import jax, jax.numpy as jnp
        import numpy as np
        E = 512
        H = 16
        D = E // H
        B, Tq, _ = hidden_states.shape
        Tk = key_value_states.shape[1]
        scaling = D ** (-0.5)
        Q = (hidden_states @ Wq.T + bq).reshape(B, Tq, H, D).transpose(0, 2, 1, 3)
        K = (key_value_states @ Wk.T + bk).reshape(B, Tk, H, D).transpose(0, 2, 1, 3)
        V = (key_value_states @ Wv.T + bv).reshape(B, Tk, H, D).transpose(0, 2, 1, 3)
        m = Tk // stride
        idx = jnp.arange(H)[:, None] + stride * jnp.arange(m)[None, :]
        gather = idx[None, :, :, None]
        Kg = jnp.take_along_axis(K, gather, axis=2)
        Vg = jnp.take_along_axis(V, gather, axis=2)
        scores = jnp.einsum('bhqd,bhkd->bhqk', Q, Kg) * scaling
        attn = jax.nn.softmax(scores, axis=-1)
        out = jnp.einsum('bhqk,bhkd->bhqd', attn, Vg)
        out = out.transpose(0, 2, 1, 3).reshape(B, Tq, E)
        return out @ Wo.T + bo

    def _L1_ffn_ref(x, Wg, W1, W2, W3):
        import jax, jax.numpy as jnp
        import numpy as np
        B, S, D = (4, 512, 512)
        E, K = (8, 2)
        H = 2 * D
        gate_out = jnp.einsum('bsd,ed->bse', x, Wg)
        top_v, top_i = jax.lax.top_k(gate_out, K)
        probs = jax.nn.softmax(top_v, axis=-1)
        out = jnp.zeros_like(x)
        for e in range(E):
            w_e = jnp.sum(probs * (top_i == e), axis=-1)
            h1 = jnp.einsum('bsd,hd->bsh', x, W1[e])
            h2 = jnp.einsum('bsd,hd->bsh', x, W2[e])
            g = h1 * jax.nn.sigmoid(h1) * h2
            y = jnp.einsum('bsh,dh->bsd', g, W3[e])
            out = out + y * w_e[..., None]
        return out
    x = x + jnp.tanh(g_xattn[0]) * _L0_xattn_ref(ctx_1024, _layernorm(x, axis=-1), mask_BxS2_bk0, L0_xattn_ln_x_g, L0_xattn_ln_x_b, L0_xattn_ln_l_g, L0_xattn_ln_l_b, L0_xattn_Wq, L0_xattn_Wkv, L0_xattn_Wout, L0_xattn_ln_o_g, L0_xattn_ln_o_b)
    x = x + jnp.tanh(g_ffn[0]) * _L0_ffn_ref(_layernorm(x, axis=-1), L0_ffn_router_w, L0_ffn_router_b, L0_ffn_w1, L0_ffn_w3, L0_ffn_w2)
    x = x + jnp.tanh(g_xattn[1]) * _L1_xattn_ref(_layernorm(x, axis=-1), ctx_1024, L1_xattn_Wq, L1_xattn_bq, L1_xattn_Wk, L1_xattn_bk, L1_xattn_Wv, L1_xattn_bv, L1_xattn_Wo, L1_xattn_bo, 16)
    x = x + jnp.tanh(g_ffn[1]) * _L1_ffn_ref(_layernorm(x, axis=-1), L1_ffn_Wg, L1_ffn_W1, L1_ffn_W2, L1_ffn_W3)
    return x

_drawn_inputs = setup_inputs


def setup_inputs(seed=0):
    import zlib

    import numpy as np

    out = dict(_drawn_inputs(seed))
    spreads = {'g_ffn': (-1.0, 0.6),
     'L0_xattn_ln_x_g': (1.0, 0.2),
     'L0_xattn_ln_x_b': (0.0, 0.1),
     'L0_xattn_ln_l_g': (1.0, 0.2),
     'L0_xattn_ln_l_b': (0.0, 0.1),
     'L0_xattn_ln_o_g': (1.0, 0.2),
     'L0_xattn_ln_o_b': (0.0, 0.1),
     'L0_ffn_router_b': (0.0, 2.0),
     'L1_xattn_bq': (0.0, 0.8),
     'L1_xattn_bk': (0.0, 2.0),
     'L1_xattn_bv': (0.0, 0.1),
     'L1_xattn_bo': (0.0, 0.1)}
    factors = {'L1_xattn_Wq': 8.0, 'L1_xattn_Wk': 8.0}
    for name, (base, spread) in spreads.items():
        noise = np.random.default_rng([zlib.crc32(name.encode()), seed]).standard_normal(out[name].shape)
        drawn = base * np.exp(spread * noise) if base else spread * noise
        out[name] = jnp.asarray(drawn.astype(out[name].dtype))
    for name, factor in factors.items():
        out[name] = (out[name] * factor).astype(out[name].dtype)
    return out
```

```python
import concourse.bass as bass
from concourse import mybir
from contextlib import ExitStack, contextmanager

F32 = mybir.dt.float32
F32R = mybir.dt.float32r
U8 = mybir.dt.uint8
ALU = mybir.AluOpType
ACT = mybir.ActivationFunctionType
AX = mybir.AxisListType


class Chain:

    def __init__(self, eng, sem):
        self.eng, self.sem, self.base, self.n = eng, sem, 1, 0

    def link(self, ins):
        self.n += 1
        ins.then_inc(self.sem, 1)
        self.eng.wait_ge(self.sem, self.base + self.n)

    @contextmanager
    def loop(self, turns, per):
        start = self.base + self.n
        with self.eng.Fori(0, turns) as i:
            self.base, self.n = start + per * i, 0
            yield i
        assert self.n == per, (self.n, per)
        self.base, self.n = start + per * turns, 0


def perceiver_attention(nc, ctx_rows, x_in, keep_mask, ln_x_g, ln_x_b, ln_l_g, ln_l_b, wq, wkv, wout,
                        ln_o_g, ln_o_b, gate, x_out):
    B, M, D = x_in.shape
    N = ctx_rows.shape[1]
    P = 128
    HD = 64
    INNER = wq.shape[1]
    PAIRS = INNER // P
    HALF = INNER // 2
    KD = D // P
    KEYS = N + M
    CT = (N + P - 1) // P
    CROWS = [min(P, N - P * t) for t in range(CT)]
    LAT = CT
    NT = CT + 1
    TILE_ROWS = CROWS + [M]
    TILE_COL = [P * t for t in range(CT)] + [N]
    KT = (KEYS + P - 1) // P
    KROWS = [min(P, KEYS - P * t) for t in range(KT)]
    BANK = 512
    PART = [(0, BANK), (BANK, KEYS - BANK)]
    FIRST_T = 4
    EPS = 1e-5
    FAR = float(2.0 ** 100)
    SCALE = HD ** -0.5

    with ExitStack() as ctx:
        def sb(name, shape, dt=F32):
            return ctx.enter_context(nc.sbuf_tensor("a_" + name, shape, dt))

        def ps(name, shape):
            return ctx.enter_context(nc.psum_tensor("a_" + name, shape, F32))

        def sem(name):
            return nc.alloc_semaphore("a_" + name)

        wkv_hi = sb("wkv_hi", [P, KD, 2 * INNER], F32R)
        wkv_lo = sb("wkv_lo", [P, KD, 2 * INNER], F32R)
        wq_sb = sb("wq_sb", [P, KD, INNER])
        wout_sb = sb("wout_sb", [P, PAIRS, D])
        rows = sb("rows", [P, CT, D])
        lat = sb("lat", [P, D])
        kvin_hi = sb("kvin_hi", [P, KD, KEYS], F32R)
        kvin_lo = sb("kvin_lo", [P, KD, KEYS], F32R)
        val = sb("val", [P, 2, KD, P])
        lat_t = sb("lat_t", [P, KD, M])
        k_hi = sb("k_hi", [P, 2, KEYS], F32R)
        k_lo = sb("k_lo", [P, 2, KEYS], F32R)
        v_sb = sb("v_sb", [P, KT, HALF])
        q_hi = sb("q_hi", [P, PAIRS, 2, M], F32R)
        q_lo = sb("q_lo", [P, PAIRS, 2, M], F32R)
        probs = sb("probs", [P, 2, KT * P])
        probs_t = sb("probs_t", [P, 2, KT * M])
        out_t = sb("out_t", [P, PAIRS, M])
        mask_u8 = sb("mask_u8", [P, N], U8)
        mask_add = sb("mask_add", [P, KEYS])
        res = sb("res", [P, D])
        tail = sb("tail", [P, D])
        gain_o = sb("gain_o", [P, D])
        bias_o = sb("bias_o", [P, D])
        gx, bx, gl, bl = (sb(n, [P, KD]) for n in ("gx", "bx", "gl", "bl"))
        tanh_g = sb("tanh_g", [P, 1])
        eps = sb("eps", [P, 1])
        ident = sb("ident", [P, P])
        stats = sb("stats", [P, NT, 6])
        mean_var = sb("mean_var", [P, NT, 2])
        std = sb("std", [P, NT])
        rstd = sb("rstd", [P, NT])
        neg_max = sb("neg_max", [P, 2])
        row_sum = sb("row_sum", [P, 2])
        row_inv = sb("row_inv", [P, 2])
        stage = v_sb[:, :, :].rearrange("p t n -> p (t n)")
        SW = INNER

        kv_ps = ps("kv_ps", [P, 2 * BANK])
        s_ps = ps("s_ps", [P, 2 * BANK])
        t_ps = ps("t_ps", [P, 2 * BANK])
        o_ps = ps("o_ps", [P, BANK])
        w_ps = ps("w_ps", [P, BANK])

        c_loaded = sem("c_loaded")
        w_loaded = [sem(f"w_loaded{n}") for n in range(2)]
        w_hi_done = sem("w_hi_done")
        w_lo_done = sem("w_lo_done")
        pq_loaded = sem("pq_loaded")
        rows_loaded = sem("rows_loaded")
        mask_loaded = sem("mask_loaded")
        res_loaded = sem("res_loaded")
        x_stored = sem("x_stored")
        const_done = sem("const_done")
        tanh_done = sem("tanh_done")
        mask_done = sem("mask_done")
        var_done = sem("var_done")
        std_done = sem("std_done")
        norm_done = sem("norm_done")
        tr_done = sem("tr_done")
        val_done = sem("val_done")
        in_hi_done = sem("in_hi_done")
        in_lo_done = sem("in_lo_done")
        q_ready = sem("q_ready")
        q_hi_done = sem("q_hi_done")
        q_lo_done = sem("q_lo_done")
        v_ready = sem("v_ready")
        v_done = sem("v_done")
        k_ready = sem("k_ready")
        k_hi_done = sem("k_hi_done")
        k_lo_done = sem("k_lo_done")
        s_ready = sem("s_ready")
        max_done = sem("max_done")
        exp_done = sem("exp_done")
        p_done = sem("p_done")
        t_ready = sem("t_ready")
        ta_done = sem("ta_done")
        tb_done = sem("tb_done")
        o_ready = sem("o_ready")
        o_done = sem("o_done")
        y_ready = sem("y_ready")
        y_read = sem("y_read")
        x_done = sem("x_done")
        held = sem("held")
        chain = sem("chain")

        block = ctx.enter_context(nc.Block())


        @block.sync
        def _(sp):
            for s in (x_stored, rows_loaded, mask_loaded, res_loaded):
                sp.sem_inc(s, 1)

            def load_rows(b):
                full = P * (CT - 1)
                sp.dma_start(rows[:, 0:CT - 1, :], ctx_rows[b, 0:full, :].rearrange("(t p) d -> p t d", p=P)).then_inc(rows_loaded, 16)
                sp.dma_start(rows[0:CROWS[-1], CT - 1, :], ctx_rows[b, full:N, :]).then_inc(rows_loaded, 16)
                sp.dma_start(lat[0:M, :], x_in[b, :, :]).then_inc(rows_loaded, 16)

            def load_mask(b):
                sp.dma_start(mask_u8[0:M, :], keep_mask[b, :].rearrange("(a n) -> a n", a=1).to_broadcast([M, N])).then_inc(mask_loaded, 16)

            def load_res(b):
                sp.dma_start(res[0:M, :], x_in[b, :, :]).then_inc(res_loaded, 16)

            load_rows(0)
            for n, (t, src) in enumerate(((gx, ln_x_g), (bx, ln_x_b), (gl, ln_l_g), (bl, ln_l_b))):
                sp.dma_start(t[:, :], src.rearrange("(k p) -> p k", p=P), allow_slow_non_contiguous=True).then_inc(c_loaded, 16)
            sp.dma_start(gain_o[0:M, :], ln_o_g.rearrange("(a n) -> a n", a=1).to_broadcast([M, D])).then_inc(c_loaded, 16)
            sp.dma_start(bias_o[0:M, :], ln_o_b.rearrange("(a n) -> a n", a=1).to_broadcast([M, D])).then_inc(c_loaded, 16)
            sp.dma_start(tanh_g[:, :], gate.to_broadcast([P, 1])).then_inc(c_loaded, 16)
            sp.dma_start(wq_sb[:, :, :], wq.rearrange("(k p) n -> p k n", p=P)).then_inc(pq_loaded, 16)
            for n in range(2 * KD):
                if n >= 2:
                    sp.wait_ge(w_lo_done, 1 + n - 1)
                sp.dma_start(stage[:, SW * (n % 2):SW * (n % 2 + 1)],
                             wkv[P * (n // 2):P * (n // 2 + 1), SW * (n % 2):SW * (n % 2 + 1)]).then_inc(w_loaded[n % 2], 16)
            sp.dma_start(wout_sb[:, :, :], wout.rearrange("(k p) n -> p k n", p=P)).then_inc(pq_loaded, 16)
            load_mask(0)
            load_res(0)

            def turn(i, last):
                if not last:
                    sp.wait_ge(tr_done, 1 + NT * i + NT)
                    sp.sem_inc(held, 1)
                    load_rows(i + 1)
                    sp.wait_ge(mask_done, 1 + i + 1)
                    sp.sem_inc(held, 1)
                    load_mask(i + 1)
                sp.wait_ge(x_done, 1 + i + 1)
                sp.sem_inc(held, 1)
                sp.dma_start(x_out[i, :, :], tail[0:M, :]).then_inc(x_stored, 16)
                if not last:
                    load_res(i + 1)

            with sp.Fori(0, B - 1) as i:
                turn(i, False)
            turn(B - 1, True)
            sp.wait_ge(x_stored, 1 + 16 * B)

        @block.gpsimd
        def _(pool):
            pool.sem_inc(const_done, 1)
            pool.sem_inc(in_hi_done, 1)
            nc.gpsimd.memset(ident[:, :], 0.0).then_inc(const_done, 1)
            nc.gpsimd.memset(probs[:, :, :], 0.0).then_inc(const_done, 1)
            nc.gpsimd.memset(mask_add[:, :], 0.0).then_inc(const_done, 1)
            nc.gpsimd.memset(mean_var[:, :, :], 1.0).then_inc(const_done, 1)
            nc.gpsimd.memset(q_hi[:, :, :, :].bitcast(F32), 0.0).then_inc(const_done, 1)
            nc.gpsimd.memset(q_lo[:, :, :, :].bitcast(F32), 0.0).then_inc(const_done, 1)
            nc.gpsimd.memset(eps[:, :], EPS).then_inc(const_done, 1)
            pool.wait_ge(const_done, 2)
            nc.gpsimd.affine_select(out=ident[:, :], in_=ident[:, :], compare_op=ALU.not_equal, fill=1.0, base=0,
                                    pattern=[[-1, P]], channel_multiplier=1).then_inc(const_done, 1)
            pool.wait_ge(w_lo_done, 1 + 2 * KD)
            nc.gpsimd.memset(v_sb[:, KT - 1, :], 0.0).then_inc(const_done, 1)

            def prepare(p):
                for t in range(NT):
                    n, c = TILE_ROWS[t], TILE_COL[t]
                    pool.wait_ge(val_done, 1 + NT * p + t + 1)
                    if t == 0:
                        pool.wait_ge(k_ready, 1 + 2 * PAIRS * p)
                    src = lat_t[:, :, :] if t == LAT else val[:, t % 2, :, 0:n]
                    pool.sem_inc(held, 1)
                    nc.gpsimd.tensor_copy(kvin_hi[:, :, c:c + n], src).then_inc(in_hi_done, 1)

            prepare(0)
            with pool.Fori(0, B - 1) as i:
                prepare(i + 1)

        @block.scalar
        def _(act):
            for s in (tanh_done, val_done, q_hi_done, v_done, k_hi_done, exp_done, ta_done, w_hi_done):
                act.sem_inc(s, 1)
            act.wait_ge(c_loaded, 16 * 7)
            nc.scalar.activation(tanh_g[:, :], tanh_g[:, :], ACT.Tanh).then_inc(tanh_done, 1)

            def deviations(p, first=False):
                act.wait_ge(var_done, 1 if first else 3 * p)
                nc.scalar.activation(std[:, 0:NT], mean_var[:, 0:NT, 1], ACT.Sqrt, bias=eps[:, :]).then_inc(std_done, 1)

            def deviation_lat(p, first=False):
                act.wait_ge(var_done, 2 if first else 3 * p + 1)
                nc.scalar.activation(std[0:M, LAT:NT], mean_var[0:M, LAT:NT, 1], ACT.Sqrt, bias=eps[0:M, :]).then_inc(std_done, 1)

            def prepare(p):
                for t in range(NT):
                    n = TILE_ROWS[t]
                    act.wait_ge(tr_done, 1 + NT * p + t + 1)
                    if t >= 2:
                        act.wait_ge(in_lo_done, 1 + NT * p + t - 1)
                    else:
                        act.wait_ge(in_lo_done, 1 + NT * p)
                    if t == LAT:
                        act.wait_ge(q_ready, 1 + p)
                    g, b = (gl, bl) if t == LAT else (gx, bx)
                    for k in range(KD):
                        dst = lat_t[:, k, :] if t == LAT else val[:, t % 2, k, 0:n]
                        src = kv_ps[:, BANK * (t % 2) + P * k:BANK * (t % 2) + P * k + n]
                        ins = nc.scalar.activation(dst, src, ACT.Identity, bias=b[:, k:k + 1], scale=g[:, k:k + 1])
                    ins.then_inc(val_done, 1)

            def queries(i):
                act.wait_ge(q_ready, 1 + i + 1)
                act.wait_ge(const_done, 10)
                for x in range(2):
                    for m in range(2):
                        n = PAIRS // 2
                        src = s_ps[HD * x:HD * x + HD, BANK * m:BANK * m + n * M].rearrange("p (h q) -> p h q", q=M)
                        ins = nc.scalar.activation(q_hi[HD * x:HD * x + HD, n * m:n * m + n, x, :], src, ACT.Copy, scale=SCALE)
                ins.then_inc(q_hi_done, 1)

            def values(i, half, t):
                act.wait_ge(v_ready, 1 + 2 * KT * i + KT * half + t + 1)
                act.wait_ge(o_ready, 1 + PAIRS * i + PAIRS // 2 * half)
                n = KROWS[t]
                nc.scalar.activation(v_sb[0:n, t, :], kv_ps[0:n, BANK * (t % 2):BANK * (t % 2) + HALF], ACT.Copy).then_inc(v_done, 1)

            def keys(i, hp, part):
                c, n = PART[part]
                act.wait_ge(k_ready, 1 + 2 * PAIRS * i + 2 * hp + part + 1)
                act.wait_ge(s_ready, 1 + 2 * PAIRS * i + (2 * hp - 2 if hp >= 2 else 0))
                nc.scalar.activation(k_hi[:, hp % 2, c:c + n], kv_ps[:, c:c + n], ACT.Copy).then_inc(k_hi_done, 1)

            def move_t(i, hp, r):
                act.wait_ge(t_ready, 1 + 4 * PAIRS * i + 4 * hp + r + 1)
                act.wait_ge(o_ready, 1 + PAIRS * i + hp)
                c, n = (0, FIRST_T * M) if r == 0 else (FIRST_T * M, (KT - FIRST_T) * M)
                nc.scalar.activation(probs_t[:, 0, c:c + n], t_ps[:, BANK * r:BANK * r + n], ACT.Copy).then_inc(ta_done, 1)

            def exponent(i, hp, x):
                act.wait_ge(max_done, 1 + 2 * PAIRS * i + 2 * hp + x + 1)
                nc.scalar.activation(probs[0:M, x, 0:KEYS], probs[0:M, x, 0:KEYS], ACT.Exp, scale=-1.0,
                                     bias=neg_max[0:M, x:x + 1], accum_out=row_sum[0:M, x:x + 1]).then_inc(exp_done, 1)

            act.wait_ge(const_done, 9)
            deviations(0, True)
            for n in range(2 * KD):
                act.wait_ge(w_loaded[n % 2], 16 * (n // 2 + 1))
                nc.scalar.activation(wkv_hi[:, n // 2, SW * (n % 2):SW * (n % 2 + 1)], stage[:, SW * (n % 2):SW * (n % 2 + 1)],
                                     ACT.Copy).then_inc(w_hi_done, 1)
                if n == 1:
                    deviation_lat(0, True)
            prepare(0)

            def turn(i, last):
                queries(i)
                for t in range(KT):
                    values(i, 0, t)
                keys(i, 0, 0)
                keys(i, 0, 1)
                for hp in range(PAIRS + 1):
                    if hp >= 1:
                        move_t(i, hp - 1, 0)
                        move_t(i, hp - 1, 1)
                    if hp < PAIRS:
                        exponent(i, hp, 0)
                        if hp + 1 < PAIRS:
                            keys(i, hp + 1, 0)
                        exponent(i, hp, 1)
                        if hp + 1 < PAIRS:
                            keys(i, hp + 1, 1)
                    if hp == PAIRS // 2:
                        for t in range(KT):
                            values(i, 1, t)
                            if not last and t == 2:
                                deviations(i + 1)
                            if not last and t == 4:
                                deviation_lat(i + 1)
                if not last:
                    prepare(i + 1)
                act.wait_ge(var_done, 3 * i + (3 if last else 5))
                nc.scalar.activation(std[0:M, 0:1], mean_var[0:M, 0:1, 1], ACT.Sqrt, bias=eps[0:M, :]).then_inc(std_done, 1)

            with act.Fori(0, B - 1) as i:
                turn(i, False)
            turn(B - 1, True)

        @block.tensor
        def _(pe):
            for s in (tr_done, q_ready, v_ready, k_ready, s_ready, t_ready, o_ready, y_ready):
                pe.sem_inc(s, 1)

            def three(out, hi_l, lo_l, hi_r, lo_r, first, last):
                nc.tensor.matmul(out, hi_l, hi_r, start=first, stop=False)
                nc.tensor.matmul(out, hi_l, lo_r, start=False, stop=False)
                return nc.tensor.matmul(out, lo_l, hi_r, start=False, stop=last)

            def prepare(p, tiles=range(NT)):
                for t in tiles:
                    n = TILE_ROWS[t]
                    pe.wait_ge(norm_done, 1 + NT * p + t + 1)
                    if t >= 2:
                        pe.wait_ge(val_done, 1 + NT * p + t - 1)
                    for k in range(KD):
                        src = lat[0:M, P * k:P * k + P] if t == LAT else rows[0:n, t, P * k:P * k + P]
                        ins = nc.tensor.transpose(kv_ps[:, BANK * (t % 2) + P * k:BANK * (t % 2) + P * k + n], src, ident[0:n, 0:n])
                    ins.then_inc(tr_done, 1)

            def queries(i):
                pe.wait_ge(val_done, 1 + NT * i + NT)
                pe.wait_ge(max_done, 1 + 2 * PAIRS * i)
                for m in range(PAIRS):
                    c = BANK * (m // (PAIRS // 2)) + M * (m % (PAIRS // 2))
                    for k in range(KD):
                        ins = nc.tensor.matmul(s_ps[:, c:c + M], wq_sb[:, k, P * m:P * m + P], lat_t[:, k, :], start=(k == 0), stop=(k == KD - 1))
                ins.then_inc(q_ready, 1)

            def values(i, half):
                if half:
                    pe.wait_ge(k_lo_done, 1 + 2 * PAIRS * i + 2 * (PAIRS // 2 + 2))
                else:
                    pe.wait_ge(in_lo_done, 1 + NT * i + NT)
                for t in range(KT):
                    n = KROWS[t]
                    if t >= 2:
                        pe.wait_ge(v_done, 1 + 2 * KT * i + KT * half + t - 1)
                    out = kv_ps[0:n, BANK * (t % 2):BANK * (t % 2) + HALF]
                    for k in range(KD):
                        r = slice(P * t, P * t + n)
                        c = slice(INNER + HALF * half, INNER + HALF * half + HALF)
                        ins = three(out, kvin_hi[:, k, r], kvin_lo[:, k, r], wkv_hi[:, k, c], wkv_lo[:, k, c], k == 0, k == KD - 1)
                    ins.then_inc(v_ready, 1)

            def keys(i, hp, part):
                if hp == 0:
                    pe.wait_ge(v_done, 1 + 2 * KT * i + KT)
                elif hp == PAIRS // 2 + 2:
                    pe.wait_ge(v_done, 1 + 2 * KT * i + 2 * KT)
                else:
                    pe.wait_ge(k_lo_done, 1 + 2 * PAIRS * i + 2 * (hp - 1) + part + 1)
                c, n = PART[part]
                m = slice(P * hp, P * hp + P)
                for k in range(KD):
                    ins = three(kv_ps[:, c:c + n], wkv_hi[:, k, m], wkv_lo[:, k, m], kvin_hi[:, k, c:c + n], kvin_lo[:, k, c:c + n],
                                k == 0, k == KD - 1)
                ins.then_inc(k_ready, 1)

            def scores(i, hp, x):
                pe.wait_ge(k_lo_done, 1 + 2 * PAIRS * i + 2 * hp + 2)
                pe.wait_ge(q_lo_done, 1 + i + 1)
                pe.wait_ge(max_done, 1 + 2 * PAIRS * i + 2 * hp + x)
                for c, n in PART:
                    ins = three(s_ps[0:M, c:c + n], q_hi[:, hp, x, :], q_lo[:, hp, x, :], k_hi[:, hp % 2, c:c + n], k_lo[:, hp % 2, c:c + n],
                                True, True)
                ins.then_inc(s_ready, 1)

            def transposes(i, hp, x):
                pe.wait_ge(p_done, 1 + 2 * PAIRS * i + 2 * hp + x + 1)
                for r in range(2):
                    if x:
                        pe.wait_ge(ta_done, 1 + 2 * PAIRS * i + 2 * hp + r + 1)
                    else:
                        pe.wait_ge(tb_done, 1 + 2 * PAIRS * i + (2 * hp + r - 1 if hp else 0))
                    for t in (range(FIRST_T) if r == 0 else range(FIRST_T, KT)):
                        c = BANK * r + M * (t - FIRST_T * r)
                        ins = nc.tensor.transpose(t_ps[:, c:c + M], probs[0:M, x, P * t:P * t + P], ident[0:M, 0:M])
                    ins.then_inc(t_ready, 1)

            def attend(i, hp):
                pe.wait_ge(ta_done, 1 + 2 * PAIRS * i + 2 * hp + 2)
                pe.wait_ge(tb_done, 1 + 2 * PAIRS * i + 2 * hp + 2)
                pe.wait_ge(v_done, 1 + 2 * KT * i + KT * (1 + hp // (PAIRS // 2)))
                pe.wait_ge(o_done, 1 + PAIRS * i + hp)
                for t in range(KT):
                    for x in range(2):
                        c = HD * (2 * (hp % (PAIRS // 2)) + x)
                        ins = nc.tensor.matmul(o_ps[HD * x:HD * x + HD, 0:M], v_sb[:, t, c:c + HD], probs_t[:, x, M * t:M * t + M],
                                               start=(t == 0), stop=(t == KT - 1))
                ins.then_inc(o_ready, 1)

            pe.wait_ge(const_done, 9)
            prepare(0)
            pe.wait_ge(const_done, 10)
            pe.wait_ge(pq_loaded, 32)
            pe.wait_ge(w_lo_done, 1 + 2 * KD)

            def turn(i, last):
                queries(i)
                values(i, 0)
                keys(i, 0, 0)
                keys(i, 0, 1)
                for hp in range(PAIRS + 1):
                    if hp >= 1:
                        transposes(i, hp - 1, 0)
                    if hp < PAIRS:
                        scores(i, hp, 0)
                    if hp + 1 < PAIRS:
                        keys(i, hp + 1, 0)
                    if hp >= 1:
                        transposes(i, hp - 1, 1)
                    if hp < PAIRS:
                        scores(i, hp, 1)
                    if hp + 1 < PAIRS:
                        keys(i, hp + 1, 1)
                    if hp == PAIRS and not last:
                        prepare(i + 1, range(0, 2))
                    if hp >= 1:
                        attend(i, hp - 1)
                    if hp == PAIRS // 2:
                        values(i, 1)
                if not last:
                    prepare(i + 1, range(2, 4))
                pe.wait_ge(o_done, 1 + PAIRS * i + PAIRS)
                pe.wait_ge(y_read, 1 + i)
                for k in range(PAIRS):
                    ins = nc.tensor.matmul(w_ps[0:M, :], out_t[:, k, :], wout_sb[:, k, :], start=(k == 0), stop=(k == PAIRS - 1))
                ins.then_inc(y_ready, 1)
                if not last:
                    prepare(i + 1, range(4, NT))

            with pe.Fori(0, B - 1) as i:
                turn(i, False)
            turn(B - 1, True)

        @block.vector
        def _(dve):
            for s in (mask_done, norm_done, in_lo_done, q_lo_done, k_lo_done, max_done, p_done, tb_done, o_done, y_read,
                      x_done, w_lo_done, chain):
                dve.sem_inc(s, 1)
            own = Chain(dve, chain)

            def moments(p):
                dve.wait_ge(rows_loaded, 1 + 48 * (p + 1))
                for t in range(NT):
                    n = TILE_ROWS[t]
                    ins = nc.vector.bn_stats(stats[0:n, t, :], lat[0:M, :] if t == LAT else rows[0:n, t, :])
                own.link(ins)
                dve.sem_inc(held, 1)
                for t in range(NT):
                    n = TILE_ROWS[t]
                    ins = nc.vector.bn_aggr(mean_var[0:n, t, :], stats[0:n, t, :])
                ins.then_inc(var_done, 1)

            def normalise(p, first=False):
                dve.wait_ge(std_done, 1 if first else 3 * p)
                own.link(nc.vector.reciprocal(rstd[:, 0:NT], std[:, 0:NT]))
                own.link(nc.vector.tensor_scalar(lat[0:M, :], lat[0:M, :], mean_var[0:M, LAT, 0:1], rstd[0:M, LAT:NT], ALU.subtract, ALU.mult))
                own.link(nc.vector.bn_stats(stats[0:M, LAT, :], lat[0:M, :]))
                dve.sem_inc(held, 1)
                nc.vector.bn_aggr(mean_var[0:M, LAT, :], stats[0:M, LAT, :]).then_inc(var_done, 1)
                for t in range(CT):
                    n = TILE_ROWS[t]
                    nc.vector.tensor_scalar(rows[0:n, t, :], rows[0:n, t, :], mean_var[0:n, t, 0:1], rstd[0:n, t:t + 1],
                                            ALU.subtract, ALU.mult).then_inc(norm_done, 1)
                dve.wait_ge(std_done, 2 if first else 3 * p + 1)
                own.link(nc.vector.reciprocal(rstd[0:M, LAT:NT], std[0:M, LAT:NT]))
                nc.vector.tensor_scalar(lat[0:M, :], lat[0:M, :], mean_var[0:M, LAT, 0:1], rstd[0:M, LAT:NT],
                                        ALU.subtract, ALU.mult).then_inc(norm_done, 1)

            def prepare(p, tiles=range(NT)):
                for t in tiles:
                    n, c = TILE_ROWS[t], TILE_COL[t]
                    dve.wait_ge(in_hi_done, 1 + NT * p + t + 1)
                    src = lat_t[:, :, :] if t == LAT else val[:, t % 2, :, 0:n]
                    nc.vector.tensor_tensor(kvin_lo[:, :, c:c + n], src, kvin_hi[:, :, c:c + n].bitcast(F32), ALU.subtract).then_inc(in_lo_done, 1)

            def mask(i):
                dve.wait_ge(mask_loaded, 1 + 16 * (i + 1))
                nc.vector.tensor_scalar(mask_add[0:M, 0:N], mask_u8[0:M, :], 1.0, FAR, ALU.subtract, ALU.mult).then_inc(mask_done, 1)
                dve.wait_ge(mask_done, 1 + i + 1)

            def queries(i):
                dve.wait_ge(q_hi_done, 1 + i + 1)
                for x in range(2):
                    for m in range(2):
                        n = PAIRS // 2
                        src = s_ps[HD * x:HD * x + HD, BANK * m:BANK * m + n * M].rearrange("p (h q) -> p h q", q=M)
                        at = (slice(HD * x, HD * x + HD), slice(n * m, n * m + n), x, slice(0, M))
                        ins = nc.vector.scalar_tensor_tensor(q_lo[at], src, SCALE, q_hi[at].bitcast(F32), ALU.mult, ALU.subtract)
                ins.then_inc(q_lo_done, 1)

            def keys(i, hp, part):
                c, n = PART[part]
                dve.wait_ge(k_hi_done, 1 + 2 * PAIRS * i + 2 * hp + part + 1)
                nc.vector.tensor_tensor(k_lo[:, hp % 2, c:c + n], kv_ps[:, c:c + n], k_hi[:, hp % 2, c:c + n].bitcast(F32),
                                        ALU.subtract).then_inc(k_lo_done, 1)

            def maximum(i, hp, x):
                dve.wait_ge(s_ready, 1 + 2 * PAIRS * i + 2 * hp + x + 1)
                dve.wait_ge(t_ready, 1 + 4 * PAIRS * i + (4 * hp - 2 + 2 * x if hp else 0))
                dve.sem_inc(held, 1)
                nc.vector.tensor_tensor_reduce(out=probs[0:M, x, 0:KEYS], in0=s_ps[0:M, 0:KEYS], in1=mask_add[0:M, :], scale=-1.0,
                                               scalar=3.0e38, op0=ALU.add, op1=ALU.min, accum_out=neg_max[0:M, x:x + 1]).then_inc(max_done, 1)

            def divide(i, hp, x):
                dve.wait_ge(exp_done, 1 + 2 * PAIRS * i + 2 * hp + x + 1)
                own.link(nc.vector.reciprocal(row_inv[0:M, x:x + 1], row_sum[0:M, x:x + 1]))
                nc.vector.tensor_scalar(probs[0:M, x, 0:KEYS], probs[0:M, x, 0:KEYS], row_inv[0:M, x:x + 1], None, ALU.mult).then_inc(p_done, 1)

            def move_t(i, hp, r):
                dve.wait_ge(t_ready, 1 + 4 * PAIRS * i + 4 * hp + 2 + r + 1)
                dve.wait_ge(o_ready, 1 + PAIRS * i + hp)
                c, n = (0, FIRST_T * M) if r == 0 else (FIRST_T * M, (KT - FIRST_T) * M)
                nc.vector.tensor_copy(probs_t[:, 1, c:c + n], t_ps[:, BANK * r:BANK * r + n]).then_inc(tb_done, 1)

            def move_o(i, hp):
                dve.wait_ge(o_ready, 1 + PAIRS * i + hp + 1)
                dve.wait_ge(y_ready, 1 + i)
                nc.vector.tensor_copy(out_t[:, hp, :], o_ps[:, 0:M]).then_inc(o_done, 1)

            def finish(i, last):
                dve.wait_ge(y_ready, 1 + i + 1)
                own.link(nc.vector.bn_stats(stats[0:M, 0, :], w_ps[0:M, :]))
                dve.sem_inc(held, 1)
                nc.vector.bn_aggr(mean_var[0:M, 0, :], stats[0:M, 0, :]).then_inc(var_done, 1)
                dve.wait_ge(std_done, 3 * i + (3 if last else 5))
                own.link(nc.vector.reciprocal(rstd[0:M, 0:1], std[0:M, 0:1]))
                dve.wait_ge(x_stored, 1 + 16 * i)
                nc.vector.tensor_scalar(tail[0:M, :], w_ps[0:M, :], mean_var[0:M, 0, 0:1], rstd[0:M, 0:1], ALU.subtract, ALU.mult).then_inc(y_read, 1)
                dve.wait_ge(y_read, 1 + i + 1)
                own.link(nc.vector.tensor_tensor(tail[0:M, :], tail[0:M, :], gain_o[0:M, :], ALU.mult))
                own.link(nc.vector.tensor_tensor(tail[0:M, :], tail[0:M, :], bias_o[0:M, :], ALU.add))
                dve.wait_ge(res_loaded, 1 + 16 * (i + 1))
                nc.vector.scalar_tensor_tensor(tail[0:M, :], tail[0:M, :], tanh_g[0:M, 0:1], res[0:M, :], ALU.mult, ALU.add).then_inc(x_done, 1)

            dve.wait_ge(const_done, 9)
            moments(0)
            normalise(0, True)
            for n in range(2 * KD):
                dve.wait_ge(w_hi_done, 1 + n + 1)
                at = (slice(0, P), n // 2, slice(SW * (n % 2), SW * (n % 2 + 1)))
                nc.vector.tensor_tensor(wkv_lo[at], stage[:, SW * (n % 2):SW * (n % 2 + 1)], wkv_hi[at].bitcast(F32), ALU.subtract).then_inc(w_lo_done, 1)
            prepare(0)
            dve.wait_ge(tanh_done, 2)
            dve.wait_ge(c_loaded, 16 * 7)

            def turn(i, last):
                mask(i)
                queries(i)
                keys(i, 0, 0)
                keys(i, 0, 1)
                for hp in range(PAIRS + 1):
                    if hp < PAIRS:
                        maximum(i, hp, 0)
                        divide(i, hp, 0)
                    if hp >= 1:
                        move_t(i, hp - 1, 0)
                        move_t(i, hp - 1, 1)
                    if hp + 1 < PAIRS:
                        keys(i, hp + 1, 0)
                    if hp < PAIRS:
                        maximum(i, hp, 1)
                        divide(i, hp, 1)
                    if hp + 1 < PAIRS:
                        keys(i, hp + 1, 1)
                    if hp == PAIRS and not last:
                        prepare(i + 1, range(0, 2))
                    if hp >= 1:
                        move_o(i, hp - 1)
                    if hp == PAIRS // 2 and not last:
                        moments(i + 1)
                        normalise(i + 1)
                if not last:
                    prepare(i + 1, range(2, NT))
                finish(i, last)

            with own.loop(B - 1, 2 * PAIRS + 9) as i:
                turn(i, False)
            turn(B - 1, True)


def three(nc, out, left_hi, left_lo, right_hi, right_lo, start, stop):
    nc.tensor.matmul(out, left_hi, right_hi, start=start, stop=False)
    nc.tensor.matmul(out, left_hi, right_lo, start=False, stop=False)
    return nc.tensor.matmul(out, left_lo, right_hi, start=False, stop=stop)


def gated_experts(nc, name, x_in, router, router_bias, w_a, w_b, w_y, out_major, gate, x_out):
    B, M, D = x_in.shape
    P = 128
    T = B * M
    HT = T // 2
    HB = B // 2
    KD = D // P
    if out_major:
        E, F = w_a.shape[0], w_a.shape[1]
    else:
        E, F = w_a.shape[0], w_a.shape[2]
    GF = 512
    GC = GF // P
    GPE = F // GF
    STEPS = 2 * GC
    PIECES = 3 * KD
    BANK = 512
    EPS = 1e-5
    TOP = 2

    with ExitStack() as ctx:
        def sb(n, shape, dt=F32):
            return ctx.enter_context(nc.sbuf_tensor(f"{name}_{n}", shape, dt))

        def ps(n, shape):
            return ctx.enter_context(nc.psum_tensor(f"{name}_{n}", shape, F32))

        def sem(n):
            return nc.alloc_semaphore(f"{name}_{n}")

        raw = sb("raw", [P, 3, GC, GF])
        w_hi = sb("w_hi", [P, 2, 3, KD, GF], F32R)
        w_lo = sb("w_lo", [P, 2, 3, KD, GF], F32R)
        xn_hi = sb("xn_hi", [P, KD, T], F32R)
        xn_lo = sb("xn_lo", [P, KD, T], F32R)
        y_acc = sb("y_acc", [P, KD, T])
        gate_bc = sb("gate_bc", [P, E, T])
        x_tok = sb("x_tok", [P, B, D])
        s_sb = sb("s_sb", [P, HT])
        h_sb = sb("h_sb", [P, HT])
        hg = sb("hg", [P, HT])
        h_hi = sb("h_hi", [P, 2, HT], F32R)
        h_lo = sb("h_lo", [P, 2, HT], F32R)
        r_hi = sb("r_hi", [P, KD, E], F32R)
        r_lo = sb("r_lo", [P, KD, E], F32R)
        r_bias = sb("r_bias", [P, 1])
        logit_t = sb("logit_t", [P, T])
        r_raw = logit_t[:, 0:D] if out_major else logit_t[:, 0:KD * E].rearrange("p (k e) -> p k e", e=E)
        logits = sb("logits", [P, B, E])
        l_max = sb("l_max", [P, B])
        p_exp = sb("p_exp", [P, B, E])
        above, equal = (gate_bc[:, n, 0:B * E * E].rearrange("p (b i j) -> p b i j", i=E, j=E) for n in range(2))
        before = sb("before", [P, E, E])
        rank = sb("rank", [P, B, E])
        p_sum = sb("p_sum", [P, B])
        gates = sb("gates", [P, B, E])
        tanh_g = sb("tanh_g", [P, 1])
        eps = sb("eps", [P, 1])
        ident = sb("ident", [P, P])
        stats = sb("stats", [P, B, 6])
        mean_var = sb("mean_var", [P, B, 2])
        std = sb("std", [P, B])
        rstd = sb("rstd", [P, B])

        a_ps = ps("a_ps", [P, BANK])
        b_ps = ps("b_ps", [P, BANK])
        y_ps = ps("y_ps", [P, 4, BANK])
        w_ps = ps("w_ps", [P, 2, BANK])

        x_loaded = [sem(f"x_loaded{n}") for n in range(2)]
        c_loaded = sem("c_loaded")
        raw_loaded = [sem(f"raw_loaded{m}") for m in range(3)]
        x_again = sem("x_again")
        x_stored = sem("x_stored")
        const_done = sem("const_done")
        tanh_done = sem("tanh_done")
        var_done = sem("var_done")
        std_done = sem("std_done")
        norm_done = sem("norm_done")
        tr_done = sem("tr_done")
        xhi_done = sem("xhi_done")
        xlo_done = sem("xlo_done")
        rt_ready = sem("rt_ready")
        rhi_done = sem("rhi_done")
        rlo_done = sem("rlo_done")
        logit_ready = sem("logit_ready")
        logit_done = sem("logit_done")
        back_ready = sem("back_ready")
        shift_done = sem("shift_done")
        exp_done = sem("exp_done")
        gates_done = sem("gates_done")
        bc_ready = sem("bc_ready")
        bc_done = sem("bc_done")
        tw_ready = sem("tw_ready")
        whi_done = sem("whi_done")
        wlo_done = sem("wlo_done")
        a_ready = sem("a_ready")
        b_ready = sem("b_ready")
        s_done = sem("s_done")
        h_done = sem("h_done")
        hg_done = sem("hg_done")
        hi_done = sem("hi_done")
        lo_done = sem("lo_done")
        y_done = sem("y_done")
        add_done = sem("add_done")
        out_ready = sem("out_ready")
        x_done = sem("x_done")
        held = sem("held")
        chain = sem("chain")

        block = ctx.enter_context(nc.Block())


        def pieces(j):
            return range(0) if j == 0 else range(PIECES * (j - 1) // (STEPS - 1), PIECES * j // (STEPS - 1))

        @block.sync
        def _(sp):
            for q in range(4):
                sp.dma_start(x_tok[0:M, 2 * q:2 * q + 2, :], x_in[2 * q:2 * q + 2].rearrange("b p d -> p b d")).then_inc(x_loaded[q // 2], 16)

            def load(m, e, gi):
                w = (w_a, w_b, w_y)[m]
                f = slice(GF * gi, GF * gi + GF)
                if (m < 2) == out_major:
                    src = w[e, f, :].rearrange("(c p) d -> p c d", p=P)
                else:
                    src = w[e, :, f].rearrange("(k p) f -> p k f", p=P)
                sp.dma_start(raw[:, m, :, :], src).then_inc(raw_loaded[m], 16)

            load(0, 0, 0)
            if out_major:
                sp.dma_start(r_raw[0:E, :], router[:, :]).then_inc(c_loaded, 16)
            else:
                sp.dma_start(r_raw[:, :, :], router.rearrange("(k p) e -> p k e", p=P), allow_slow_non_contiguous=True).then_inc(c_loaded, 16)
                sp.dma_start(r_bias[0:E, :], router_bias.rearrange("(e a) -> e a", a=1), allow_slow_non_contiguous=True).then_inc(c_loaded, 16)
            sp.dma_start(tanh_g[:, :], gate.to_broadcast([P, 1])).then_inc(c_loaded, 16)
            load(1, 0, 0)
            load(2, 0, 0)

            def refill(e, gi, last):
                for m in range(3):
                    if last and gi == GPE - 1:
                        continue
                    sp.wait_ge(tw_ready if out_major else wlo_done, 1 + PIECES * (GPE * e + gi) + KD * (m + 1))
                    sp.sem_inc(held, 1)
                    if gi + 1 < GPE:
                        load(m, e, gi + 1)
                    else:
                        load(m, e + 1, 0)

            with sp.Fori(0, E - 1) as e:
                for gi in range(GPE):
                    refill(e, gi, False)
            for gi in range(GPE):
                refill(E - 1, gi, True)
            sp.wait_ge(tr_done, 1 + B)
            sp.dma_start(x_tok[0:M, :, :], x_in.rearrange("b p d -> p b d")).then_inc(x_again, 16)
            for b in range(B):
                sp.wait_ge(x_done, b + 1)
                sp.dma_start(x_out[b, :, :], x_tok[0:M, b, :]).then_inc(x_stored, 16)
            sp.wait_ge(x_stored, 16 * B)

        @block.gpsimd
        def _(pool):
            pool.sem_inc(hg_done, 1)
            nc.gpsimd.memset(ident[:, :], 0.0).then_inc(const_done, 1)
            nc.gpsimd.memset(before[:, :, :], 1.0).then_inc(const_done, 1)
            nc.gpsimd.memset(eps[:, :], EPS).then_inc(const_done, 1)
            pool.wait_ge(const_done, 2)
            nc.gpsimd.affine_select(out=ident[:, :], in_=ident[:, :], compare_op=ALU.not_equal, fill=1.0, base=0,
                                    pattern=[[-1, P]], channel_multiplier=1).then_inc(const_done, 1)
            nc.gpsimd.affine_select(out=before[:, :, :], in_=before[:, :, :], compare_op=ALU.is_gt, fill=0.0, base=0,
                                    pattern=[[1, E], [-1, E]], channel_multiplier=0).then_inc(const_done, 1)
            nc.gpsimd.memset(y_acc[:, :, :], 0.0).then_inc(const_done, 1)

            def step(e, gi, j):
                n = STEPS * (GPE * e + gi) + j
                half = j // GC
                pool.wait_ge(h_done, 1 + n + 1)
                pool.wait_ge(lo_done, 1 + n)
                pool.sem_inc(held, 1)
                nc.gpsimd.tensor_tensor(hg[:, :], h_sb[:, :], gate_bc[:, e, HT * half:HT * half + HT], ALU.mult).then_inc(hg_done, 1)

            pool.wait_ge(bc_done, 1 + 2 * E)
            with pool.Fori(0, E) as e:
                for gi in range(GPE):
                    for j in range(STEPS):
                        step(e, gi, j)

        @block.scalar
        def _(act):
            for s in (whi_done, s_done, hi_done):
                act.sem_inc(s, 1)
            act.wait_ge(c_loaded, 16 * (2 if out_major else 3))
            nc.scalar.activation(tanh_g[:, :], tanh_g[:, :], ACT.Tanh).then_inc(tanh_done, 1)
            act.wait_ge(const_done, 3)
            act.wait_ge(var_done, 1)
            nc.scalar.activation(std[0:M, :], mean_var[0:M, :, 1], ACT.Sqrt, bias=eps[0:M, :]).then_inc(std_done, 1)
            if out_major:
                act.wait_ge(rt_ready, 1)
                nc.scalar.activation(r_hi[:, :, :], a_ps[:, 0:KD * E].rearrange("p (k e) -> p k e", e=E), ACT.Copy).then_inc(rhi_done, 1)
            else:
                nc.scalar.activation(r_hi[:, :, :], r_raw[:, :, :], ACT.Copy).then_inc(rhi_done, 1)
            for b in range(B):
                act.wait_ge(tr_done, 1 + b + 1)
                nc.scalar.activation(xn_hi[:, :, M * b:M * b + M], y_ps[:, b % 4, :].rearrange("p (k q) -> p k q", q=P)[:, :, 0:M],
                                     ACT.Copy).then_inc(xhi_done, 1)

            def split(g, slot, q):
                m, k = q // KD, q % KD
                if out_major:
                    act.wait_ge(tw_ready, 1 + PIECES * g + q + 1)
                    src = w_ps[:, q % 2, :]
                else:
                    act.wait_ge(raw_loaded[m], 16 * (g + 1))
                    src = raw[:, m, k, :]
                nc.scalar.activation(w_hi[:, slot, m, k, :], src, ACT.Copy).then_inc(whi_done, 1)

            for half in range(2):
                act.wait_ge(logit_ready, half + 1)
                src = (a_ps, b_ps)[half][0:E, 0:HT]
                dst = logit_t[0:E, HT * half:HT * half + HT]
                if out_major:
                    nc.scalar.activation(dst, src, ACT.Copy).then_inc(logit_done, 1)
                else:
                    nc.scalar.activation(dst, src, ACT.Identity, bias=r_bias[0:E, :]).then_inc(logit_done, 1)
            act.wait_ge(shift_done, 1)
            nc.scalar.activation(p_exp[0:M, :, :], p_exp[0:M, :, :], ACT.Exp).then_inc(exp_done, 1)
            for q in range(PIECES):
                split(0, 0, q)

            def step(e, gi, j, last):
                g = GPE * e + gi
                n = STEPS * g + j
                act.wait_ge(a_ready, 1 + n + 1)
                act.wait_ge(h_done, 1 + n)
                nc.scalar.activation(s_sb[:, :], a_ps[:, 0:HT], ACT.Silu).then_inc(s_done, 1)
                if not (last and gi == GPE - 1):
                    for q in pieces(j):
                        act.wait_ge(y_done, 2 + STEPS * g)
                        split(g + 1, (gi + 1) % 2, q)
                act.wait_ge(hg_done, 1 + n + 1)
                act.wait_ge(y_done, 1 + n)
                nc.scalar.activation(h_hi[:, j % 2, :], hg[:, :], ACT.Copy).then_inc(hi_done, 1)

            with act.Fori(0, E - 1) as e:
                for gi in range(GPE):
                    for j in range(STEPS):
                        step(e, gi, j, False)
            for gi in range(GPE):
                for j in range(STEPS):
                    step(E - 1, gi, j, True)

        @block.tensor
        def _(pe):
            for s in (tr_done, tw_ready, a_ready, b_ready, y_done, y_done):
                pe.sem_inc(s, 1)
            pe.wait_ge(const_done, 6)
            if out_major:
                pe.wait_ge(c_loaded, 32)
                for k in range(KD):
                    ins = nc.tensor.transpose(a_ps[:, E * k:E * k + E], r_raw[0:E, P * k:P * k + P], ident[0:E, 0:E])
                ins.then_inc(rt_ready, 1)
            for b in range(B):
                pe.wait_ge(norm_done, b + 1)
                if b >= 4:
                    pe.wait_ge(xlo_done, b - 3)
                for k in range(KD):
                    ins = nc.tensor.transpose(y_ps[:, b % 4, P * k:P * k + M], x_tok[0:M, b, P * k:P * k + P], ident[0:M, 0:M])
                ins.then_inc(tr_done, 1)
            pe.wait_ge(rlo_done, 1)
            for half in range(2):
                pe.wait_ge(xlo_done, HB * (half + 1))
                t = slice(HT * half, HT * half + HT)
                for k in range(KD):
                    ins = three(nc, (a_ps, b_ps)[half][0:E, 0:HT], r_hi[:, k, :], r_lo[:, k, :], xn_hi[:, k, t], xn_lo[:, k, t], k == 0, k == KD - 1)
                ins.then_inc(logit_ready, 1)
            pe.wait_ge(logit_done, 2)
            for b in range(B):
                ins = nc.tensor.transpose(y_ps[0:M, 0, E * b:E * b + E], logit_t[0:E, M * b:M * b + M], ident[0:E, 0:E])
            ins.then_inc(back_ready, 1)

            def turn_piece(g, q):
                m, k = q // KD, q % KD
                pe.wait_ge(raw_loaded[m], 16 * (g + 1))
                pe.wait_ge(wlo_done, PIECES * g + q if q else PIECES * g + 1)
                for c in range(GC):
                    ins = nc.tensor.transpose(w_ps[:, q % 2, P * c:P * c + P], raw[:, m, c, P * k:P * k + P], ident[:, :])
                ins.then_inc(tw_ready, 1)

            if out_major:
                for q in range(PIECES):
                    turn_piece(0, q)
            pe.wait_ge(gates_done, 1)
            for n in range(2 * E):
                e, half = n // 2, n % 2
                if n >= 4:
                    pe.wait_ge(bc_done, 1 + n - 3)
                for b in range(HB):
                    ins = nc.tensor.matmul(y_ps[:, n % 4, M * b:M * b + M], gates[0:M, HB * half + b, e:e + 1].to_broadcast([M, P]),
                                           ident[0:M, 0:M], start=True, stop=True)
                ins.then_inc(bc_ready, 1)

            def hidden(e, gi, j):
                g = GPE * e + gi
                n = STEPS * g + j
                slot, half, c = gi % 2, j // GC, j % GC
                t = slice(HT * half, HT * half + HT)
                f = slice(P * c, P * c + P)
                if j == 0:
                    pe.wait_ge(wlo_done, 1 + PIECES * (g + 1))
                pe.wait_ge(s_done, 1 + n)
                for k in range(KD):
                    ins = three(nc, a_ps[:, 0:HT], w_hi[:, slot, 0, k, f], w_lo[:, slot, 0, k, f], xn_hi[:, k, t], xn_lo[:, k, t], k == 0, k == KD - 1)
                ins.then_inc(a_ready, 1)
                pe.wait_ge(h_done, 1 + n)
                for k in range(KD):
                    ins = three(nc, b_ps[:, 0:HT], w_hi[:, slot, 1, k, f], w_lo[:, slot, 1, k, f], xn_hi[:, k, t], xn_lo[:, k, t], k == 0, k == KD - 1)
                ins.then_inc(b_ready, 1)

            def project(e, gi, j):
                g = GPE * e + gi
                n = STEPS * g + j
                slot, half, c = gi % 2, j // GC, j % GC
                pe.wait_ge(lo_done, 1 + n + 1)
                if c == 0:
                    pe.wait_ge(add_done, 1 + 2 * g + half)
                for k in range(KD):
                    d = slice(P * k, P * k + P)
                    ins = three(nc, y_ps[:, k, 0:HT], w_hi[:, slot, 2, c, d], w_lo[:, slot, 2, c, d], h_hi[:, j % 2, :], h_lo[:, j % 2, :],
                                c == 0, c == GC - 1)
                ins.then_inc(y_done, 1)

            pe.wait_ge(bc_done, 1 + 2 * E)

            def turn(e, last):
                for gi in range(GPE):
                    for j in range(STEPS):
                        hidden(e, gi, j)
                        if out_major and not (last and gi == GPE - 1):
                            for q in pieces(j):
                                turn_piece(GPE * e + gi + 1, q)
                        if j:
                            project(e, gi, j - 1)
                        elif gi:
                            project(e, gi - 1, STEPS - 1)
                project(e, GPE - 1, STEPS - 1)

            with pe.Fori(0, E - 1) as e:
                turn(e, False)
            turn(E - 1, True)
            pe.wait_ge(add_done, 1 + 2 * GPE * E)
            for b in range(B):
                if b >= 4:
                    pe.wait_ge(x_done, b - 3)
                for k in range(KD):
                    ins = nc.tensor.transpose(y_ps[0:M, b % 4, P * k:P * k + P], y_acc[:, k, M * b:M * b + M], ident[:, :])
                ins.then_inc(out_ready, 1)

        @block.vector
        def _(dve):
            for s in (bc_done, wlo_done, h_done, lo_done, add_done, chain):
                dve.sem_inc(s, 1)
            own = Chain(dve, chain)
            for b in range(B):
                if b % HB == 0:
                    dve.wait_ge(x_loaded[b // HB], 32)
                ins = nc.vector.bn_stats(stats[0:M, b, :], x_tok[0:M, b, :])
            own.link(ins)
            for b in range(B):
                ins = nc.vector.bn_aggr(mean_var[0:M, b, :], stats[0:M, b, :])
            ins.then_inc(var_done, 1)
            dve.wait_ge(std_done, 1)
            own.link(nc.vector.reciprocal(rstd[0:M, :], std[0:M, :]))
            for b in range(B):
                nc.vector.tensor_scalar(x_tok[0:M, b, :], x_tok[0:M, b, :], mean_var[0:M, b, 0:1], rstd[0:M, b:b + 1],
                                        ALU.subtract, ALU.mult).then_inc(norm_done, 1)
            dve.wait_ge(rhi_done, 1)
            src = a_ps[:, 0:KD * E].rearrange("p (k e) -> p k e", e=E) if out_major else r_raw[:, :, :]
            nc.vector.tensor_tensor(r_lo[:, :, :], src, r_hi[:, :, :].bitcast(F32), ALU.subtract).then_inc(rlo_done, 1)
            for b in range(B):
                dve.wait_ge(xhi_done, b + 1)
                t = slice(M * b, M * b + M)
                nc.vector.tensor_tensor(xn_lo[:, :, t], y_ps[:, b % 4, :].rearrange("p (k q) -> p k q", q=P)[:, :, 0:M],
                                        xn_hi[:, :, t].bitcast(F32), ALU.subtract).then_inc(xlo_done, 1)
            dve.wait_ge(back_ready, 1)
            own.link(nc.vector.tensor_copy(logits[0:M, :, :], y_ps[0:M, 0, 0:B * E].rearrange("p (b e) -> p b e", e=E)))
            own.link(nc.vector.tensor_reduce(l_max[0:M, :], logits[0:M, :, :], axis=AX.X, op=ALU.max))
            nc.vector.tensor_tensor(p_exp[0:M, :, :], logits[0:M, :, :], l_max[0:M, :].unsqueeze(2).to_broadcast([M, B, E]), ALU.subtract).then_inc(shift_done, 1)
            for b in range(B):
                other = logits[0:M, b, :].unsqueeze(1).to_broadcast([M, E, E])
                this = logits[0:M, b, :].unsqueeze(2).to_broadcast([M, E, E])
                nc.vector.tensor_tensor(above[0:M, b, :, :], other, this, ALU.is_gt)
                ins = nc.vector.tensor_tensor(equal[0:M, b, :, :], other, this, ALU.is_equal)
            own.link(ins)
            ins = nc.vector.tensor_tensor(equal[0:M, :, :, :], equal[0:M, :, :, :], before[0:M, :, :].unsqueeze(1).to_broadcast([M, B, E, E]), ALU.mult)
            own.link(ins)
            own.link(nc.vector.tensor_tensor(above[0:M, :, :, :], above[0:M, :, :, :], equal[0:M, :, :, :], ALU.add))
            own.link(nc.vector.tensor_reduce(rank[0:M, :, :], above[0:M, :, :, :], axis=AX.X, op=ALU.add))
            dve.wait_ge(exp_done, 1)
            own.link(nc.vector.scalar_tensor_tensor(gates[0:M, :, :], rank[0:M, :, :], TOP - 0.5, p_exp[0:M, :, :], ALU.is_lt, ALU.mult))
            own.link(nc.vector.tensor_reduce(p_sum[0:M, :], gates[0:M, :, :], axis=AX.X, op=ALU.add))
            own.link(nc.vector.reciprocal(p_sum[0:M, :], p_sum[0:M, :]))
            nc.vector.tensor_tensor(gates[0:M, :, :], gates[0:M, :, :], p_sum[0:M, :].unsqueeze(2).to_broadcast([M, B, E]), ALU.mult).then_inc(gates_done, 1)

            def split(g, slot, q):
                m, k = q // KD, q % KD
                dve.wait_ge(whi_done, 1 + PIECES * g + q + 1)
                src = w_ps[:, q % 2, :] if out_major else raw[:, m, k, :]
                nc.vector.tensor_tensor(w_lo[:, slot, m, k, :], src, w_hi[:, slot, m, k, :].bitcast(F32), ALU.subtract).then_inc(wlo_done, 1)

            for q in range(PIECES):
                split(0, 0, q)
            for n in range(2 * E):
                dve.wait_ge(bc_ready, n + 1)
                nc.vector.tensor_copy(gate_bc[:, n // 2, HT * (n % 2):HT * (n % 2) + HT], y_ps[:, n % 4, 0:HT]).then_inc(bc_done, 1)
            dve.wait_ge(const_done, 6)

            def add(e, gi, half):
                g = GPE * e + gi
                dve.wait_ge(y_done, 2 + STEPS * g + GC * (half + 1))
                dve.wait_ge(add_done, 1 + 2 * g + half)
                t = slice(HT * half, HT * half + HT)
                ins = nc.vector.tensor_tensor(y_acc[:, :, t], y_acc[:, :, t], y_ps[:, :, 0:HT], ALU.add)
                ins.then_inc(add_done, 1)

            def step(e, gi, j, last):
                g = GPE * e + gi
                n = STEPS * g + j
                dve.wait_ge(b_ready, 1 + n + 1)
                dve.wait_ge(s_done, 1 + n + 1)
                dve.wait_ge(hg_done, 1 + n)
                nc.vector.tensor_tensor(h_sb[:, :], s_sb[:, :], b_ps[:, 0:HT], ALU.mult).then_inc(h_done, 1)
                if not (last and gi == GPE - 1):
                    for q in pieces(j):
                        split(g + 1, (gi + 1) % 2, q)
                dve.wait_ge(hi_done, 1 + n + 1)
                nc.vector.tensor_tensor(h_lo[:, j % 2, :], hg[:, :], h_hi[:, j % 2, :].bitcast(F32), ALU.subtract).then_inc(lo_done, 1)
                if j == GC:
                    add(e, gi, 0)
                elif j == 0 and gi:
                    add(e, gi - 1, 1)

            def turn(e, last):
                for gi in range(GPE):
                    for j in range(STEPS):
                        step(e, gi, j, last)
                add(e, GPE - 1, 1)

            with dve.Fori(0, E - 1) as e:
                turn(e, False)
            turn(E - 1, True)
            dve.wait_ge(tanh_done, 1)
            dve.wait_ge(x_again, 16)
            for b in range(B):
                dve.wait_ge(out_ready, b + 1)
                nc.vector.scalar_tensor_tensor(x_tok[0:M, b, :], y_ps[0:M, b % 4, :], tanh_g[0:M, 0:1], x_tok[0:M, b, :],
                                               ALU.mult, ALU.add).then_inc(x_done, 1)


def strided_attention(nc, x_in, ctx_rows, wq, bq, wk, bk, wv, bv, wo, bo, gate, x_out):
    B, M, D = x_in.shape
    P = 128
    H = 16
    HD = D // H
    J = ctx_rows.shape[1] // H
    KD = D // P
    QH = P // HD
    HH = H // 2
    T = B * M
    HT = T // 2
    HB = B // 2
    BJ = HB * J
    BANK = 512
    EPS = 1e-5
    SCALE = HD ** -0.5

    with ExitStack() as ctx:
        def sb(n, shape, dt=F32):
            return ctx.enter_context(nc.sbuf_tensor("g_" + n, shape, dt))

        def sem(n):
            return nc.alloc_semaphore("g_" + n)

        ctx_t = sb("ctx_t", [P, KD, H, BJ])
        rows = sb("rows", [P, 2, HH * D])
        wq_hi, wq_lo, wo_hi, wo_lo = (sb(n, [P, KD, D], F32R) for n in ("wq_hi", "wq_lo", "wo_hi", "wo_lo"))
        wk_t, wv_t = (sb(n, [P, KD, D]) for n in ("wk_t", "wv_t"))
        xn_hi = sb("xn_hi", [P, KD, T], F32R)
        xn_lo = sb("xn_lo", [P, KD, T], F32R)
        shared = sb("shared", [P, B * D])
        k_t = sb("k_t", [P, KD, B * J])
        v_t = sb("v_t", [P, KD, B * J])
        q_b = sb("q_b", [P, 2, H, M])
        v_tb = sb("v_tb", [P, 2, KD, J])
        v_b = sb("v_b", [P, 2, D])
        probs = sb("probs", [P, 2, H * J])
        probs_t = sb("probs_t", [P, H * M])
        s_max = sb("s_max", [P, 2, HH])
        s_sum = sb("s_sum", [P, 2, HH])
        bias = {n: sb("b" + n, [P, KD]) for n in "qkvo"}
        tanh_g = sb("tanh_g", [P, 1])
        eps = sb("eps", [P, 1])
        ident = sb("ident", [P, P])
        stats = sb("stats", [P, B, 6])
        mean_var = sb("mean_var", [P, B, 2])
        std = sb("std", [P, B])
        rstd = sb("rstd", [P, B])
        x_tok = shared[:, :].rearrange("p (b d) -> p b d", d=D)
        q_t = shared[:, 0:KD * T].rearrange("p (k t) -> p k t", t=T)
        y_t = q_t
        raw = ctx_t[:, :, :, :].rearrange("p k h j -> p (k h j)")[:, 0:4 * KD * D].rearrange("p (w c d) -> p w c d", c=KD, d=D)
        x_res = rows[:, 0, :].rearrange("p (b d) -> p b d", d=D)

        banks = ctx.enter_context(nc.psum_tensor("g_banks", [P, 8, BANK], F32))
        S, TP, V, O = 0, 4, 6, 7

        x_loaded = [sem(f"x_loaded{n}") for n in range(2)]
        c_loaded = sem("c_loaded")
        w_loaded = [sem(f"w_loaded{n}") for n in range(4)]
        rows_loaded = [sem(f"rows_loaded{n}") for n in range(2)]
        x_again = sem("x_again")
        x_stored = sem("x_stored")
        const_done = sem("const_done")
        tanh_done = sem("tanh_done")
        var_done = sem("var_done")
        std_done = sem("std_done")
        norm_done = sem("norm_done")
        fill_ready = sem("fill_ready")
        fill_hi = sem("fill_hi")
        fill_done = sem("fill_done")
        q_ready = sem("q_ready")
        q_done = sem("q_done")
        ctx_ready = sem("ctx_ready")
        ctx_a = sem("ctx_a")
        ctx_b = sem("ctx_b")
        kv_ready = sem("kv_ready")
        kv_done = sem("kv_done")
        qv_done = sem("qv_done")
        s_ready = sem("s_ready")
        sub_done = sem("sub_done")
        exp_done = sem("exp_done")
        p_done = sem("p_done")
        v_ready = sem("v_ready")
        v_done = sem("v_done")
        t_ready = sem("t_ready")
        ta_done = sem("ta_done")
        tb_done = sem("tb_done")
        o_ready = sem("o_ready")
        ohi_done = sem("ohi_done")
        olo_done = sem("olo_done")
        y_ready = sem("y_ready")
        y_done = sem("y_done")
        out_ready = sem("out_ready")
        x_done = sem("x_done")
        held = sem("held")
        chain = sem("chain")
        pool_chain = sem("pool_chain")

        block = ctx.enter_context(nc.Block())

        CTX0, KV0, S0, SUB0, V0, T0, O0 = 2, 4, 2, 2, 2, 5, 2

        W = (wq, wk, wv, wo)
        FILLS = 4 * KD + B

        @block.sync
        def _(sp):
            for n, w in enumerate(W):
                sp.dma_start(raw[:, n, :, :], w.rearrange("(c p) d -> p c d", p=P)).then_inc(w_loaded[n], 16)
                if n == 0:
                    for q in range(4):
                        sp.dma_start(x_tok[0:M, 2 * q:2 * q + 2, :], x_in[2 * q:2 * q + 2].rearrange("b p d -> p b d")).then_inc(x_loaded[q // 2], 16)
            for n, src in zip("qkvo", (bq, bk, bv, bo)):
                sp.dma_start(bias[n][:, :], src.rearrange("(c p) -> p c", p=P), allow_slow_non_contiguous=True).then_inc(c_loaded, 16)
            sp.dma_start(tanh_g[:, :], gate.to_broadcast([P, 1])).then_inc(c_loaded, 16)

            def load_rows(b, hh):
                src = ctx_rows[b, 0:H * J, :].rearrange("(j h) d -> j h d", h=H)[:, HH * hh:HH * hh + HH, :]
                sp.dma_start(rows[0:J, hh, :].rearrange("p (h d) -> p h d", d=D), src).then_inc(rows_loaded[hh], 16)

            load_rows(0, 0)
            load_rows(0, 1)
            with sp.Fori(0, B - 1) as i:
                for hh in range(2):
                    sp.wait_ge(ctx_ready, 1 + KD * (2 * i + hh + 1))
                    sp.sem_inc(held, 1)
                    load_rows(i + 1, hh)
            sp.wait_ge(ctx_ready, 1 + KD * 2 * B)
            sp.dma_start(x_res[0:M, :, :], x_in.rearrange("b p d -> p b d")).then_inc(x_again, 16)
            for b in range(B):
                sp.wait_ge(x_done, b + 1)
                sp.dma_start(x_out[b, :, :], x_res[0:M, b, :]).then_inc(x_stored, 16)
            sp.wait_ge(x_stored, 16 * B)

        @block.gpsimd
        def _(pool):
            pool.sem_inc(qv_done, 1)
            nc.gpsimd.memset(ident[:, :], 0.0).then_inc(const_done, 1)
            nc.gpsimd.memset(eps[:, :], EPS).then_inc(const_done, 1)
            nc.gpsimd.memset(q_b[:, :, :, :], 0.0).then_inc(const_done, 1)
            pool.wait_ge(const_done, 3)
            nc.gpsimd.affine_select(out=ident[:, :], in_=ident[:, :], compare_op=ALU.not_equal, fill=1.0, base=0,
                                    pattern=[[-1, P]], channel_multiplier=1).then_inc(const_done, 1)
            pool.sem_inc(pool_chain, 1)
            pool.wait_ge(q_done, 2 * KD)
            pool.wait_ge(kv_done, KV0 + 4 * KD)
            pool.sem_inc(held, 1)
            own = Chain(pool, pool_chain)
            with own.loop(B // 2, 4) as i:
                for u in range(2):
                    n = 2 * i + u
                    pool.wait_ge(s_ready, S0 + n - 1)
                    pool.wait_ge(v_ready, V0 + n - 1)
                    pool.sem_inc(held, 1)
                    for r in range(QH):
                        p = slice(HD * r, HD * r + HD)
                        ins = nc.gpsimd.tensor_copy(q_b[p, u, :, :].rearrange("p (c r) q -> p c r q", r=QH)[:, :, r, :], q_t[p, :, bass.ds(M * n, M)])
                    own.link(ins)
                    pool.sem_inc(held, 1)
                    own.link(nc.gpsimd.tensor_copy(v_tb[:, u, :, :], v_t[:, :, bass.ds(J * n, J)]))
                    pool.sem_inc(qv_done, 1)

        @block.scalar
        def _(act):
            for s, start in ((ctx_a, CTX0), (kv_done, KV0), (exp_done, 1), (v_done, 1), (ta_done, 1), (ohi_done, 1)):
                act.sem_inc(s, start)
            act.wait_ge(c_loaded, 80)
            nc.scalar.activation(tanh_g[:, :], tanh_g[:, :], ACT.Tanh).then_inc(tanh_done, 1)
            act.wait_ge(const_done, 3)
            act.wait_ge(var_done, 1)
            nc.scalar.activation(std[0:M, :], mean_var[0:M, :, 1], ACT.Sqrt, bias=eps[0:M, :]).then_inc(std_done, 1)
            for n in range(FILLS):
                if n < KD or 3 * KD <= n < 4 * KD:
                    act.wait_ge(fill_ready, n + 1)
                    dst = wq_hi if n < KD else wo_hi
                    nc.scalar.activation(dst[:, n % KD, :], banks[:, n % 4, :], ACT.Copy).then_inc(fill_hi, 1)
                elif n >= 4 * KD:
                    b = n - 4 * KD
                    act.wait_ge(fill_ready, n + 1)
                    nc.scalar.activation(xn_hi[:, :, M * b:M * b + M], banks[:, n % 4, :].rearrange("p (k q) -> p k q", q=P)[:, :, 0:M],
                                         ACT.Copy).then_inc(fill_hi, 1)

            with act.Fori(0, 2) as half:
                for u in range(2 * HB):
                    bl, hh = u // 2, u % 2
                    for k in range(0, KD, 2):
                        act.wait_ge(ctx_ready, 1 + KD * (2 * HB * half + u) + k + 1)
                        nc.scalar.activation(ctx_t[:, k, HH * hh:HH * hh + HH, J * bl:J * bl + J],
                                             banks[:, S + k, 0:HH * J].rearrange("p (h j) -> p h j", j=J), ACT.Copy).then_inc(ctx_a, 1)
                for n in range(2 * KD):
                    act.wait_ge(kv_ready, 1 + 2 * KD * half + n + 1)
                    dst, b = ((k_t, "k"), (v_t, "v"))[n % 2]
                    nc.scalar.activation(dst[:, n // 2, bass.ds(BJ * half, BJ)], banks[:, TP + n % 4, 0:BJ], ACT.Identity,
                                         bias=bias[b][:, n // 2:n // 2 + 1]).then_inc(kv_done, 1)

            def exponent(n, u):
                act.wait_ge(sub_done, SUB0 + n + 1)
                nc.scalar.activation(probs[0:M, u, :], probs[0:M, u, :], ACT.Exp).then_inc(exp_done, 1)

            def element(n, u, last):
                act.wait_ge(v_ready, V0 + n + 1)
                act.wait_ge(o_ready, O0 + n - 1)
                nc.scalar.activation(v_b[0:J, u, :], banks[0:J, V, :], ACT.Copy).then_inc(v_done, 1)
                for r in (0, 2):
                    act.wait_ge(t_ready, T0 + 4 * n + r + 1)
                    act.wait_ge(o_ready, O0 + n)
                    nc.scalar.activation(probs_t[0:J, 4 * M * r:4 * M * r + 4 * M], banks[0:J, TP, 0:4 * M], ACT.Copy).then_inc(ta_done, 1)
                if not last:
                    exponent(n + 1, (u + 1) % 2)
                act.wait_ge(o_ready, O0 + n + 1)
                nc.scalar.activation(xn_hi[:, :, bass.ds(M * n, M)], banks[:, O, 0:KD * M].rearrange("p (k q) -> p k q", q=M),
                                     ACT.Copy).then_inc(ohi_done, 1)

            exponent(0, 0)
            with act.Fori(0, B // 2 - 1) as i:
                element(2 * i, 0, False)
                element(2 * i + 1, 1, False)
            element(B - 2, 0, False)
            element(B - 1, 1, True)
            for n in range(2 * KD):
                half, d = n // KD, n % KD
                act.wait_ge(y_ready, n + 1)
                nc.scalar.activation(y_t[:, d, HT * half:HT * half + HT], banks[:, n % 4, 0:HT], ACT.Identity,
                                     bias=bias["o"][:, d:d + 1]).then_inc(y_done, 1)

        @block.tensor
        def _(pe):
            for s, start in ((ctx_ready, 1), (kv_ready, 1), (s_ready, S0), (v_ready, V0), (t_ready, T0), (o_ready, O0)):
                pe.sem_inc(s, start)
            pe.wait_ge(const_done, 4)
            for n in range(FILLS):
                if n >= 4:
                    pe.wait_ge(fill_done, n - 3)
                if n < 4 * KD:
                    w, k = n // KD, n % KD
                    pe.wait_ge(w_loaded[w], 16)
                    for c in range(KD):
                        ins = nc.tensor.transpose(banks[:, n % 4, P * c:P * c + P], raw[:, w, c, P * k:P * k + P], ident[:, :])
                else:
                    b = n - 4 * KD
                    pe.wait_ge(norm_done, b + 1)
                    for k in range(KD):
                        ins = nc.tensor.transpose(banks[:, n % 4, P * k:P * k + M], x_tok[0:M, b, P * k:P * k + P], ident[0:M, 0:M])
                ins.then_inc(fill_ready, 1)
            pe.wait_ge(fill_done, FILLS)
            for n in range(2 * KD):
                half, m = n // KD, n % KD
                if n >= 4:
                    pe.wait_ge(q_done, n - 3)
                t = slice(HT * half, HT * half + HT)
                c = slice(P * m, P * m + P)
                for k in range(KD):
                    ins = three(nc, banks[:, TP + n % 4, 0:HT], wq_hi[:, k, c], wq_lo[:, k, c], xn_hi[:, k, t], xn_lo[:, k, t], k == 0, k == KD - 1)
                ins.then_inc(q_ready, 1)
            pe.wait_ge(q_done, 2 * KD)

            with pe.Fori(0, 2) as half:
                for u in range(2 * HB):
                    bl, hh = u // 2, u % 2
                    n = 2 * HB * half + u
                    pe.wait_ge(rows_loaded[hh], 16 * (HB * half + bl + 1))
                    for k in range(KD):
                        pe.wait_ge((ctx_a, ctx_b)[k % 2], CTX0 + 2 * n - 1 + k // 2)
                        pe.sem_inc(held, 1)
                        for h in range(HH):
                            ins = nc.tensor.transpose(banks[:, S + k, J * h:J * h + J], rows[0:J, hh, D * h + P * k:D * h + P * k + P], ident[0:J, 0:J])
                        ins.then_inc(ctx_ready, 1)
                pe.wait_ge(ctx_a, CTX0 + 4 * HB * (half + 1))
                pe.wait_ge(ctx_b, CTX0 + 4 * HB * (half + 1))
                for n in range(2 * KD):
                    w = (wk_t, wv_t)[n % 2]
                    pe.wait_ge(kv_done, KV0 + 2 * KD * half + n - 3)
                    for k in range(KD):
                        for r in range(QH):
                            h = QH * (n // 2) + r
                            ins = nc.tensor.matmul(banks[HD * r:HD * r + HD, TP + n % 4, 0:BJ], w[:, k, HD * h:HD * h + HD], ctx_t[:, k, h, :],
                                                   start=(k == 0), stop=(k == KD - 1))
                    ins.then_inc(kv_ready, 1)

            def scores(n, u):
                pe.wait_ge(qv_done, 1 + n + 1)
                pe.wait_ge(sub_done, SUB0 + n - 1)
                for h in range(H):
                    c = J * (h % HH)
                    ins = nc.tensor.matmul(banks[0:M, S + 2 * u + h // HH, c:c + J], q_b[:, u, h, :], k_t[:, h // QH, bass.ds(J * n, J)],
                                           start=True, stop=True)
                ins.then_inc(s_ready, 1)

            def element(n, u, last):
                if not last:
                    scores(n + 1, (u + 1) % 2)
                pe.wait_ge(v_done, 1 + n)
                pe.sem_inc(held, 1)
                for c in range(KD):
                    ins = nc.tensor.transpose(banks[0:J, V, P * c:P * c + P], v_tb[:, u, c, :], ident[:, :])
                ins.then_inc(v_ready, 1)
                pe.wait_ge(p_done, 1 + n + 1)
                for r in range(4):
                    pe.wait_ge((ta_done, tb_done)[r % 2], 1 + 2 * n + r // 2)
                    pe.sem_inc(held, 1)
                    for x in range(4):
                        h = 4 * r + x
                        ins = nc.tensor.transpose(banks[0:J, TP + r % 2, M * x:M * x + M], probs[0:M, u, J * h:J * h + J], ident[0:M, 0:M])
                    ins.then_inc(t_ready, 1)
                pe.wait_ge(ta_done, 1 + 2 * n + 2)
                pe.wait_ge(tb_done, 1 + 2 * n + 2)
                pe.wait_ge(v_done, 1 + n + 1)
                pe.wait_ge(olo_done, 1 + n)
                pe.sem_inc(held, 1)
                for h in range(H):
                    p, c = HD * (h % QH), M * (h // QH)
                    ins = nc.tensor.matmul(banks[p:p + HD, O, c:c + M], v_b[0:J, u, HD * h:HD * h + HD], probs_t[0:J, M * h:M * h + M],
                                           start=True, stop=True)
                ins.then_inc(o_ready, 1)

            pe.wait_ge(kv_done, KV0 + 4 * KD)
            scores(0, 0)
            with pe.Fori(0, B // 2 - 1) as i:
                element(2 * i, 0, False)
                element(2 * i + 1, 1, False)
            element(B - 2, 0, False)
            element(B - 1, 1, True)
            pe.wait_ge(olo_done, 1 + B)
            for n in range(2 * KD):
                half, d = n // KD, n % KD
                if n >= 4:
                    pe.wait_ge(y_done, n - 3)
                t = slice(HT * half, HT * half + HT)
                c = slice(P * d, P * d + P)
                for k in range(KD):
                    ins = three(nc, banks[:, n % 4, 0:HT], wo_hi[:, k, c], wo_lo[:, k, c], xn_hi[:, k, t], xn_lo[:, k, t], k == 0, k == KD - 1)
                ins.then_inc(y_ready, 1)
            for b in range(B):
                pe.wait_ge(y_done, KD * (1 + b // HB))
                if b >= 4:
                    pe.wait_ge(x_done, b - 3)
                for k in range(KD):
                    ins = nc.tensor.transpose(banks[0:M, 4 + b % 4, P * k:P * k + P], y_t[:, k, M * b:M * b + M], ident[:, :])
                ins.then_inc(out_ready, 1)

        @block.vector
        def _(dve):
            for s, start in ((ctx_b, CTX0), (sub_done, SUB0), (p_done, 1), (tb_done, 1), (olo_done, 1), (chain, 1)):
                dve.sem_inc(s, start)
            own = Chain(dve, chain)
            for b in range(B):
                if b % HB == 0:
                    dve.wait_ge(x_loaded[b // HB], 32)
                ins = nc.vector.bn_stats(stats[0:M, b, :], x_tok[0:M, b, :])
            own.link(ins)
            for b in range(B):
                ins = nc.vector.bn_aggr(mean_var[0:M, b, :], stats[0:M, b, :])
            ins.then_inc(var_done, 1)
            dve.wait_ge(std_done, 1)
            own.link(nc.vector.reciprocal(rstd[0:M, :], std[0:M, :]))
            for b in range(B):
                nc.vector.tensor_scalar(x_tok[0:M, b, :], x_tok[0:M, b, :], mean_var[0:M, b, 0:1], rstd[0:M, b:b + 1],
                                        ALU.subtract, ALU.mult).then_inc(norm_done, 1)
            for n in range(FILLS):
                bank = banks[:, n % 4, :]
                if KD <= n < 3 * KD:
                    dve.wait_ge(fill_ready, n + 1)
                    nc.vector.tensor_copy((wk_t, wv_t)[n // KD - 1][:, n % KD, :], bank).then_inc(fill_done, 1)
                elif n < 4 * KD:
                    hi, lo = (wq_hi, wq_lo) if n < KD else (wo_hi, wo_lo)
                    dve.wait_ge(fill_hi, n + 1 if n < KD else n + 1 - 2 * KD)
                    nc.vector.tensor_tensor(lo[:, n % KD, :], bank, hi[:, n % KD, :].bitcast(F32), ALU.subtract).then_inc(fill_done, 1)
                else:
                    b = n - 4 * KD
                    dve.wait_ge(fill_hi, n + 1 - 2 * KD)
                    t = slice(M * b, M * b + M)
                    nc.vector.tensor_tensor(xn_lo[:, :, t], bank.rearrange("p (k q) -> p k q", q=P)[:, :, 0:M], xn_hi[:, :, t].bitcast(F32),
                                            ALU.subtract).then_inc(fill_done, 1)
            dve.wait_ge(c_loaded, 80)
            for n in range(2 * KD):
                half, m = n // KD, n % KD
                dve.wait_ge(q_ready, n + 1)
                nc.vector.tensor_scalar(q_t[:, m, HT * half:HT * half + HT], banks[:, TP + n % 4, 0:HT], bias["q"][:, m:m + 1], SCALE,
                                        ALU.add, ALU.mult).then_inc(q_done, 1)

            with dve.Fori(0, 2) as half:
                for u in range(2 * HB):
                    bl, hh = u // 2, u % 2
                    for k in range(1, KD, 2):
                        dve.wait_ge(ctx_ready, 1 + KD * (2 * HB * half + u) + k + 1)
                        nc.vector.tensor_copy(ctx_t[:, k, HH * hh:HH * hh + HH, J * bl:J * bl + J],
                                              banks[:, S + k, 0:HH * J].rearrange("p (h j) -> p h j", j=J)).then_inc(ctx_b, 1)

            def rowwise(t):
                return t[0:M, :, :].unsqueeze(3).to_broadcast([M, 2, HH, J])

            def lower(n, u):
                s = banks[0:M, S + 2 * u:S + 2 * u + 2, 0:HH * J].rearrange("p r (h j) -> p r h j", j=J)
                dve.wait_ge(s_ready, S0 + n + 1)
                own.link(nc.vector.tensor_reduce(s_max[0:M, :, :], s, axis=AX.X, op=ALU.max))
                dve.wait_ge(t_ready, T0 + 4 * (n - 1))
                nc.vector.tensor_tensor(probs[0:M, u, :].rearrange("p (r h j) -> p r h j", h=HH, j=J), s, rowwise(s_max), ALU.subtract).then_inc(sub_done, 1)

            def element(n, u, last):
                p = probs[0:M, u, :].rearrange("p (r h j) -> p r h j", h=HH, j=J)
                dve.wait_ge(exp_done, 1 + n + 1)
                own.link(nc.vector.tensor_reduce(s_sum[0:M, :, :], p, axis=AX.X, op=ALU.add))
                own.link(nc.vector.reciprocal(s_sum[0:M, :, :], s_sum[0:M, :, :]))
                nc.vector.tensor_tensor(p, p, rowwise(s_sum), ALU.mult).then_inc(p_done, 1)
                if not last:
                    lower(n + 1, (u + 1) % 2)
                for r in (1, 3):
                    dve.wait_ge(t_ready, T0 + 4 * n + r + 1)
                    dve.wait_ge(o_ready, O0 + n)
                    nc.vector.tensor_copy(probs_t[0:J, 4 * M * r:4 * M * r + 4 * M], banks[0:J, TP + 1, 0:4 * M]).then_inc(tb_done, 1)
                dve.wait_ge(ohi_done, 1 + n + 1)
                t = bass.ds(M * n, M)
                nc.vector.tensor_tensor(xn_lo[:, :, t], banks[:, O, 0:KD * M].rearrange("p (k q) -> p k q", q=M), xn_hi[:, :, t].bitcast(F32),
                                        ALU.subtract).then_inc(olo_done, 1)

            lower(0, 0)
            with own.loop(B // 2 - 1, 6) as i:
                element(2 * i, 0, False)
                element(2 * i + 1, 1, False)
            element(B - 2, 0, False)
            element(B - 1, 1, True)
            dve.wait_ge(tanh_done, 1)
            dve.wait_ge(x_again, 16)
            for b in range(B):
                dve.wait_ge(out_ready, b + 1)
                nc.vector.scalar_tensor_tensor(x_res[0:M, b, :], banks[0:M, 4 + b % 4, :], tanh_g[0:M, 0:1], x_res[0:M, b, :],
                                               ALU.mult, ALU.add).then_inc(x_done, 1)


def flamingo_layers(nc, x, ctx_1024, mask_BxS2_bk0, g_xattn, g_ffn,
                    a_ln_x_g, a_ln_x_b, a_ln_l_g, a_ln_l_b, a_wq, a_wkv, a_wout, a_ln_o_g, a_ln_o_b,
                    f_router_w, f_router_b, f_w1, f_w3, f_w2,
                    g_wq, g_bq, g_wk, g_bk, g_wv, g_bv, g_wo, g_bo,
                    m_wg, m_w1, m_w2, m_w3, out):
    x1, x2, x3 = (nc.dram_tensor(f"x_after_{n}", x.shape, F32, kind="Internal").ap() for n in range(1, 4))
    with nc.cleanup_on_exit():
        perceiver_attention(nc, ctx_1024, x, mask_BxS2_bk0, a_ln_x_g, a_ln_x_b, a_ln_l_g, a_ln_l_b, a_wq, a_wkv, a_wout,
                            a_ln_o_g, a_ln_o_b, g_xattn[0:1], x1)
    with nc.cleanup_on_exit():
        gated_experts(nc, "f", x1, f_router_w, f_router_b, f_w1, f_w3, f_w2, False, g_ffn[0:1], x2)
    with nc.cleanup_on_exit():
        strided_attention(nc, x2, ctx_1024, g_wq, g_bq, g_wk, g_bk, g_wv, g_bv, g_wo, g_bo, g_xattn[1:2], x3)
    with nc.cleanup_on_exit():
        gated_experts(nc, "m", x3, m_wg, None, m_w1, m_w2, m_w3, True, g_ffn[1:2], out)


_INS = ["x", "ctx_1024", "mask_BxS2_bk0", "g_xattn", "g_ffn",
        "L0_xattn_ln_x_g", "L0_xattn_ln_x_b", "L0_xattn_ln_l_g", "L0_xattn_ln_l_b", "L0_xattn_Wq", "L0_xattn_Wkv",
        "L0_xattn_Wout", "L0_xattn_ln_o_g", "L0_xattn_ln_o_b",
        "L0_ffn_router_w", "L0_ffn_router_b", "L0_ffn_w1", "L0_ffn_w3", "L0_ffn_w2",
        "L1_xattn_Wq", "L1_xattn_bq", "L1_xattn_Wk", "L1_xattn_bk", "L1_xattn_Wv", "L1_xattn_bv", "L1_xattn_Wo", "L1_xattn_bo",
        "L1_ffn_Wg", "L1_ffn_W1", "L1_ffn_W2", "L1_ffn_W3"]


def kernel(**inputs):
    import numpy as _np
    import concourse.bacc as _bacc
    from concourse import mybir as _mybir
    from concourse.bass_utils import run_bass_kernel_spmd as _run

    nc = _bacc.Bacc("TRN2", target_bir_lowering=False, num_devices=1, dynamic_dma_scratch_size=4096)
    arrays, args = {}, []
    for name in _INS:
        a = _np.ascontiguousarray(inputs[name])
        arrays[name] = a
        args.append(nc.dram_tensor(name, a.shape, _mybir.dt.from_np(a.dtype), kind="ExternalInput").ap())
    args.append(nc.dram_tensor("out", inputs["x"].shape, F32, kind="ExternalOutput").ap())
    flamingo_layers(nc, *args)
    r = _run(nc, [arrays], core_ids=[0])
    return r.results[0]["out"]
```

```python
import concourse.bass as bass
from concourse import mybir
from contextlib import ExitStack, contextmanager

F32 = mybir.dt.float32
F32R = mybir.dt.float32r
U8 = mybir.dt.uint8
ALU = mybir.AluOpType
ACT = mybir.ActivationFunctionType
AX = mybir.AxisListType


class Chain:

    def __init__(self, eng, sem):
        self.eng, self.sem, self.base, self.n = eng, sem, 1, 0

    def link(self, ins):
        self.n += 1
        ins.then_inc(self.sem, 1)
        self.eng.wait_ge(self.sem, self.base + self.n)

    @contextmanager
    def loop(self, turns, per):
        start = self.base + self.n
        with self.eng.Fori(0, turns) as i:
            self.base, self.n = start + per * i, 0
            yield i
        assert self.n == per, (self.n, per)
        self.base, self.n = start + per * turns, 0


def perceiver_attention(nc, ctx_rows, x_in, keep_mask, ln_x_g, ln_x_b, ln_l_g, ln_l_b, wq, wkv, wout,
                        ln_o_g, ln_o_b, gate, x_out):
    B, M, D = x_in.shape
    N = ctx_rows.shape[1]
    P = 128
    HD = 64
    INNER = wq.shape[1]
    PAIRS = INNER // P
    HALF = INNER // 2
    KD = D // P
    KEYS = N + M
    CT = (N + P - 1) // P
    CROWS = [min(P, N - P * t) for t in range(CT)]
    LAT = CT
    NT = CT + 1
    TILE_ROWS = CROWS + [M]
    TILE_COL = [P * t for t in range(CT)] + [N]
    KT = (KEYS + P - 1) // P
    KROWS = [min(P, KEYS - P * t) for t in range(KT)]
    BANK = 512
    PART = [(0, BANK), (BANK, KEYS - BANK)]
    FIRST_T = 4
    EPS = 1e-5
    FAR = float(2.0 ** 100)
    SCALE = HD ** -0.5

    with ExitStack() as ctx:
        def sb(name, shape, dt=F32):
            return ctx.enter_context(nc.sbuf_tensor("a_" + name, shape, dt))

        def ps(name, shape):
            return ctx.enter_context(nc.psum_tensor("a_" + name, shape, F32))

        def sem(name):
            return nc.alloc_semaphore("a_" + name)

        wkv_hi = sb("wkv_hi", [P, KD, 2 * INNER], F32R)
        wkv_lo = sb("wkv_lo", [P, KD, 2 * INNER], F32R)
        wq_sb = sb("wq_sb", [P, KD, INNER])
        wout_sb = sb("wout_sb", [P, PAIRS, D])
        rows = sb("rows", [P, CT, D])
        lat = sb("lat", [P, D])
        kvin_hi = sb("kvin_hi", [P, KD, KEYS], F32R)
        kvin_lo = sb("kvin_lo", [P, KD, KEYS], F32R)
        lat_t = sb("lat_t", [P, KD, M])
        k_hi = sb("k_hi", [P, 2, KEYS], F32R)
        k_lo = sb("k_lo", [P, 2, KEYS], F32R)
        v_sb = sb("v_sb", [P, KT, HALF])
        q_hi = sb("q_hi", [P, PAIRS, 2, M], F32R)
        q_lo = sb("q_lo", [P, PAIRS, 2, M], F32R)
        probs = sb("probs", [P, 2, KT * P])
        probs_t = sb("probs_t", [P, 2, KT * M])
        out_t = sb("out_t", [P, PAIRS, M])
        mask_u8 = sb("mask_u8", [P, N], U8)
        mask_add = sb("mask_add", [P, KEYS])
        res = sb("res", [P, D])
        tail = sb("tail", [P, D])
        gain_o = sb("gain_o", [P, D])
        bias_o = sb("bias_o", [P, D])
        gain_x, bias_x, gain_l, bias_l = (sb(n, [P, D]) for n in ("gain_x", "bias_x", "gain_l", "bias_l"))
        tanh_g = sb("tanh_g", [P, 1])
        eps = sb("eps", [P, 1])
        ident = sb("ident", [P, P])
        stats = sb("stats", [P, NT, 6])
        mean_var = sb("mean_var", [P, NT, 2])
        std = sb("std", [P, NT])
        rstd = sb("rstd", [P, NT])
        neg_max = sb("neg_max", [P, 2])
        row_sum = sb("row_sum", [P, 2])
        row_inv = sb("row_inv", [P, 2])
        stage = v_sb[:, :, :].rearrange("p t n -> p (t n)")
        SW = INNER

        kv_ps = ps("kv_ps", [P, 2 * BANK])
        s_ps = ps("s_ps", [P, 2 * BANK])
        t_ps = ps("t_ps", [P, 2 * BANK])
        o_ps = ps("o_ps", [P, BANK])
        w_ps = ps("w_ps", [P, BANK])

        c_loaded = sem("c_loaded")
        w_loaded = [sem(f"w_loaded{n}") for n in range(2)]
        w_hi_done = sem("w_hi_done")
        w_lo_done = sem("w_lo_done")
        pq_loaded = sem("pq_loaded")
        rows_loaded = sem("rows_loaded")
        mask_loaded = sem("mask_loaded")
        res_loaded = sem("res_loaded")
        x_stored = sem("x_stored")
        const_done = sem("const_done")
        tanh_done = sem("tanh_done")
        mask_done = sem("mask_done")
        var_done = sem("var_done")
        std_done = sem("std_done")
        norm_done = sem("norm_done")
        tr_done = sem("tr_done")
        scaled_done = sem("scaled_done")
        in_hi_done = sem("in_hi_done")
        in_lo_done = sem("in_lo_done")
        q_ready = sem("q_ready")
        q_hi_done = sem("q_hi_done")
        q_lo_done = sem("q_lo_done")
        v_ready = sem("v_ready")
        v_done = sem("v_done")
        k_ready = sem("k_ready")
        k_hi_done = sem("k_hi_done")
        k_lo_done = sem("k_lo_done")
        s_ready = sem("s_ready")
        max_done = sem("max_done")
        exp_done = sem("exp_done")
        p_done = sem("p_done")
        t_ready = sem("t_ready")
        ta_done = sem("ta_done")
        tb_done = sem("tb_done")
        o_ready = sem("o_ready")
        o_done = sem("o_done")
        y_ready = sem("y_ready")
        y_read = sem("y_read")
        x_done = sem("x_done")
        held = sem("held")
        chain = sem("chain")
        pool_chain = sem("pool_chain")

        block = ctx.enter_context(nc.Block())


        @block.sync
        def _(sp):
            for s in (x_stored, rows_loaded, mask_loaded, res_loaded):
                sp.sem_inc(s, 1)

            def load_rows(b):
                full = P * (CT - 1)
                sp.dma_start(rows[:, 0:CT - 1, :], ctx_rows[b, 0:full, :].rearrange("(t p) d -> p t d", p=P)).then_inc(rows_loaded, 16)
                sp.dma_start(rows[0:CROWS[-1], CT - 1, :], ctx_rows[b, full:N, :]).then_inc(rows_loaded, 16)
                sp.dma_start(lat[0:M, :], x_in[b, :, :]).then_inc(rows_loaded, 16)

            def load_mask(b):
                sp.dma_start(mask_u8[0:M, :], keep_mask[b, :].rearrange("(a n) -> a n", a=1).to_broadcast([M, N])).then_inc(mask_loaded, 16)

            def load_res(b):
                sp.dma_start(res[0:M, :], x_in[b, :, :]).then_inc(res_loaded, 16)

            load_rows(0)
            for t, src in ((gain_x, ln_x_g), (bias_x, ln_x_b), (gain_l, ln_l_g), (bias_l, ln_l_b)):
                sp.dma_start(t[:, :], src.rearrange("(a n) -> a n", a=1).to_broadcast([P, D])).then_inc(c_loaded, 16)
            sp.dma_start(gain_o[0:M, :], ln_o_g.rearrange("(a n) -> a n", a=1).to_broadcast([M, D])).then_inc(c_loaded, 16)
            sp.dma_start(bias_o[0:M, :], ln_o_b.rearrange("(a n) -> a n", a=1).to_broadcast([M, D])).then_inc(c_loaded, 16)
            sp.dma_start(tanh_g[:, :], gate.to_broadcast([P, 1])).then_inc(c_loaded, 16)
            sp.dma_start(wq_sb[:, :, :], wq.rearrange("(k p) n -> p k n", p=P)).then_inc(pq_loaded, 16)
            for n in range(2 * KD):
                if n >= 2:
                    sp.wait_ge(w_lo_done, 1 + n - 1)
                sp.dma_start(stage[:, SW * (n % 2):SW * (n % 2 + 1)],
                             wkv[P * (n // 2):P * (n // 2 + 1), SW * (n % 2):SW * (n % 2 + 1)]).then_inc(w_loaded[n % 2], 16)
            sp.dma_start(wout_sb[:, :, :], wout.rearrange("(k p) n -> p k n", p=P)).then_inc(pq_loaded, 16)
            load_mask(0)
            load_res(0)

            def turn(i, last):
                if not last:
                    sp.wait_ge(tr_done, 1 + NT * i + NT)
                    sp.sem_inc(held, 1)
                    load_rows(i + 1)
                    sp.wait_ge(mask_done, 1 + i + 1)
                    sp.sem_inc(held, 1)
                    load_mask(i + 1)
                sp.wait_ge(x_done, 1 + i + 1)
                sp.sem_inc(held, 1)
                sp.dma_start(x_out[i, :, :], tail[0:M, :]).then_inc(x_stored, 16)
                if not last:
                    load_res(i + 1)

            with sp.Fori(0, B - 1) as i:
                turn(i, False)
            turn(B - 1, True)
            sp.wait_ge(x_stored, 1 + 16 * B)

        @block.gpsimd
        def _(pool):
            for s in (const_done, scaled_done, pool_chain):
                pool.sem_inc(s, 1)
            own = Chain(pool, pool_chain)
            nc.gpsimd.memset(ident[:, :], 0.0).then_inc(const_done, 1)
            nc.gpsimd.memset(probs[:, :, :], 0.0).then_inc(const_done, 1)
            nc.gpsimd.memset(mask_add[:, :], 0.0).then_inc(const_done, 1)
            nc.gpsimd.memset(mean_var[:, :, :], 1.0).then_inc(const_done, 1)
            nc.gpsimd.memset(q_hi[:, :, :, :].bitcast(F32), 0.0).then_inc(const_done, 1)
            nc.gpsimd.memset(q_lo[:, :, :, :].bitcast(F32), 0.0).then_inc(const_done, 1)
            nc.gpsimd.memset(eps[:, :], EPS).then_inc(const_done, 1)
            pool.wait_ge(const_done, 2)
            nc.gpsimd.affine_select(out=ident[:, :], in_=ident[:, :], compare_op=ALU.not_equal, fill=1.0, base=0,
                                    pattern=[[-1, P]], channel_multiplier=1).then_inc(const_done, 1)

            def scale(p):
                for t in range(NT):
                    n = TILE_ROWS[t]
                    pool.wait_ge(norm_done, 1 + NT * p + t + 1)
                    row = lat[0:M, :] if t == LAT else rows[0:n, t, :]
                    g, b = (gain_l, bias_l) if t == LAT else (gain_x, bias_x)
                    pool.sem_inc(held, 1)
                    own.link(nc.gpsimd.tensor_tensor(row, row, g[0:n, :], ALU.mult))
                    nc.gpsimd.tensor_tensor(row, row, b[0:n, :], ALU.add).then_inc(scaled_done, 1)

            pool.wait_ge(c_loaded, 16 * 7)
            scale(0)
            pool.wait_ge(w_lo_done, 1 + 2 * KD)
            nc.gpsimd.memset(v_sb[:, KT - 1, :], 0.0).then_inc(const_done, 1)
            with own.loop(B - 1, NT) as i:
                scale(i + 1)

        @block.scalar
        def _(act):
            for s in (tanh_done, in_hi_done, q_hi_done, v_done, k_hi_done, exp_done, ta_done, w_hi_done):
                act.sem_inc(s, 1)
            act.wait_ge(c_loaded, 16 * 7)
            nc.scalar.activation(tanh_g[:, :], tanh_g[:, :], ACT.Tanh).then_inc(tanh_done, 1)

            def deviations(p, first=False):
                act.wait_ge(var_done, 1 if first else 3 * p)
                nc.scalar.activation(std[:, 0:NT], mean_var[:, 0:NT, 1], ACT.Sqrt, bias=eps[:, :]).then_inc(std_done, 1)

            def deviation_lat(p, first=False):
                act.wait_ge(var_done, 2 if first else 3 * p + 1)
                nc.scalar.activation(std[0:M, LAT:NT], mean_var[0:M, LAT:NT, 1], ACT.Sqrt, bias=eps[0:M, :]).then_inc(std_done, 1)

            def prepare(p, t):
                n, c = TILE_ROWS[t], TILE_COL[t]
                act.wait_ge(tr_done, 1 + NT * p + t + 1)
                src = kv_ps[:, BANK * (t % 2):BANK * (t % 2) + BANK].rearrange("p (k q) -> p k q", q=P)[:, :, 0:n]
                if t == LAT:
                    act.wait_ge(q_ready, 1 + p)
                    nc.scalar.activation(lat_t[:, :, :], src, ACT.Copy)
                nc.scalar.activation(kvin_hi[:, :, c:c + n], src, ACT.Copy).then_inc(in_hi_done, 1)

            def queries(i):
                act.wait_ge(q_ready, 1 + i + 1)
                act.wait_ge(const_done, 10)
                for x in range(2):
                    for m in range(2):
                        n = PAIRS // 2
                        src = s_ps[HD * x:HD * x + HD, BANK * m:BANK * m + n * M].rearrange("p (h q) -> p h q", q=M)
                        ins = nc.scalar.activation(q_hi[HD * x:HD * x + HD, n * m:n * m + n, x, :], src, ACT.Copy, scale=SCALE)
                ins.then_inc(q_hi_done, 1)

            def values(i, half, t):
                act.wait_ge(v_ready, 1 + 2 * KT * i + KT * half + t + 1)
                act.wait_ge(o_ready, 1 + PAIRS * i + PAIRS // 2 * half)
                n = KROWS[t]
                nc.scalar.activation(v_sb[0:n, t, :], kv_ps[0:n, BANK * (t % 2):BANK * (t % 2) + HALF], ACT.Copy).then_inc(v_done, 1)

            def keys(i, hp, part):
                c, n = PART[part]
                act.wait_ge(k_ready, 1 + 2 * PAIRS * i + 2 * hp + part + 1)
                act.wait_ge(s_ready, 1 + 2 * PAIRS * i + (2 * hp - 2 if hp >= 2 else 0))
                nc.scalar.activation(k_hi[:, hp % 2, c:c + n], kv_ps[:, c:c + n], ACT.Copy).then_inc(k_hi_done, 1)

            def move_t(i, hp, r):
                act.wait_ge(t_ready, 1 + 4 * PAIRS * i + 4 * hp + r + 1)
                act.wait_ge(o_ready, 1 + PAIRS * i + hp)
                c, n = (0, FIRST_T * M) if r == 0 else (FIRST_T * M, (KT - FIRST_T) * M)
                nc.scalar.activation(probs_t[:, 0, c:c + n], t_ps[:, BANK * r:BANK * r + n], ACT.Copy).then_inc(ta_done, 1)

            def exponent(i, hp, x):
                act.wait_ge(max_done, 1 + 2 * PAIRS * i + 2 * hp + x + 1)
                nc.scalar.activation(probs[0:M, x, 0:KEYS], probs[0:M, x, 0:KEYS], ACT.Exp, scale=-1.0,
                                     bias=neg_max[0:M, x:x + 1], accum_out=row_sum[0:M, x:x + 1]).then_inc(exp_done, 1)

            act.wait_ge(const_done, 9)
            deviations(0, True)
            for n in range(2 * KD):
                act.wait_ge(w_loaded[n % 2], 16 * (n // 2 + 1))
                nc.scalar.activation(wkv_hi[:, n // 2, SW * (n % 2):SW * (n % 2 + 1)], stage[:, SW * (n % 2):SW * (n % 2 + 1)],
                                     ACT.Copy).then_inc(w_hi_done, 1)
                if n == 1:
                    deviation_lat(0, True)
            for t in range(NT):
                prepare(0, t)
            queries(0)
            keys(0, 0, 0)
            keys(0, 0, 1)

            def turn(i, last):
                for t in range(KT):
                    values(i, 0, t)
                    if t in (2, 4):
                        exponent(i, 0, (t - 2) // 2)
                move_t(i, 0, 0)
                move_t(i, 0, 1)
                keys(i, 1, 0)
                keys(i, 1, 1)
                for hp in range(1, PAIRS):
                    if hp >= 2:
                        move_t(i, hp - 1, 0)
                        move_t(i, hp - 1, 1)
                    for x in range(2):
                        if hp == PAIRS - 1 and not last:
                            prepare(i + 1, 2 * x)
                            prepare(i + 1, 2 * x + 1)
                        exponent(i, hp, x)
                        if hp + 1 < PAIRS:
                            keys(i, hp + 1, x)
                    if hp == PAIRS // 2:
                        for t in range(KT):
                            values(i, 1, t)
                            if not last and t == 2:
                                deviations(i + 1)
                            if not last and t == 4:
                                deviation_lat(i + 1)
                if not last:
                    prepare(i + 1, 4)
                move_t(i, PAIRS - 1, 0)
                move_t(i, PAIRS - 1, 1)
                if not last:
                    prepare(i + 1, 5)
                    prepare(i + 1, 6)
                    queries(i + 1)
                    keys(i + 1, 0, 0)
                    keys(i + 1, 0, 1)
                act.wait_ge(var_done, 3 * i + (3 if last else 5))
                nc.scalar.activation(std[0:M, 0:1], mean_var[0:M, 0:1, 1], ACT.Sqrt, bias=eps[0:M, :]).then_inc(std_done, 1)

            with act.Fori(0, B - 1) as i:
                turn(i, False)
            turn(B - 1, True)

        @block.tensor
        def _(pe):
            for s in (tr_done, q_ready, v_ready, k_ready, s_ready, t_ready, o_ready, y_ready):
                pe.sem_inc(s, 1)

            def three(out, hi_l, lo_l, hi_r, lo_r, first, last):
                nc.tensor.matmul(out, hi_l, hi_r, start=first, stop=False)
                nc.tensor.matmul(out, hi_l, lo_r, start=False, stop=False)
                return nc.tensor.matmul(out, lo_l, hi_r, start=False, stop=last)

            def prepare(p, t):
                n = TILE_ROWS[t]
                pe.wait_ge(scaled_done, 1 + NT * p + t + 1)
                if t < 2:
                    pe.wait_ge(k_lo_done, 1 + 2 * PAIRS * p)
                else:
                    pe.wait_ge(in_lo_done, 1 + NT * p + t - 1)
                for k in range(KD):
                    src = lat[0:M, P * k:P * k + P] if t == LAT else rows[0:n, t, P * k:P * k + P]
                    ins = nc.tensor.transpose(kv_ps[:, BANK * (t % 2) + P * k:BANK * (t % 2) + P * k + n], src, ident[0:n, 0:n])
                ins.then_inc(tr_done, 1)

            def queries(i):
                pe.wait_ge(in_hi_done, 1 + NT * i + NT)
                pe.wait_ge(max_done, 1 + 2 * PAIRS * i)
                for m in range(PAIRS):
                    c = BANK * (m // (PAIRS // 2)) + M * (m % (PAIRS // 2))
                    for k in range(KD):
                        ins = nc.tensor.matmul(s_ps[:, c:c + M], wq_sb[:, k, P * m:P * m + P], lat_t[:, k, :], start=(k == 0), stop=(k == KD - 1))
                ins.then_inc(q_ready, 1)

            def values(i, half, t):
                n = KROWS[t]
                if t >= 2:
                    pe.wait_ge(v_done, 1 + 2 * KT * i + KT * half + t - 1)
                elif half:
                    pe.wait_ge(k_lo_done, 1 + 2 * PAIRS * i + 2 * (PAIRS // 2 + 1) + t + 1)
                else:
                    pe.wait_ge(k_lo_done, 1 + 2 * PAIRS * i + t + 1)
                out = kv_ps[0:n, BANK * (t % 2):BANK * (t % 2) + HALF]
                for k in range(KD):
                    r = slice(P * t, P * t + n)
                    c = slice(INNER + HALF * half, INNER + HALF * half + HALF)
                    ins = three(out, kvin_hi[:, k, r], kvin_lo[:, k, r], wkv_hi[:, k, c], wkv_lo[:, k, c], k == 0, k == KD - 1)
                ins.then_inc(v_ready, 1)

            def keys(i, hp, part):
                if hp == 0:
                    pe.wait_ge(in_lo_done, 1 + NT * i + NT)
                elif hp == 1:
                    pe.wait_ge(v_done, 1 + 2 * KT * i + KT)
                elif hp == PAIRS // 2 + 2:
                    pe.wait_ge(v_done, 1 + 2 * KT * i + 2 * KT)
                else:
                    pe.wait_ge(k_lo_done, 1 + 2 * PAIRS * i + 2 * (hp - 1) + part + 1)
                c, n = PART[part]
                m = slice(P * hp, P * hp + P)
                for k in range(KD):
                    ins = three(kv_ps[:, c:c + n], wkv_hi[:, k, m], wkv_lo[:, k, m], kvin_hi[:, k, c:c + n], kvin_lo[:, k, c:c + n],
                                k == 0, k == KD - 1)
                ins.then_inc(k_ready, 1)

            def scores(i, hp, x):
                pe.wait_ge(k_lo_done, 1 + 2 * PAIRS * i + 2 * hp + 2)
                pe.wait_ge(q_lo_done, 1 + i + 1)
                pe.wait_ge(max_done, 1 + 2 * PAIRS * i + 2 * hp + x)
                for c, n in PART:
                    ins = three(s_ps[0:M, c:c + n], q_hi[:, hp, x, :], q_lo[:, hp, x, :], k_hi[:, hp % 2, c:c + n], k_lo[:, hp % 2, c:c + n],
                                True, True)
                ins.then_inc(s_ready, 1)

            def transposes(i, hp, x):
                pe.wait_ge(p_done, 1 + 2 * PAIRS * i + 2 * hp + x + 1)
                for r in range(2):
                    if x:
                        pe.wait_ge(ta_done, 1 + 2 * PAIRS * i + 2 * hp + r + 1)
                    else:
                        pe.wait_ge(tb_done, 1 + 2 * PAIRS * i + (2 * hp + r - 1 if hp else 0))
                    for t in (range(FIRST_T) if r == 0 else range(FIRST_T, KT)):
                        c = BANK * r + M * (t - FIRST_T * r)
                        ins = nc.tensor.transpose(t_ps[:, c:c + M], probs[0:M, x, P * t:P * t + P], ident[0:M, 0:M])
                    ins.then_inc(t_ready, 1)

            def attend(i, hp):
                pe.wait_ge(ta_done, 1 + 2 * PAIRS * i + 2 * hp + 2)
                pe.wait_ge(tb_done, 1 + 2 * PAIRS * i + 2 * hp + 2)
                pe.wait_ge(v_done, 1 + 2 * KT * i + KT * (1 + hp // (PAIRS // 2)))
                pe.wait_ge(o_done, 1 + PAIRS * i + hp)
                for t in range(KT):
                    for x in range(2):
                        c = HD * (2 * (hp % (PAIRS // 2)) + x)
                        ins = nc.tensor.matmul(o_ps[HD * x:HD * x + HD, 0:M], v_sb[:, t, c:c + HD], probs_t[:, x, M * t:M * t + M],
                                               start=(t == 0), stop=(t == KT - 1))
                ins.then_inc(o_ready, 1)

            def finish(i):
                pe.wait_ge(o_done, 1 + PAIRS * i + PAIRS)
                pe.wait_ge(y_read, 1 + i)
                for k in range(PAIRS):
                    ins = nc.tensor.matmul(w_ps[0:M, :], out_t[:, k, :], wout_sb[:, k, :], start=(k == 0), stop=(k == PAIRS - 1))
                ins.then_inc(y_ready, 1)

            pe.wait_ge(const_done, 9)
            for t in range(NT):
                prepare(0, t)
            pe.wait_ge(pq_loaded, 32)
            queries(0)
            pe.wait_ge(w_lo_done, 1 + 2 * KD)
            keys(0, 0, 0)
            keys(0, 0, 1)
            pe.wait_ge(const_done, 10)

            def turn(i, last):
                for t in range(KT):
                    values(i, 0, t)
                    if t in (1, 3):
                        scores(i, 0, t // 2)
                for x in range(2):
                    transposes(i, 0, x)
                    keys(i, 1, x)
                attend(i, 0)
                for hp in range(1, PAIRS):
                    for x in range(2):
                        if hp >= 2:
                            transposes(i, hp - 1, x)
                        scores(i, hp, x)
                        if hp + 1 < PAIRS:
                            keys(i, hp + 1, x)
                        elif not last:
                            prepare(i + 1, 2 * x)
                            prepare(i + 1, 2 * x + 1)
                    if hp >= 2:
                        attend(i, hp - 1)
                    if hp == PAIRS // 2:
                        for t in range(KT):
                            values(i, 1, t)
                for x in range(2):
                    if not last:
                        prepare(i + 1, 4 + x)
                    transposes(i, PAIRS - 1, x)
                if not last:
                    prepare(i + 1, 6)
                attend(i, PAIRS - 1)
                if not last:
                    queries(i + 1)
                finish(i)
                if not last:
                    keys(i + 1, 0, 0)
                    keys(i + 1, 0, 1)

            with pe.Fori(0, B - 1) as i:
                turn(i, False)
            turn(B - 1, True)

        @block.vector
        def _(dve):
            for s in (mask_done, norm_done, in_lo_done, q_lo_done, k_lo_done, max_done, p_done, tb_done, o_done, y_read,
                      x_done, w_lo_done, chain):
                dve.sem_inc(s, 1)
            own = Chain(dve, chain)

            def moments(p):
                dve.wait_ge(rows_loaded, 1 + 48 * (p + 1))
                for t in range(NT):
                    n = TILE_ROWS[t]
                    ins = nc.vector.bn_stats(stats[0:n, t, :], lat[0:M, :] if t == LAT else rows[0:n, t, :])
                own.link(ins)
                dve.sem_inc(held, 1)
                for t in range(NT):
                    n = TILE_ROWS[t]
                    ins = nc.vector.bn_aggr(mean_var[0:n, t, :], stats[0:n, t, :])
                ins.then_inc(var_done, 1)

            def normalise(p, first=False):
                dve.wait_ge(std_done, 1 if first else 3 * p)
                own.link(nc.vector.reciprocal(rstd[:, 0:NT], std[:, 0:NT]))
                own.link(nc.vector.tensor_scalar(lat[0:M, :], lat[0:M, :], mean_var[0:M, LAT, 0:1], rstd[0:M, LAT:NT], ALU.subtract, ALU.mult))
                own.link(nc.vector.bn_stats(stats[0:M, LAT, :], lat[0:M, :]))
                dve.sem_inc(held, 1)
                nc.vector.bn_aggr(mean_var[0:M, LAT, :], stats[0:M, LAT, :]).then_inc(var_done, 1)
                for t in range(CT):
                    n = TILE_ROWS[t]
                    nc.vector.tensor_scalar(rows[0:n, t, :], rows[0:n, t, :], mean_var[0:n, t, 0:1], rstd[0:n, t:t + 1],
                                            ALU.subtract, ALU.mult).then_inc(norm_done, 1)
                dve.wait_ge(std_done, 2 if first else 3 * p + 1)
                own.link(nc.vector.reciprocal(rstd[0:M, LAT:NT], std[0:M, LAT:NT]))
                nc.vector.tensor_scalar(lat[0:M, :], lat[0:M, :], mean_var[0:M, LAT, 0:1], rstd[0:M, LAT:NT],
                                        ALU.subtract, ALU.mult).then_inc(norm_done, 1)

            def prepare(p, t):
                n, c = TILE_ROWS[t], TILE_COL[t]
                dve.wait_ge(in_hi_done, 1 + NT * p + t + 1)
                src = kv_ps[:, BANK * (t % 2):BANK * (t % 2) + BANK].rearrange("p (k q) -> p k q", q=P)[:, :, 0:n]
                nc.vector.tensor_tensor(kvin_lo[:, :, c:c + n], src, kvin_hi[:, :, c:c + n].bitcast(F32), ALU.subtract).then_inc(in_lo_done, 1)

            def mask(i):
                dve.wait_ge(mask_loaded, 1 + 16 * (i + 1))
                nc.vector.tensor_scalar(mask_add[0:M, 0:N], mask_u8[0:M, :], 1.0, FAR, ALU.subtract, ALU.mult).then_inc(mask_done, 1)
                dve.wait_ge(mask_done, 1 + i + 1)

            def queries(i):
                dve.wait_ge(q_hi_done, 1 + i + 1)
                for x in range(2):
                    for m in range(2):
                        n = PAIRS // 2
                        src = s_ps[HD * x:HD * x + HD, BANK * m:BANK * m + n * M].rearrange("p (h q) -> p h q", q=M)
                        at = (slice(HD * x, HD * x + HD), slice(n * m, n * m + n), x, slice(0, M))
                        ins = nc.vector.scalar_tensor_tensor(q_lo[at], src, SCALE, q_hi[at].bitcast(F32), ALU.mult, ALU.subtract)
                ins.then_inc(q_lo_done, 1)

            def keys(i, hp, part):
                c, n = PART[part]
                dve.wait_ge(k_hi_done, 1 + 2 * PAIRS * i + 2 * hp + part + 1)
                nc.vector.tensor_tensor(k_lo[:, hp % 2, c:c + n], kv_ps[:, c:c + n], k_hi[:, hp % 2, c:c + n].bitcast(F32),
                                        ALU.subtract).then_inc(k_lo_done, 1)

            def maximum(i, hp, x):
                dve.wait_ge(s_ready, 1 + 2 * PAIRS * i + 2 * hp + x + 1)
                dve.wait_ge(t_ready, 1 + 4 * PAIRS * i + (4 * hp - 2 + 2 * x if hp else 0))
                dve.sem_inc(held, 1)
                nc.vector.tensor_tensor_reduce(out=probs[0:M, x, 0:KEYS], in0=s_ps[0:M, 0:KEYS], in1=mask_add[0:M, :], scale=-1.0,
                                               scalar=3.0e38, op0=ALU.add, op1=ALU.min, accum_out=neg_max[0:M, x:x + 1]).then_inc(max_done, 1)

            def divide(i, hp, x):
                dve.wait_ge(exp_done, 1 + 2 * PAIRS * i + 2 * hp + x + 1)
                own.link(nc.vector.reciprocal(row_inv[0:M, x:x + 1], row_sum[0:M, x:x + 1]))
                nc.vector.tensor_scalar(probs[0:M, x, 0:KEYS], probs[0:M, x, 0:KEYS], row_inv[0:M, x:x + 1], None, ALU.mult).then_inc(p_done, 1)

            def move_t(i, hp, r):
                dve.wait_ge(t_ready, 1 + 4 * PAIRS * i + 4 * hp + 2 + r + 1)
                dve.wait_ge(o_ready, 1 + PAIRS * i + hp)
                c, n = (0, FIRST_T * M) if r == 0 else (FIRST_T * M, (KT - FIRST_T) * M)
                nc.vector.tensor_copy(probs_t[:, 1, c:c + n], t_ps[:, BANK * r:BANK * r + n]).then_inc(tb_done, 1)

            def move_o(i, hp):
                dve.wait_ge(o_ready, 1 + PAIRS * i + hp + 1)
                dve.wait_ge(y_ready, 1 + i)
                nc.vector.tensor_copy(out_t[:, hp, :], o_ps[:, 0:M]).then_inc(o_done, 1)

            def finish(i, last):
                dve.wait_ge(y_ready, 1 + i + 1)
                own.link(nc.vector.bn_stats(stats[0:M, 0, :], w_ps[0:M, :]))
                dve.sem_inc(held, 1)
                nc.vector.bn_aggr(mean_var[0:M, 0, :], stats[0:M, 0, :]).then_inc(var_done, 1)
                dve.wait_ge(std_done, 3 * i + (3 if last else 5))
                own.link(nc.vector.reciprocal(rstd[0:M, 0:1], std[0:M, 0:1]))
                dve.wait_ge(x_stored, 1 + 16 * i)
                nc.vector.tensor_scalar(tail[0:M, :], w_ps[0:M, :], mean_var[0:M, 0, 0:1], rstd[0:M, 0:1], ALU.subtract, ALU.mult).then_inc(y_read, 1)
                dve.wait_ge(y_read, 1 + i + 1)
                own.link(nc.vector.tensor_tensor(tail[0:M, :], tail[0:M, :], gain_o[0:M, :], ALU.mult))
                own.link(nc.vector.tensor_tensor(tail[0:M, :], tail[0:M, :], bias_o[0:M, :], ALU.add))
                dve.wait_ge(res_loaded, 1 + 16 * (i + 1))
                nc.vector.scalar_tensor_tensor(tail[0:M, :], tail[0:M, :], tanh_g[0:M, 0:1], res[0:M, :], ALU.mult, ALU.add).then_inc(x_done, 1)

            dve.wait_ge(const_done, 9)
            moments(0)
            normalise(0, True)
            for n in range(2 * KD):
                dve.wait_ge(w_hi_done, 1 + n + 1)
                at = (slice(0, P), n // 2, slice(SW * (n % 2), SW * (n % 2 + 1)))
                nc.vector.tensor_tensor(wkv_lo[at], stage[:, SW * (n % 2):SW * (n % 2 + 1)], wkv_hi[at].bitcast(F32), ALU.subtract).then_inc(w_lo_done, 1)
            for t in range(NT):
                prepare(0, t)
            queries(0)
            keys(0, 0, 0)
            keys(0, 0, 1)
            dve.wait_ge(tanh_done, 2)
            dve.wait_ge(c_loaded, 16 * 7)

            def turn(i, last):
                mask(i)
                for x in range(2):
                    maximum(i, 0, x)
                    divide(i, 0, x)
                for x in range(2):
                    if x == 1:
                        move_t(i, 0, 0)
                        move_t(i, 0, 1)
                    keys(i, 1, x)
                move_o(i, 0)
                for hp in range(1, PAIRS):
                    for x in range(2):
                        maximum(i, hp, x)
                        if hp == PAIRS - 1 and not last:
                            prepare(i + 1, 2 * x)
                            prepare(i + 1, 2 * x + 1)
                        divide(i, hp, x)
                        if hp >= 2 and x == 0:
                            move_t(i, hp - 1, 0)
                            move_t(i, hp - 1, 1)
                        if hp + 1 < PAIRS:
                            keys(i, hp + 1, x)
                    if hp >= 2:
                        move_o(i, hp - 1)
                    if hp == PAIRS // 2 and not last:
                        moments(i + 1)
                        normalise(i + 1)
                if not last:
                    prepare(i + 1, 4)
                move_t(i, PAIRS - 1, 0)
                move_t(i, PAIRS - 1, 1)
                if not last:
                    prepare(i + 1, 5)
                    prepare(i + 1, 6)
                move_o(i, PAIRS - 1)
                if not last:
                    queries(i + 1)
                    keys(i + 1, 0, 0)
                    keys(i + 1, 0, 1)
                finish(i, last)

            with own.loop(B - 1, 2 * PAIRS + 9) as i:
                turn(i, False)
            turn(B - 1, True)


def three(nc, out, left_hi, left_lo, right_hi, right_lo, start, stop):
    nc.tensor.matmul(out, left_hi, right_hi, start=start, stop=False)
    nc.tensor.matmul(out, left_hi, right_lo, start=False, stop=False)
    return nc.tensor.matmul(out, left_lo, right_hi, start=False, stop=stop)


def gated_experts(nc, name, x_in, router, router_bias, w_a, w_b, w_y, out_major, gate, x_out):
    B, M, D = x_in.shape
    P = 128
    T = B * M
    HT = T // 2
    HB = B // 2
    KD = D // P
    if out_major:
        E, F = w_a.shape[0], w_a.shape[1]
    else:
        E, F = w_a.shape[0], w_a.shape[2]
    G = F // P
    TOP = 2
    TILES = (T + P - 1) // P
    SLOTS = (TOP * T - E) // P + E
    SLOTS += SLOTS % 2
    RESIDENT = not out_major
    STAGED = SLOTS if RESIDENT else 3
    RING = 3 * E if RESIDENT else 4
    BANK = 512
    EPS = 1e-5
    U32 = mybir.dt.uint32

    tokens_dram = nc.dram_tensor(f"{name}_tokens", [SLOTS * P, D], F32, kind="Internal").ap()
    y_dram = nc.dram_tensor(f"{name}_y", [SLOTS * P, D], F32, kind="Internal").ap()

    with ExitStack() as ctx:
        def sb(n, shape, dt=F32):
            return ctx.enter_context(nc.sbuf_tensor(f"{name}_{n}", shape, dt))

        def sem(n):
            return nc.alloc_semaphore(f"{name}_{n}")

        wab_hi = sb("wab_hi", [P, E, KD, 2 * P], F32R)
        wab_lo = sb("wab_lo", [P, E, KD, 2 * P], F32R)
        wy_hi = sb("wy_hi", [P, E, D], F32R)
        wy_lo = sb("wy_lo", [P, E, D], F32R)
        xs = sb("xs", [P, SLOTS, KD, P])
        x_hi = sb("x_hi", [P, STAGED, KD, P], F32R)
        x_lo = sb("x_lo", [P, STAGED, KD, P], F32R)
        y_acc = sb("y_acc", [P, SLOTS, D])
        ht_hi = sb("ht_hi", [P, SLOTS, P], F32R)
        ht_lo = sb("ht_lo", [P, SLOTS, P], F32R)
        raw = sb("raw", [P, RING, KD, P])
        s_sb = sb("s_sb", [P, 2, P])
        h_sb = sb("h_sb", [P, 2, P])
        ident = sb("ident", [P, P])
        expert = sb("expert", [1, SLOTS], U32)
        place = sb("place", [P, B, TOP], U32)
        gates = sb("gates", [P, B, TOP])
        tanh_g = sb("tanh_g", [P, 1])
        table = sb("table", [1, 2])

        x_tok = y_acc[:, 0:B, :]
        zeros = y_acc[:, B, :]
        slot_rows = y_acc
        y_got = xs[:, 0:TOP * B, :, :].rearrange("p s k q -> p s (k q)")
        free = [xs[:, :, :, :].rearrange("p s k q -> p (s k q)")]

        def cut(*dims):
            n = 1
            for d in dims:
                n *= d
            piece, free[0] = free[0][:, 0:n], free[0][:, n:]
            if len(dims) == 2:
                return piece.rearrange("p (a b) -> p a b", b=dims[1])
            if len(dims) == 3:
                return piece.rearrange("p (a b c) -> p a b c", b=dims[1], c=dims[2])
            return piece

        xn_t = cut(KD, T)
        logit_t = cut(T)
        r_raw = cut(D) if out_major else None
        r_t = cut(KD, E)
        r_bias = cut(1)
        logits, p_exp, rank, chosen, pos, work = (cut(B, E) for _ in range(6))
        above, equal = (cut(B, E, E) for _ in range(2))
        before, starts_of = (cut(E, E) for _ in range(2))
        l_max, p_sum, pos_f = cut(B), cut(B), cut(B)
        earlier = cut(P)
        ones = cut(P)
        threshold = cut(TILES)
        filled = cut(E, TILES)
        count, start, end = cut(E), cut(E), cut(E)
        slot_no = cut(SLOTS)
        passed = cut(SLOTS, E)
        expert_f = cut(SLOTS)
        eps = cut(1)
        stats, mean_var = cut(B, 6), cut(B, 2)
        std, rstd = cut(B), cut(B)

        banks = ctx.enter_context(nc.psum_tensor(f"{name}_banks", [P, 8, BANK], F32))
        H, HT_T, W = 0, 2, 6
        Y = (4, 5, 2, 3)

        x_loaded = [sem(f"x_loaded{n}") for n in range(2)]
        c_loaded = sem("c_loaded")
        raw_loaded = [sem(f"raw_loaded{n}") for n in range(RING)]
        zeroed = sem("zeroed")
        scattered = sem("scattered")
        rows_loaded = [sem(f"rows_loaded{n}") for n in range(SLOTS // 4)]
        y_stored = sem("y_stored")
        y_gathered = [sem(f"y_gathered{b}") for b in range(B)]
        x_again = sem("x_again")
        x_stored = sem("x_stored")
        const_done = sem("const_done")
        zero_tile = sem("zero_tile")
        acc_zeroed = sem("acc_zeroed")
        tanh_done = sem("tanh_done")
        var_done = sem("var_done")
        std_done = sem("std_done")
        norm_done = sem("norm_done")
        tr_done = sem("tr_done")
        xn_done = sem("xn_done")
        rt_ready = sem("rt_ready")
        rt_done = sem("rt_done")
        logit_ready = sem("logit_ready")
        logit_done = sem("logit_done")
        back_ready = sem("back_ready")
        shift_done = sem("shift_done")
        exp_done = sem("exp_done")
        chosen_done = sem("chosen_done")
        count_ready = sem("count_ready")
        expert_done = sem("expert_done")
        gates_done = sem("gates_done")
        place_done = sem("place_done")
        st_ready = sem("st_ready")
        xs_a = sem("xs_a")
        xs_b = sem("xs_b")
        tw_ready = sem("tw_ready")
        whi_done = sem("whi_done")
        wlo_done = sem("wlo_done")
        xhi_a = sem("xhi_a")
        xhi_b = sem("xhi_b")
        xlo_done = sem("xlo_done")
        h_ready = sem("h_ready")
        s_done = sem("s_done")
        h_done = sem("h_done")
        t_ready = sem("t_ready")
        hi_done = sem("hi_done")
        lo_done = sem("lo_done")
        y_ready = sem("y_ready")
        add_done = sem("add_done")
        x_done = sem("x_done")
        held = sem("held")
        chain = sem("chain")

        block = ctx.enter_context(nc.Block())


        def since(g, s, back):
            return 1 + SLOTS * g + max(s - back + 1, 0)

        PIECES = 3 * E
        LAST = 2 * E

        def last_pieces(s):
            n = SLOTS - 4
            return range(min(LAST + E * s // n, PIECES), min(LAST + E * (s + 1) // n, PIECES))

        def first_pieces(s):
            n = SLOTS - 4
            return range(min(LAST * s // n, LAST), min(LAST * (s + 1) // n, LAST))

        def number(g, c):
            return PIECES * g + c

        def loads(g, c):
            return PIECES // RING * g + c // RING + 1

        @block.sync
        def _(sp):
            for q in range(4):
                sp.dma_start(x_tok[0:M, 2 * q:2 * q + 2, :], x_in[2 * q:2 * q + 2].rearrange("b p d -> p b d")).then_inc(x_loaded[q // 2], 16)
            if out_major:
                sp.dma_start(r_raw[0:E, :], router[:, :]).then_inc(c_loaded, 16)
            else:
                sp.dma_start(r_t[:, :, :], router.rearrange("(k p) e -> p k e", p=P), allow_slow_non_contiguous=True).then_inc(c_loaded, 16)
                sp.dma_start(r_bias[0:E, :], router_bias.rearrange("(e a) -> e a", a=1), allow_slow_non_contiguous=True).then_inc(c_loaded, 16)
            sp.dma_start(tanh_g[:, :], gate.to_broadcast([P, 1])).then_inc(c_loaded, 16)

            def load(g, c):
                w, e = (w_y, c - LAST) if c >= LAST else ((w_a, w_b)[c % 2], c // 2)
                if (c >= LAST) == out_major:
                    dst, src = raw[:, c % RING, :, :], w[e, :, bass.ds(P * g, P)].rearrange("(k p) f -> p k f", p=P)
                else:
                    dst, src = raw[:, c % RING, :, :].rearrange("p k q -> p (k q)"), w[e, bass.ds(P * g, P), :]
                sp.dma_start(dst, src).then_inc(raw_loaded[c % RING], 16)

            def reload(g, c):
                sp.wait_ge(tw_ready if out_major else wlo_done, 1 + number(g, c) - RING + 1)
                sp.sem_inc(held, 1)
                load(g, c)

            for c in range(RING):
                load(0, c)
            sp.wait_ge(zero_tile, 1)
            sp.dma_start(tokens_dram.rearrange("(s p) d -> p s d", p=P), zeros.unsqueeze(1).to_broadcast([P, SLOTS, D])).then_inc(zeroed, 16)
            early = max(E, RING)
            for c in range(RING, early):
                reload(0, c)
            sp.wait_ge(scattered, 16 * TOP * B)
            for q in range(SLOTS // 4):
                sp.dma_start(slot_rows[:, 4 * q:4 * q + 4, :],
                             tokens_dram[4 * P * q:4 * P * q + 4 * P, :].rearrange("(s p) d -> p s d", p=P)).then_inc(rows_loaded[q], 16)
            for c in range(early, LAST):
                reload(0, c)
            with sp.Fori(0, G - 1) as g:
                for c in range(max(LAST, RING), PIECES):
                    reload(g, c)
                for c in range(max(LAST, RING)):
                    reload(g + 1, c)
            for c in range(max(LAST, RING), PIECES):
                reload(G - 1, c)
            for q in range(SLOTS // 4):
                sp.wait_ge(add_done, 1 + SLOTS * (G - 1) + 4 * q + 4)
                sp.dma_start(y_dram[4 * P * q:4 * P * q + 4 * P, :].rearrange("(s p) d -> p s d", p=P),
                             y_acc[:, 4 * q:4 * q + 4, :]).then_inc(y_stored, 16)
            sp.wait_ge(y_stored, 16 * (SLOTS // 4))
            sp.dma_start(x_tok[0:M, :, :], x_in.rearrange("b p d -> p b d")).then_inc(x_again, 16)
            for b in range(B):
                sp.wait_ge(x_done, b + 1)
                sp.dma_start(x_out[b, :, :], x_tok[0:M, b, :]).then_inc(x_stored, 16)
            sp.wait_ge(x_stored, 16 * B)

        def split_dst(ab, y, c):
            if c >= LAST:
                return y[:, c - LAST, :].rearrange("p (k q) -> p k q", q=P)
            return ab[:, c // 2, :, P * (c % 2):P * (c % 2) + P]

        def split_src(c):
            if out_major:
                return banks[:, W + c % 2, :].rearrange("p (k q) -> p k q", q=P)
            return raw[:, c % RING, :, :]

        @block.gpsimd
        def _(pool):
            pool.sem_inc(xlo_done, 1)
            if not out_major:
                pool.sem_inc(wlo_done, 1)

            def split(g, c):
                pool.wait_ge(whi_done, 1 + number(g, c) + 1)
                pool.sem_inc(held, 1)
                nc.gpsimd.tensor_tensor(split_dst(wab_lo, wy_lo, c), split_src(c), split_dst(wab_hi, wy_hi, c).bitcast(F32),
                                        ALU.subtract).then_inc(wlo_done, 1)

            nc.gpsimd.memset(zeros, 0.0).then_inc(zero_tile, 1)
            nc.gpsimd.memset(ident[:, :], 0.0).then_inc(const_done, 1)
            nc.gpsimd.memset(before, 1.0).then_inc(const_done, 1)
            nc.gpsimd.memset(earlier, 1.0).then_inc(const_done, 1)
            nc.gpsimd.memset(table[:, :], 0.0).then_inc(const_done, 1)
            nc.gpsimd.memset(eps, EPS).then_inc(const_done, 1)
            pool.wait_ge(const_done, 5)
            nc.gpsimd.affine_select(out=ident[:, :], in_=ident[:, :], compare_op=ALU.not_equal, fill=1.0, base=0,
                                    pattern=[[-1, P]], channel_multiplier=1).then_inc(const_done, 1)
            nc.gpsimd.affine_select(out=before, in_=before, compare_op=ALU.is_gt, fill=0.0, base=0,
                                    pattern=[[1, E], [-1, E]], channel_multiplier=0).then_inc(const_done, 1)
            nc.gpsimd.affine_select(out=earlier, in_=earlier, compare_op=ALU.is_gt, fill=0.0, base=0,
                                    pattern=[[1, P]], channel_multiplier=-1).then_inc(const_done, 1)
            nc.gpsimd.memset(ones, 1.0).then_inc(const_done, 1)
            for n in range(TILES):
                nc.gpsimd.memset(threshold[:, n:n + 1], float(P * n)).then_inc(const_done, 1)
            for n in range(SLOTS):
                nc.gpsimd.memset(slot_no[:, n:n + 1], float(n)).then_inc(const_done, 1)
            pool.wait_ge(zeroed, 16)
            pool.wait_ge(place_done, 1)
            for b in range(B):
                for k in range(TOP):
                    nc.gpsimd.indirect_dma_start(tokens_dram[:, :], bass.IndirectOffsetOnAxis(ap=place[0:M, b, k:k + 1], axis=0),
                                                 x_tok[0:M, b, :], None).then_inc(scattered, 16)
            if not out_major:
                for c in range(LAST):
                    split(0, c)
            pool.wait_ge(st_ready, SLOTS)
            nc.gpsimd.memset(y_acc[:, :, :], 0.0).then_inc(acc_zeroed, 1)

            def low_part(g, s):
                pool.wait_ge((xhi_a, xhi_b)[s % 2], 1 + SLOTS // 2 * g + s // 2 + 1)
                pool.sem_inc(held, 1)
                nc.gpsimd.tensor_tensor(x_lo[:, s % STAGED, :, :], xs[:, s, :, :], x_hi[:, s % STAGED, :, :].bitcast(F32), ALU.subtract).then_inc(xlo_done, 1)

            pool.wait_ge(xs_a, SLOTS // 2)
            pool.wait_ge(xs_b, SLOTS // 2)
            if RESIDENT:
                for s in range(SLOTS):
                    low_part(0, s)
                with pool.Fori(0, G - 1) as g:
                    for c in range(LAST, PIECES):
                        split(g, c)
                    for c in range(LAST):
                        split(g + 1, c)
                for c in range(LAST, PIECES):
                    split(G - 1, c)
            else:
                with pool.Fori(0, G) as g:
                    for s in range(SLOTS):
                        low_part(g, s)
            pool.wait_ge(y_stored, 16 * (SLOTS // 4))
            pool.wait_ge(h_ready, 1 + SLOTS * G)
            for b in range(B):
                for k in range(TOP):
                    nc.gpsimd.indirect_dma_start(y_got[0:M, TOP * b + k, :], None, y_dram[:, :],
                                                 bass.IndirectOffsetOnAxis(ap=place[0:M, b, k:k + 1], axis=0)).then_inc(y_gathered[b], 16)

        @block.scalar
        def _(act):
            for s in (whi_done, xhi_a, s_done, hi_done):
                act.sem_inc(s, 1)
            act.wait_ge(c_loaded, 16 * (2 if out_major else 3))
            nc.scalar.activation(tanh_g[:, :], tanh_g[:, :], ACT.Tanh).then_inc(tanh_done, 1)
            act.wait_ge(const_done, 5)
            act.wait_ge(var_done, 1)
            nc.scalar.activation(std[0:M, :], mean_var[0:M, :, 1], ACT.Sqrt, bias=eps[0:M, :]).then_inc(std_done, 1)
            if out_major:
                act.wait_ge(rt_ready, 1)
                nc.scalar.activation(r_t, banks[:, 0, 0:KD * E].rearrange("p (k e) -> p k e", e=E), ACT.Copy).then_inc(rt_done, 1)
            for b in range(B):
                act.wait_ge(tr_done, b + 1)
                nc.scalar.activation(xn_t[:, :, M * b:M * b + M], banks[:, 2 + b % 4, :].rearrange("p (k q) -> p k q", q=P)[:, :, 0:M],
                                     ACT.Copy).then_inc(xn_done, 1)
            for half in range(2):
                act.wait_ge(logit_ready, half + 1)
                src = banks[0:E, half, 0:HT]
                dst = logit_t[0:E, HT * half:HT * half + HT]
                if out_major:
                    nc.scalar.activation(dst, src, ACT.Copy).then_inc(logit_done, 1)
                else:
                    nc.scalar.activation(dst, src, ACT.Identity, bias=r_bias[0:E, :]).then_inc(logit_done, 1)
            act.wait_ge(shift_done, 1)
            nc.scalar.activation(p_exp[0:M, :, :], p_exp[0:M, :, :], ACT.Exp).then_inc(exp_done, 1)

            def split(g, c):
                if out_major:
                    act.wait_ge(tw_ready, 1 + number(g, c) + 1)
                else:
                    act.wait_ge(raw_loaded[c % RING], 16 * loads(g, c))
                nc.scalar.activation(split_dst(wab_hi, wy_hi, c), split_src(c), ACT.Copy).then_inc(whi_done, 1)

            def move_tokens(s):
                act.wait_ge(rows_loaded[s // 4], 16)
                act.wait_ge(st_ready, s + 1)
                nc.scalar.activation(xs[:, s, :, :], banks[:, s % 4, :].rearrange("p (k q) -> p k q", q=P), ACT.Copy).then_inc(xs_a, 1)

            def high_part(g, s):
                if s % 2 == 0:
                    act.wait_ge(h_ready, since(g, s, STAGED))
                    nc.scalar.activation(x_hi[:, s % STAGED, :, :], xs[:, s, :, :], ACT.Copy).then_inc(xhi_a, 1)

            def stage_a(g):
                nc.scalar.activation(table[0:1, 1:2], table[0:1, 0:1], ACT.Silu)
                for s in range(SLOTS):
                    n = SLOTS * g + s
                    act.wait_ge(h_ready, 1 + n + 1)
                    act.wait_ge(h_done, since(g, s, 2))
                    nc.scalar.activation(s_sb[:, s % 2, :], banks[:, H + s % 2, 0:P], ACT.Silu).then_inc(s_done, 1)
                    if s + STAGED < SLOTS:
                        high_part(g, s + STAGED)
                    if s:
                        high_hidden(g, s - 1)
                    for c in last_pieces(s):
                        act.wait_ge(y_ready, 1 + SLOTS * g)
                        split(g, c)
                high_hidden(g, SLOTS - 1)

            def high_hidden(g, s):
                act.wait_ge(t_ready, 1 + SLOTS * g + s + 1)
                nc.scalar.activation(ht_hi[:, s, :], banks[:, HT_T + s % 2, 0:P], ACT.Copy).then_inc(hi_done, 1)

            def stage_b(g):
                if not RESIDENT:
                    for s in range(STAGED):
                        high_part(g + 1, s)
                for s in range(SLOTS):
                    for c in first_pieces(s):
                        act.wait_ge(h_ready, 1 + SLOTS * (g + 1))
                        split(g + 1, c)

            for c in range(E):
                split(0, c)
            act.wait_ge(gates_done, 1)
            for s in range(0, SLOTS, 2):
                move_tokens(s)
            for c in range(E, LAST):
                split(0, c)
            act.wait_ge(xs_a, SLOTS // 2)
            for s in range(STAGED):
                high_part(0, s)
            with act.Fori(0, G - 1) as g:
                stage_a(g)
                stage_b(g)
            stage_a(G - 1)

        @block.tensor
        def _(pe):
            for s in (tw_ready, h_ready, t_ready, y_ready):
                pe.sem_inc(s, 1)
            pe.wait_ge(const_done, 8)
            if out_major:
                pe.wait_ge(c_loaded, 32)
                for k in range(KD):
                    ins = nc.tensor.transpose(banks[:, 0, E * k:E * k + E], r_raw[0:E, P * k:P * k + P], ident[0:E, 0:E])
                ins.then_inc(rt_ready, 1)
            for b in range(B):
                pe.wait_ge(norm_done, b + 1)
                if b >= 4:
                    pe.wait_ge(xn_done, b - 3)
                for k in range(KD):
                    ins = nc.tensor.transpose(banks[:, 2 + b % 4, P * k:P * k + M], x_tok[0:M, b, P * k:P * k + P], ident[0:M, 0:M])
                ins.then_inc(tr_done, 1)
            if out_major:
                pe.wait_ge(rt_done, 1)
            else:
                pe.wait_ge(c_loaded, 48)
            for half in range(2):
                pe.wait_ge(xn_done, HB * (half + 1))
                for k in range(KD):
                    ins = nc.tensor.matmul(banks[0:E, half, 0:HT], r_t[:, k, :], xn_t[:, k, HT * half:HT * half + HT], start=(k == 0), stop=(k == KD - 1))
                ins.then_inc(logit_ready, 1)
            pe.wait_ge(logit_done, 2)
            for b in range(B):
                ins = nc.tensor.transpose(banks[0:M, 2, E * b:E * b + E], logit_t[0:E, M * b:M * b + M], ident[0:E, 0:E])
            ins.then_inc(back_ready, 1)

            def turn_piece(g, c):
                pe.wait_ge(raw_loaded[c % RING], 16 * loads(g, c))
                pe.wait_ge(wlo_done, number(g, max(c, 1)))
                for k in range(KD):
                    ins = nc.tensor.transpose(banks[:, W + c % 2, P * k:P * k + P], raw[:, c % RING, k, :], ident[:, :])
                ins.then_inc(tw_ready, 1)

            pe.wait_ge(chosen_done, 1)
            for b in range(B):
                nc.tensor.matmul(banks[0:M, 0, E * b:E * b + E], earlier[0:M, 0:M], chosen[0:M, b, :], start=True, stop=(b == 0))
                for c in range(b):
                    nc.tensor.matmul(banks[0:M, 0, E * b:E * b + E], ones[0:M, 0:M], chosen[0:M, c, :], start=False, stop=(c == b - 1))
            for b in range(B):
                ins = nc.tensor.matmul(banks[:, 1, 0:E], ones[0:M, :], chosen[0:M, b, :], start=(b == 0), stop=(b == B - 1))
            ins.then_inc(count_ready, 1)
            pe.wait_ge(expert_done, 1)
            experts = [pe.value_load(expert[0:1, s:s + 1], min_val=0, max_val=E - 1) for s in range(SLOTS)]
            if out_major:
                for c in range(E):
                    turn_piece(0, c)
            for s in range(SLOTS):
                pe.wait_ge(rows_loaded[s // 4], 16)
                if s >= 4:
                    pe.wait_ge((xs_a, xs_b)[s % 2], (s - 4) // 2 + 1)
                for k in range(KD):
                    ins = nc.tensor.transpose(banks[:, s % 4, P * k:P * k + P], slot_rows[:, s, P * k:P * k + P], ident[:, :])
                ins.then_inc(st_ready, 1)
            pe.wait_ge(xs_a, SLOTS // 2)
            pe.wait_ge(xs_b, SLOTS // 2)
            if out_major:
                for c in range(E, LAST):
                    turn_piece(0, c)

            def hidden(g, s):
                if s == 0:
                    pe.wait_ge(wlo_done, 1 + number(g, LAST))
                pe.wait_ge(xlo_done, 1 + (s if RESIDENT else SLOTS * g + s) + 1)
                pe.wait_ge(h_done, since(g, s, 2))
                e = experts[s]
                for k in range(KD):
                    ins = three(nc, banks[:, H + s % 2, 0:2 * P], x_hi[:, s % STAGED, k, :], x_lo[:, s % STAGED, k, :], wab_hi[:, e, k, :], wab_lo[:, e, k, :],
                                k == 0, k == KD - 1)
                ins.then_inc(h_ready, 1)

            def turn_hidden(g, s):
                pe.wait_ge(h_done, 1 + SLOTS * g + s + 1)
                pe.wait_ge(lo_done, since(g, s, 2))
                if s < 2:
                    pe.wait_ge(add_done, 1 + SLOTS * g)
                nc.tensor.transpose(banks[:, HT_T + s % 2, 0:P], h_sb[:, s % 2, :], ident[:, :]).then_inc(t_ready, 1)

            def project(g, s):
                if s == 0:
                    pe.wait_ge(wlo_done, 1 + number(g, PIECES))
                pe.wait_ge(lo_done, 1 + SLOTS * g + s + 1)
                pe.wait_ge(add_done, since(g, s, 4))
                if s in (2, 3):
                    pe.wait_ge(lo_done, 1 + SLOTS * g + SLOTS - 3 + s)
                e = experts[s]
                three(nc, banks[:, Y[s % 4], :], ht_hi[:, s, :], ht_lo[:, s, :], wy_hi[:, e, :], wy_lo[:, e, :], True, True).then_inc(y_ready, 1)

            def stage_a(g):
                for s in range(SLOTS):
                    hidden(g, s)
                    if s:
                        turn_hidden(g, s - 1)
                    if out_major:
                        for c in last_pieces(s):
                            turn_piece(g, c)

            def stage_b(g, last):
                for s in range(SLOTS):
                    project(g, s)
                    if s == 0:
                        turn_hidden(g, SLOTS - 1)
                    if out_major and not last:
                        for c in first_pieces(s):
                            turn_piece(g + 1, c)

            with pe.Fori(0, G - 1) as g:
                stage_a(g)
                stage_b(g, False)
            stage_a(G - 1)
            stage_b(G - 1, True)

        @block.vector
        def _(dve):
            for s in (xhi_b, h_done, lo_done, add_done, chain):
                dve.sem_inc(s, 1)
            if out_major:
                dve.sem_inc(wlo_done, 1)
            own = Chain(dve, chain)
            for b in range(B):
                if b % HB == 0:
                    dve.wait_ge(x_loaded[b // HB], 32)
                ins = nc.vector.bn_stats(stats[0:M, b, :], x_tok[0:M, b, :])
            own.link(ins)
            for b in range(B):
                ins = nc.vector.bn_aggr(mean_var[0:M, b, :], stats[0:M, b, :])
            ins.then_inc(var_done, 1)
            dve.wait_ge(std_done, 1)
            own.link(nc.vector.reciprocal(rstd[0:M, :], std[0:M, :]))
            for b in range(B):
                nc.vector.tensor_scalar(x_tok[0:M, b, :], x_tok[0:M, b, :], mean_var[0:M, b, 0:1], rstd[0:M, b:b + 1],
                                        ALU.subtract, ALU.mult).then_inc(norm_done, 1)
            dve.wait_ge(back_ready, 1)
            dve.wait_ge(const_done, 9 + TILES + SLOTS)
            own.link(nc.vector.tensor_copy(logits[0:M, :, :], banks[0:M, 2, 0:B * E].rearrange("p (b e) -> p b e", e=E)))
            own.link(nc.vector.tensor_reduce(l_max[0:M, :], logits[0:M, :, :], axis=AX.X, op=ALU.max))
            nc.vector.tensor_tensor(p_exp[0:M, :, :], logits[0:M, :, :], l_max[0:M, :].unsqueeze(2).to_broadcast([M, B, E]), ALU.subtract).then_inc(shift_done, 1)
            for b in range(B):
                other = logits[0:M, b, :].unsqueeze(1).to_broadcast([M, E, E])
                this = logits[0:M, b, :].unsqueeze(2).to_broadcast([M, E, E])
                nc.vector.tensor_tensor(above[0:M, b, :, :], other, this, ALU.is_gt)
                ins = nc.vector.tensor_tensor(equal[0:M, b, :, :], other, this, ALU.is_equal)
            own.link(ins)
            own.link(nc.vector.tensor_tensor(equal[0:M, :, :, :], equal[0:M, :, :, :], before[0:M, :, :].unsqueeze(1).to_broadcast([M, B, E, E]), ALU.mult))
            own.link(nc.vector.tensor_tensor(above[0:M, :, :, :], above[0:M, :, :, :], equal[0:M, :, :, :], ALU.add))
            own.link(nc.vector.tensor_reduce(rank[0:M, :, :], above[0:M, :, :, :], axis=AX.X, op=ALU.add))
            nc.vector.tensor_scalar(chosen[0:M, :, :], rank[0:M, :, :], TOP - 0.5, None, ALU.is_lt).then_inc(chosen_done, 1)
            dve.wait_ge(count_ready, 1)
            own.link(nc.vector.tensor_copy(count, banks[:, 1, 0:E]))
            own.link(nc.vector.tensor_tensor(filled, count.unsqueeze(2).to_broadcast([P, E, TILES]), threshold.unsqueeze(1).to_broadcast([P, E, TILES]), ALU.is_gt))
            own.link(nc.vector.tensor_reduce(count, filled, axis=AX.X, op=ALU.add))
            own.link(nc.vector.tensor_tensor(starts_of, before, count.unsqueeze(1).to_broadcast([P, E, E]), ALU.mult))
            own.link(nc.vector.tensor_reduce(start, starts_of, axis=AX.X, op=ALU.add))
            own.link(nc.vector.tensor_tensor(end, start, count, ALU.add))
            own.link(nc.vector.tensor_tensor(passed, slot_no.unsqueeze(2).to_broadcast([P, SLOTS, E]), end.unsqueeze(1).to_broadcast([P, SLOTS, E]), ALU.is_ge))
            own.link(nc.vector.tensor_reduce(expert_f, passed, axis=AX.X, op=ALU.add))
            own.link(nc.vector.tensor_scalar(expert_f, expert_f, float(E - 1), None, ALU.min))
            nc.vector.tensor_copy(expert[:, :], expert_f[0:1, :]).then_inc(expert_done, 1)
            own.link(nc.vector.tensor_scalar(start, start, float(P), None, ALU.mult))
            own.link(nc.vector.tensor_tensor(pos[0:M, :, :], banks[0:M, 0, 0:B * E].rearrange("p (b e) -> p b e", e=E),
                                             start[0:M, :].unsqueeze(1).to_broadcast([M, B, E]), ALU.add))
            for k in range(TOP):
                own.link(nc.vector.scalar_tensor_tensor(work[0:M, :, :], rank[0:M, :, :], float(k), pos[0:M, :, :], ALU.is_equal, ALU.mult))
                own.link(nc.vector.tensor_reduce(pos_f[0:M, :], work[0:M, :, :], axis=AX.X, op=ALU.add))
                own.link(nc.vector.tensor_copy(place[0:M, :, k], pos_f[0:M, :]))
            dve.sem_inc(place_done, 1)
            dve.wait_ge(exp_done, 1)
            for k in range(TOP):
                own.link(nc.vector.scalar_tensor_tensor(work[0:M, :, :], rank[0:M, :, :], float(k), p_exp[0:M, :, :], ALU.is_equal, ALU.mult))
                own.link(nc.vector.tensor_reduce(gates[0:M, :, k], work[0:M, :, :], axis=AX.X, op=ALU.add))
            own.link(nc.vector.tensor_reduce(p_sum[0:M, :], gates[0:M, :, :], axis=AX.X, op=ALU.add))
            own.link(nc.vector.reciprocal(p_sum[0:M, :], p_sum[0:M, :]))
            dve.wait_ge(tanh_done, 1)
            own.link(nc.vector.tensor_scalar(p_sum[0:M, :], p_sum[0:M, :], tanh_g[0:M, 0:1], None, ALU.mult))
            own.link(nc.vector.tensor_tensor(gates[0:M, :, :], gates[0:M, :, :], p_sum[0:M, :].unsqueeze(2).to_broadcast([M, B, TOP]), ALU.mult))
            dve.sem_inc(gates_done, 1)

            def split(g, c):
                dve.wait_ge(whi_done, 1 + number(g, c) + 1)
                nc.vector.tensor_tensor(split_dst(wab_lo, wy_lo, c), split_src(c), split_dst(wab_hi, wy_hi, c).bitcast(F32),
                                        ALU.subtract).then_inc(wlo_done, 1)

            def move_tokens(s):
                dve.wait_ge(st_ready, s + 1)
                nc.vector.tensor_copy(xs[:, s, :, :], banks[:, s % 4, :].rearrange("p (k q) -> p k q", q=P)).then_inc(xs_b, 1)

            def high_part(g, s):
                if s % 2:
                    dve.wait_ge(h_ready, since(g, s, STAGED))
                    nc.vector.tensor_copy(x_hi[:, s % STAGED, :, :], xs[:, s, :, :]).then_inc(xhi_b, 1)

            def low_hidden(g, s):
                dve.wait_ge(hi_done, 1 + SLOTS * g + s + 1)
                nc.vector.tensor_tensor(ht_lo[:, s, :], banks[:, HT_T + s % 2, 0:P], ht_hi[:, s, :].bitcast(F32), ALU.subtract).then_inc(lo_done, 1)

            def stage_a(g):
                for s in range(SLOTS):
                    n = SLOTS * g + s
                    dve.wait_ge(h_ready, 1 + n + 1)
                    dve.wait_ge(s_done, 1 + n + 1)
                    dve.wait_ge(t_ready, since(g, s, 2))
                    nc.vector.tensor_tensor(h_sb[:, s % 2, :], s_sb[:, s % 2, :], banks[:, H + s % 2, P:2 * P], ALU.mult).then_inc(h_done, 1)
                    if s + STAGED < SLOTS:
                        high_part(g, s + STAGED)
                    if s:
                        low_hidden(g, s - 1)
                    if out_major:
                        for c in last_pieces(s):
                            split(g, c)
                low_hidden(g, SLOTS - 1)

            def stage_b(g, last):
                if not last and not RESIDENT:
                    for s in range(STAGED):
                        high_part(g + 1, s)
                for s in range(SLOTS):
                    n = SLOTS * g + s
                    dve.wait_ge(y_ready, 1 + n + 1)
                    dve.wait_ge(add_done, 1 + SLOTS * g)
                    nc.vector.tensor_tensor(y_acc[:, s, :], y_acc[:, s, :], banks[:, Y[s % 4], :], ALU.add).then_inc(add_done, 1)
                    if out_major and not last:
                        for c in first_pieces(s):
                            split(g + 1, c)

            if out_major:
                for c in range(E):
                    split(0, c)
            for s in range(1, SLOTS, 2):
                move_tokens(s)
            if out_major:
                for c in range(E, LAST):
                    split(0, c)
            dve.wait_ge(xs_b, SLOTS // 2)
            for s in range(STAGED):
                high_part(0, s)
            dve.wait_ge(acc_zeroed, 1)
            with dve.Fori(0, G - 1) as g:
                stage_a(g)
                stage_b(g, False)
            stage_a(G - 1)
            stage_b(G - 1, True)
            dve.wait_ge(x_again, 16)
            for b in range(B):
                dve.wait_ge(y_gathered[b], 16 * TOP)
                for k in range(TOP):
                    ins = nc.vector.scalar_tensor_tensor(x_tok[0:M, b, :], y_got[0:M, TOP * b + k, :], gates[0:M, b, k:k + 1], x_tok[0:M, b, :],
                                                         ALU.mult, ALU.add)
                    if k == 0:
                        own.link(ins)
                ins.then_inc(x_done, 1)


def strided_attention(nc, x_in, ctx_rows, wq, bq, wk, bk, wv, bv, wo, bo, gate, x_out):
    B, M, D = x_in.shape
    P = 128
    H = 16
    HD = D // H
    J = ctx_rows.shape[1] // H
    KD = D // P
    QH = P // HD
    HH = H // 2
    T = B * M
    HT = T // 2
    HB = B // 2
    BJ = HB * J
    BANK = 512
    EPS = 1e-5
    SCALE = HD ** -0.5

    with ExitStack() as ctx:
        def sb(n, shape, dt=F32):
            return ctx.enter_context(nc.sbuf_tensor("g_" + n, shape, dt))

        def sem(n):
            return nc.alloc_semaphore("g_" + n)

        ctx_t = sb("ctx_t", [P, KD, H, BJ])
        rows = sb("rows", [P, 2, HH * D])
        wq_hi, wq_lo, wo_hi, wo_lo = (sb(n, [P, KD, D], F32R) for n in ("wq_hi", "wq_lo", "wo_hi", "wo_lo"))
        wk_t, wv_t = (sb(n, [P, KD, D]) for n in ("wk_t", "wv_t"))
        xn_hi = sb("xn_hi", [P, KD, T], F32R)
        xn_lo = sb("xn_lo", [P, KD, T], F32R)
        shared = sb("shared", [P, B * D])
        k_t = sb("k_t", [P, KD, B * J])
        v_t = sb("v_t", [P, KD, B * J])
        q_b = sb("q_b", [P, 2, H, M])
        v_tb = sb("v_tb", [P, 2, KD, J])
        v_b = sb("v_b", [P, 2, D])
        probs = sb("probs", [P, 2, H * J])
        probs_t = sb("probs_t", [P, H * M])
        s_max = sb("s_max", [P, 2, HH])
        s_sum = sb("s_sum", [P, 2, HH])
        bias = {n: sb("b" + n, [P, KD]) for n in "qkvo"}
        tanh_g = sb("tanh_g", [P, 1])
        eps = sb("eps", [P, 1])
        ident = sb("ident", [P, P])
        stats = sb("stats", [P, B, 6])
        mean_var = sb("mean_var", [P, B, 2])
        std = sb("std", [P, B])
        rstd = sb("rstd", [P, B])
        x_tok = shared[:, :].rearrange("p (b d) -> p b d", d=D)
        q_t = shared[:, 0:KD * T].rearrange("p (k t) -> p k t", t=T)
        y_t = q_t
        raw = ctx_t[:, :, :, :].rearrange("p k h j -> p (k h j)")[:, 0:4 * KD * D].rearrange("p (w c d) -> p w c d", c=KD, d=D)
        x_res = rows[:, 0, :].rearrange("p (b d) -> p b d", d=D)

        banks = ctx.enter_context(nc.psum_tensor("g_banks", [P, 8, BANK], F32))
        S, TP, V, O = 0, 4, 6, 7

        x_loaded = [sem(f"x_loaded{n}") for n in range(2)]
        c_loaded = sem("c_loaded")
        w_loaded = [sem(f"w_loaded{n}") for n in range(4)]
        rows_loaded = [sem(f"rows_loaded{n}") for n in range(2)]
        x_again = sem("x_again")
        x_stored = sem("x_stored")
        const_done = sem("const_done")
        tanh_done = sem("tanh_done")
        var_done = sem("var_done")
        std_done = sem("std_done")
        norm_done = sem("norm_done")
        fill_ready = sem("fill_ready")
        fill_hi = sem("fill_hi")
        fill_done = sem("fill_done")
        q_ready = sem("q_ready")
        q_done = sem("q_done")
        ctx_ready = sem("ctx_ready")
        ctx_a = sem("ctx_a")
        ctx_b = sem("ctx_b")
        kv_ready = sem("kv_ready")
        kv_done = sem("kv_done")
        qv_done = sem("qv_done")
        s_ready = sem("s_ready")
        sub_done = sem("sub_done")
        exp_done = sem("exp_done")
        p_done = sem("p_done")
        v_ready = sem("v_ready")
        v_done = sem("v_done")
        t_ready = sem("t_ready")
        ta_done = sem("ta_done")
        tb_done = sem("tb_done")
        o_ready = sem("o_ready")
        ohi_done = sem("ohi_done")
        olo_done = sem("olo_done")
        y_ready = sem("y_ready")
        y_done = sem("y_done")
        out_ready = sem("out_ready")
        x_done = sem("x_done")
        held = sem("held")
        chain = sem("chain")
        pool_chain = sem("pool_chain")

        block = ctx.enter_context(nc.Block())

        CTX0, KV0, S0, SUB0, V0, T0, O0 = 2, 4, 2, 2, 2, 5, 2

        W = (wq, wk, wv, wo)
        FILLS = 4 * KD + B

        @block.sync
        def _(sp):
            for n, w in enumerate(W):
                sp.dma_start(raw[:, n, :, :], w.rearrange("(c p) d -> p c d", p=P)).then_inc(w_loaded[n], 16)
                if n == 0:
                    for q in range(4):
                        sp.dma_start(x_tok[0:M, 2 * q:2 * q + 2, :], x_in[2 * q:2 * q + 2].rearrange("b p d -> p b d")).then_inc(x_loaded[q // 2], 16)
            for n, src in zip("qkvo", (bq, bk, bv, bo)):
                sp.dma_start(bias[n][:, :], src.rearrange("(c p) -> p c", p=P), allow_slow_non_contiguous=True).then_inc(c_loaded, 16)
            sp.dma_start(tanh_g[:, :], gate.to_broadcast([P, 1])).then_inc(c_loaded, 16)

            def load_rows(b, hh):
                src = ctx_rows[b, 0:H * J, :].rearrange("(j h) d -> j h d", h=H)[:, HH * hh:HH * hh + HH, :]
                sp.dma_start(rows[0:J, hh, :].rearrange("p (h d) -> p h d", d=D), src).then_inc(rows_loaded[hh], 16)

            load_rows(0, 0)
            load_rows(0, 1)
            with sp.Fori(0, B - 1) as i:
                for hh in range(2):
                    sp.wait_ge(ctx_ready, 1 + KD * (2 * i + hh + 1))
                    sp.sem_inc(held, 1)
                    load_rows(i + 1, hh)
            sp.wait_ge(ctx_ready, 1 + KD * 2 * B)
            sp.dma_start(x_res[0:M, :, :], x_in.rearrange("b p d -> p b d")).then_inc(x_again, 16)
            for b in range(B):
                sp.wait_ge(x_done, b + 1)
                sp.dma_start(x_out[b, :, :], x_res[0:M, b, :]).then_inc(x_stored, 16)
            sp.wait_ge(x_stored, 16 * B)

        @block.gpsimd
        def _(pool):
            pool.sem_inc(qv_done, 1)
            nc.gpsimd.memset(ident[:, :], 0.0).then_inc(const_done, 1)
            nc.gpsimd.memset(eps[:, :], EPS).then_inc(const_done, 1)
            nc.gpsimd.memset(q_b[:, :, :, :], 0.0).then_inc(const_done, 1)
            pool.wait_ge(const_done, 3)
            nc.gpsimd.affine_select(out=ident[:, :], in_=ident[:, :], compare_op=ALU.not_equal, fill=1.0, base=0,
                                    pattern=[[-1, P]], channel_multiplier=1).then_inc(const_done, 1)
            pool.sem_inc(pool_chain, 1)
            pool.wait_ge(q_done, 2 * KD)
            pool.wait_ge(kv_done, KV0 + 4 * KD)
            pool.sem_inc(held, 1)
            own = Chain(pool, pool_chain)
            with own.loop(B // 2, 4) as i:
                for u in range(2):
                    n = 2 * i + u
                    pool.wait_ge(s_ready, S0 + n - 1)
                    pool.wait_ge(v_ready, V0 + n - 1)
                    pool.sem_inc(held, 1)
                    for r in range(QH):
                        p = slice(HD * r, HD * r + HD)
                        ins = nc.gpsimd.tensor_copy(q_b[p, u, :, :].rearrange("p (c r) q -> p c r q", r=QH)[:, :, r, :], q_t[p, :, bass.ds(M * n, M)])
                    own.link(ins)
                    pool.sem_inc(held, 1)
                    own.link(nc.gpsimd.tensor_copy(v_tb[:, u, :, :], v_t[:, :, bass.ds(J * n, J)]))
                    pool.sem_inc(qv_done, 1)

        @block.scalar
        def _(act):
            for s, start in ((ctx_a, CTX0), (kv_done, KV0), (exp_done, 1), (v_done, 1), (ta_done, 1), (ohi_done, 1)):
                act.sem_inc(s, start)
            act.wait_ge(c_loaded, 80)
            nc.scalar.activation(tanh_g[:, :], tanh_g[:, :], ACT.Tanh).then_inc(tanh_done, 1)
            act.wait_ge(const_done, 3)
            act.wait_ge(var_done, 1)
            nc.scalar.activation(std[0:M, :], mean_var[0:M, :, 1], ACT.Sqrt, bias=eps[0:M, :]).then_inc(std_done, 1)
            for n in range(FILLS):
                if n < KD or 3 * KD <= n < 4 * KD:
                    act.wait_ge(fill_ready, n + 1)
                    dst = wq_hi if n < KD else wo_hi
                    nc.scalar.activation(dst[:, n % KD, :], banks[:, n % 4, :], ACT.Copy).then_inc(fill_hi, 1)
                elif n >= 4 * KD:
                    b = n - 4 * KD
                    act.wait_ge(fill_ready, n + 1)
                    nc.scalar.activation(xn_hi[:, :, M * b:M * b + M], banks[:, n % 4, :].rearrange("p (k q) -> p k q", q=P)[:, :, 0:M],
                                         ACT.Copy).then_inc(fill_hi, 1)

            with act.Fori(0, 2) as half:
                for u in range(2 * HB):
                    bl, hh = u // 2, u % 2
                    for k in range(0, KD, 2):
                        act.wait_ge(ctx_ready, 1 + KD * (2 * HB * half + u) + k + 1)
                        nc.scalar.activation(ctx_t[:, k, HH * hh:HH * hh + HH, J * bl:J * bl + J],
                                             banks[:, S + k, 0:HH * J].rearrange("p (h j) -> p h j", j=J), ACT.Copy).then_inc(ctx_a, 1)
                for n in range(2 * KD):
                    act.wait_ge(kv_ready, 1 + 2 * KD * half + n + 1)
                    dst, b = ((k_t, "k"), (v_t, "v"))[n % 2]
                    nc.scalar.activation(dst[:, n // 2, bass.ds(BJ * half, BJ)], banks[:, TP + n % 4, 0:BJ], ACT.Identity,
                                         bias=bias[b][:, n // 2:n // 2 + 1]).then_inc(kv_done, 1)

            def exponent(n, u):
                act.wait_ge(sub_done, SUB0 + n + 1)
                nc.scalar.activation(probs[0:M, u, :], probs[0:M, u, :], ACT.Exp).then_inc(exp_done, 1)

            def element(n, u, last):
                act.wait_ge(v_ready, V0 + n + 1)
                act.wait_ge(o_ready, O0 + n - 1)
                nc.scalar.activation(v_b[0:J, u, :], banks[0:J, V, :], ACT.Copy).then_inc(v_done, 1)
                for r in (0, 2):
                    act.wait_ge(t_ready, T0 + 4 * n + r + 1)
                    act.wait_ge(o_ready, O0 + n)
                    nc.scalar.activation(probs_t[0:J, 4 * M * r:4 * M * r + 4 * M], banks[0:J, TP, 0:4 * M], ACT.Copy).then_inc(ta_done, 1)
                if not last:
                    exponent(n + 1, (u + 1) % 2)
                act.wait_ge(o_ready, O0 + n + 1)
                nc.scalar.activation(xn_hi[:, :, bass.ds(M * n, M)], banks[:, O, 0:KD * M].rearrange("p (k q) -> p k q", q=M),
                                     ACT.Copy).then_inc(ohi_done, 1)

            exponent(0, 0)
            with act.Fori(0, B // 2 - 1) as i:
                element(2 * i, 0, False)
                element(2 * i + 1, 1, False)
            element(B - 2, 0, False)
            element(B - 1, 1, True)
            for n in range(2 * KD):
                half, d = n // KD, n % KD
                act.wait_ge(y_ready, n + 1)
                nc.scalar.activation(y_t[:, d, HT * half:HT * half + HT], banks[:, n % 4, 0:HT], ACT.Identity,
                                     bias=bias["o"][:, d:d + 1]).then_inc(y_done, 1)

        @block.tensor
        def _(pe):
            for s, start in ((ctx_ready, 1), (kv_ready, 1), (s_ready, S0), (v_ready, V0), (t_ready, T0), (o_ready, O0)):
                pe.sem_inc(s, start)
            pe.wait_ge(const_done, 4)
            for n in range(FILLS):
                if n >= 4:
                    pe.wait_ge(fill_done, n - 3)
                if n < 4 * KD:
                    w, k = n // KD, n % KD
                    pe.wait_ge(w_loaded[w], 16)
                    for c in range(KD):
                        ins = nc.tensor.transpose(banks[:, n % 4, P * c:P * c + P], raw[:, w, c, P * k:P * k + P], ident[:, :])
                else:
                    b = n - 4 * KD
                    pe.wait_ge(norm_done, b + 1)
                    for k in range(KD):
                        ins = nc.tensor.transpose(banks[:, n % 4, P * k:P * k + M], x_tok[0:M, b, P * k:P * k + P], ident[0:M, 0:M])
                ins.then_inc(fill_ready, 1)
            pe.wait_ge(fill_done, FILLS)
            for n in range(2 * KD):
                half, m = n // KD, n % KD
                if n >= 4:
                    pe.wait_ge(q_done, n - 3)
                t = slice(HT * half, HT * half + HT)
                c = slice(P * m, P * m + P)
                for k in range(KD):
                    ins = three(nc, banks[:, TP + n % 4, 0:HT], wq_hi[:, k, c], wq_lo[:, k, c], xn_hi[:, k, t], xn_lo[:, k, t], k == 0, k == KD - 1)
                ins.then_inc(q_ready, 1)
            pe.wait_ge(q_done, 2 * KD)

            with pe.Fori(0, 2) as half:
                for u in range(2 * HB):
                    bl, hh = u // 2, u % 2
                    n = 2 * HB * half + u
                    pe.wait_ge(rows_loaded[hh], 16 * (HB * half + bl + 1))
                    for k in range(KD):
                        pe.wait_ge((ctx_a, ctx_b)[k % 2], CTX0 + 2 * n - 1 + k // 2)
                        pe.sem_inc(held, 1)
                        for h in range(HH):
                            ins = nc.tensor.transpose(banks[:, S + k, J * h:J * h + J], rows[0:J, hh, D * h + P * k:D * h + P * k + P], ident[0:J, 0:J])
                        ins.then_inc(ctx_ready, 1)
                pe.wait_ge(ctx_a, CTX0 + 4 * HB * (half + 1))
                pe.wait_ge(ctx_b, CTX0 + 4 * HB * (half + 1))
                for n in range(2 * KD):
                    w = (wk_t, wv_t)[n % 2]
                    pe.wait_ge(kv_done, KV0 + 2 * KD * half + n - 3)
                    for k in range(KD):
                        for r in range(QH):
                            h = QH * (n // 2) + r
                            ins = nc.tensor.matmul(banks[HD * r:HD * r + HD, TP + n % 4, 0:BJ], w[:, k, HD * h:HD * h + HD], ctx_t[:, k, h, :],
                                                   start=(k == 0), stop=(k == KD - 1))
                    ins.then_inc(kv_ready, 1)

            def scores(n, u):
                pe.wait_ge(qv_done, 1 + n + 1)
                pe.wait_ge(sub_done, SUB0 + n - 1)
                for h in range(H):
                    c = J * (h % HH)
                    ins = nc.tensor.matmul(banks[0:M, S + 2 * u + h // HH, c:c + J], q_b[:, u, h, :], k_t[:, h // QH, bass.ds(J * n, J)],
                                           start=True, stop=True)
                ins.then_inc(s_ready, 1)

            def element(n, u, last):
                if not last:
                    scores(n + 1, (u + 1) % 2)
                pe.wait_ge(v_done, 1 + n)
                pe.sem_inc(held, 1)
                for c in range(KD):
                    ins = nc.tensor.transpose(banks[0:J, V, P * c:P * c + P], v_tb[:, u, c, :], ident[:, :])
                ins.then_inc(v_ready, 1)
                pe.wait_ge(p_done, 1 + n + 1)
                for r in range(4):
                    pe.wait_ge((ta_done, tb_done)[r % 2], 1 + 2 * n + r // 2)
                    pe.sem_inc(held, 1)
                    for x in range(4):
                        h = 4 * r + x
                        ins = nc.tensor.transpose(banks[0:J, TP + r % 2, M * x:M * x + M], probs[0:M, u, J * h:J * h + J], ident[0:M, 0:M])
                    ins.then_inc(t_ready, 1)
                pe.wait_ge(ta_done, 1 + 2 * n + 2)
                pe.wait_ge(tb_done, 1 + 2 * n + 2)
                pe.wait_ge(v_done, 1 + n + 1)
                pe.wait_ge(olo_done, 1 + n)
                pe.sem_inc(held, 1)
                for h in range(H):
                    p, c = HD * (h % QH), M * (h // QH)
                    ins = nc.tensor.matmul(banks[p:p + HD, O, c:c + M], v_b[0:J, u, HD * h:HD * h + HD], probs_t[0:J, M * h:M * h + M],
                                           start=True, stop=True)
                ins.then_inc(o_ready, 1)

            pe.wait_ge(kv_done, KV0 + 4 * KD)
            scores(0, 0)
            with pe.Fori(0, B // 2 - 1) as i:
                element(2 * i, 0, False)
                element(2 * i + 1, 1, False)
            element(B - 2, 0, False)
            element(B - 1, 1, True)
            pe.wait_ge(olo_done, 1 + B)
            for n in range(2 * KD):
                half, d = n // KD, n % KD
                if n >= 4:
                    pe.wait_ge(y_done, n - 3)
                t = slice(HT * half, HT * half + HT)
                c = slice(P * d, P * d + P)
                for k in range(KD):
                    ins = three(nc, banks[:, n % 4, 0:HT], wo_hi[:, k, c], wo_lo[:, k, c], xn_hi[:, k, t], xn_lo[:, k, t], k == 0, k == KD - 1)
                ins.then_inc(y_ready, 1)
            for b in range(B):
                pe.wait_ge(y_done, KD * (1 + b // HB))
                if b >= 4:
                    pe.wait_ge(x_done, b - 3)
                for k in range(KD):
                    ins = nc.tensor.transpose(banks[0:M, 4 + b % 4, P * k:P * k + P], y_t[:, k, M * b:M * b + M], ident[:, :])
                ins.then_inc(out_ready, 1)

        @block.vector
        def _(dve):
            for s, start in ((ctx_b, CTX0), (sub_done, SUB0), (p_done, 1), (tb_done, 1), (olo_done, 1), (chain, 1)):
                dve.sem_inc(s, start)
            own = Chain(dve, chain)
            for b in range(B):
                if b % HB == 0:
                    dve.wait_ge(x_loaded[b // HB], 32)
                ins = nc.vector.bn_stats(stats[0:M, b, :], x_tok[0:M, b, :])
            own.link(ins)
            for b in range(B):
                ins = nc.vector.bn_aggr(mean_var[0:M, b, :], stats[0:M, b, :])
            ins.then_inc(var_done, 1)
            dve.wait_ge(std_done, 1)
            own.link(nc.vector.reciprocal(rstd[0:M, :], std[0:M, :]))
            for b in range(B):
                nc.vector.tensor_scalar(x_tok[0:M, b, :], x_tok[0:M, b, :], mean_var[0:M, b, 0:1], rstd[0:M, b:b + 1],
                                        ALU.subtract, ALU.mult).then_inc(norm_done, 1)
            for n in range(FILLS):
                bank = banks[:, n % 4, :]
                if KD <= n < 3 * KD:
                    dve.wait_ge(fill_ready, n + 1)
                    nc.vector.tensor_copy((wk_t, wv_t)[n // KD - 1][:, n % KD, :], bank).then_inc(fill_done, 1)
                elif n < 4 * KD:
                    hi, lo = (wq_hi, wq_lo) if n < KD else (wo_hi, wo_lo)
                    dve.wait_ge(fill_hi, n + 1 if n < KD else n + 1 - 2 * KD)
                    nc.vector.tensor_tensor(lo[:, n % KD, :], bank, hi[:, n % KD, :].bitcast(F32), ALU.subtract).then_inc(fill_done, 1)
                else:
                    b = n - 4 * KD
                    dve.wait_ge(fill_hi, n + 1 - 2 * KD)
                    t = slice(M * b, M * b + M)
                    nc.vector.tensor_tensor(xn_lo[:, :, t], bank.rearrange("p (k q) -> p k q", q=P)[:, :, 0:M], xn_hi[:, :, t].bitcast(F32),
                                            ALU.subtract).then_inc(fill_done, 1)
            dve.wait_ge(c_loaded, 80)
            for n in range(2 * KD):
                half, m = n // KD, n % KD
                dve.wait_ge(q_ready, n + 1)
                nc.vector.tensor_scalar(q_t[:, m, HT * half:HT * half + HT], banks[:, TP + n % 4, 0:HT], bias["q"][:, m:m + 1], SCALE,
                                        ALU.add, ALU.mult).then_inc(q_done, 1)

            with dve.Fori(0, 2) as half:
                for u in range(2 * HB):
                    bl, hh = u // 2, u % 2
                    for k in range(1, KD, 2):
                        dve.wait_ge(ctx_ready, 1 + KD * (2 * HB * half + u) + k + 1)
                        nc.vector.tensor_copy(ctx_t[:, k, HH * hh:HH * hh + HH, J * bl:J * bl + J],
                                              banks[:, S + k, 0:HH * J].rearrange("p (h j) -> p h j", j=J)).then_inc(ctx_b, 1)

            def rowwise(t):
                return t[0:M, :, :].unsqueeze(3).to_broadcast([M, 2, HH, J])

            def lower(n, u):
                s = banks[0:M, S + 2 * u:S + 2 * u + 2, 0:HH * J].rearrange("p r (h j) -> p r h j", j=J)
                dve.wait_ge(s_ready, S0 + n + 1)
                own.link(nc.vector.tensor_reduce(s_max[0:M, :, :], s, axis=AX.X, op=ALU.max))
                dve.wait_ge(t_ready, T0 + 4 * (n - 1))
                nc.vector.tensor_tensor(probs[0:M, u, :].rearrange("p (r h j) -> p r h j", h=HH, j=J), s, rowwise(s_max), ALU.subtract).then_inc(sub_done, 1)

            def element(n, u, last):
                p = probs[0:M, u, :].rearrange("p (r h j) -> p r h j", h=HH, j=J)
                dve.wait_ge(exp_done, 1 + n + 1)
                own.link(nc.vector.tensor_reduce(s_sum[0:M, :, :], p, axis=AX.X, op=ALU.add))
                own.link(nc.vector.reciprocal(s_sum[0:M, :, :], s_sum[0:M, :, :]))
                nc.vector.tensor_tensor(p, p, rowwise(s_sum), ALU.mult).then_inc(p_done, 1)
                if not last:
                    lower(n + 1, (u + 1) % 2)
                for r in (1, 3):
                    dve.wait_ge(t_ready, T0 + 4 * n + r + 1)
                    dve.wait_ge(o_ready, O0 + n)
                    nc.vector.tensor_copy(probs_t[0:J, 4 * M * r:4 * M * r + 4 * M], banks[0:J, TP + 1, 0:4 * M]).then_inc(tb_done, 1)
                dve.wait_ge(ohi_done, 1 + n + 1)
                t = bass.ds(M * n, M)
                nc.vector.tensor_tensor(xn_lo[:, :, t], banks[:, O, 0:KD * M].rearrange("p (k q) -> p k q", q=M), xn_hi[:, :, t].bitcast(F32),
                                        ALU.subtract).then_inc(olo_done, 1)

            lower(0, 0)
            with own.loop(B // 2 - 1, 6) as i:
                element(2 * i, 0, False)
                element(2 * i + 1, 1, False)
            element(B - 2, 0, False)
            element(B - 1, 1, True)
            dve.wait_ge(tanh_done, 1)
            dve.wait_ge(x_again, 16)
            for b in range(B):
                dve.wait_ge(out_ready, b + 1)
                nc.vector.scalar_tensor_tensor(x_res[0:M, b, :], banks[0:M, 4 + b % 4, :], tanh_g[0:M, 0:1], x_res[0:M, b, :],
                                               ALU.mult, ALU.add).then_inc(x_done, 1)


def flamingo_layers(nc, x, ctx_1024, mask_BxS2_bk0, g_xattn, g_ffn,
                    a_ln_x_g, a_ln_x_b, a_ln_l_g, a_ln_l_b, a_wq, a_wkv, a_wout, a_ln_o_g, a_ln_o_b,
                    f_router_w, f_router_b, f_w1, f_w3, f_w2,
                    g_wq, g_bq, g_wk, g_bk, g_wv, g_bv, g_wo, g_bo,
                    m_wg, m_w1, m_w2, m_w3, out):
    x1, x2, x3 = (nc.dram_tensor(f"x_after_{n}", x.shape, F32, kind="Internal").ap() for n in range(1, 4))
    with nc.cleanup_on_exit():
        perceiver_attention(nc, ctx_1024, x, mask_BxS2_bk0, a_ln_x_g, a_ln_x_b, a_ln_l_g, a_ln_l_b, a_wq, a_wkv, a_wout,
                            a_ln_o_g, a_ln_o_b, g_xattn[0:1], x1)
    with nc.cleanup_on_exit():
        gated_experts(nc, "f", x1, f_router_w, f_router_b, f_w1, f_w3, f_w2, False, g_ffn[0:1], x2)
    with nc.cleanup_on_exit():
        strided_attention(nc, x2, ctx_1024, g_wq, g_bq, g_wk, g_bk, g_wv, g_bv, g_wo, g_bo, g_xattn[1:2], x3)
    with nc.cleanup_on_exit():
        gated_experts(nc, "m", x3, m_wg, None, m_w1, m_w2, m_w3, True, g_ffn[1:2], out)


_INS = ["x", "ctx_1024", "mask_BxS2_bk0", "g_xattn", "g_ffn",
        "L0_xattn_ln_x_g", "L0_xattn_ln_x_b", "L0_xattn_ln_l_g", "L0_xattn_ln_l_b", "L0_xattn_Wq", "L0_xattn_Wkv",
        "L0_xattn_Wout", "L0_xattn_ln_o_g", "L0_xattn_ln_o_b",
        "L0_ffn_router_w", "L0_ffn_router_b", "L0_ffn_w1", "L0_ffn_w3", "L0_ffn_w2",
        "L1_xattn_Wq", "L1_xattn_bq", "L1_xattn_Wk", "L1_xattn_bk", "L1_xattn_Wv", "L1_xattn_bv", "L1_xattn_Wo", "L1_xattn_bo",
        "L1_ffn_Wg", "L1_ffn_W1", "L1_ffn_W2", "L1_ffn_W3"]


def kernel(**inputs):
    import numpy as _np
    import concourse.bacc as _bacc
    from concourse import mybir as _mybir
    from concourse.bass_utils import run_bass_kernel_spmd as _run

    nc = _bacc.Bacc("TRN2", target_bir_lowering=False, num_devices=1, dynamic_dma_scratch_size=4096)
    arrays, args = {}, []
    for name in _INS:
        a = _np.ascontiguousarray(inputs[name])
        arrays[name] = a
        args.append(nc.dram_tensor(name, a.shape, _mybir.dt.from_np(a.dtype), kind="ExternalInput").ap())
    args.append(nc.dram_tensor("out", inputs["x"].shape, F32, kind="ExternalOutput").ap())
    flamingo_layers(nc, *args)
    r = _run(nc, [arrays], core_ids=[0])
    return r.results[0]["out"]
```

```python
import concourse.bass as bass
from concourse import mybir
from contextlib import ExitStack, contextmanager

F32 = mybir.dt.float32
F32R = mybir.dt.float32r
U8 = mybir.dt.uint8
ALU = mybir.AluOpType
ACT = mybir.ActivationFunctionType
AX = mybir.AxisListType


class Chain:

    def __init__(self, eng, sem):
        self.eng, self.sem, self.base, self.n = eng, sem, 1, 0

    def link(self, ins):
        self.n += 1
        ins.then_inc(self.sem, 1)
        self.eng.wait_ge(self.sem, self.base + self.n)

    @contextmanager
    def loop(self, turns, per):
        start = self.base + self.n
        with self.eng.Fori(0, turns) as i:
            self.base, self.n = start + per * i, 0
            yield i
        assert self.n == per, (self.n, per)
        self.base, self.n = start + per * turns, 0


def perceiver_attention(nc, ctx_rows, x_in, keep_mask, ln_x_g, ln_x_b, ln_l_g, ln_l_b, wq, wkv, wout,
                        ln_o_g, ln_o_b, gate, x_out):
    B, M, D = x_in.shape
    N = ctx_rows.shape[1]
    P = 128
    HD = 64
    INNER = wq.shape[1]
    PAIRS = INNER // P
    HALF = INNER // 2
    KD = D // P
    KEYS = N + M
    CT = (N + P - 1) // P
    CROWS = [min(P, N - P * t) for t in range(CT)]
    LAT = CT
    NT = CT + 1
    TILE_ROWS = CROWS + [M]
    TILE_COL = [P * t for t in range(CT)] + [N]
    KT = (KEYS + P - 1) // P
    KROWS = [min(P, KEYS - P * t) for t in range(KT)]
    BANK = 512
    PART = [(0, BANK), (BANK, KEYS - BANK)]
    FIRST_T = 4
    EPS = 1e-5
    FAR = float(2.0 ** 100)
    SCALE = HD ** -0.5

    with ExitStack() as ctx:
        def sb(name, shape, dt=F32):
            return ctx.enter_context(nc.sbuf_tensor("a_" + name, shape, dt))

        def ps(name, shape):
            return ctx.enter_context(nc.psum_tensor("a_" + name, shape, F32))

        def sem(name):
            return nc.alloc_semaphore("a_" + name)

        wkv_hi = sb("wkv_hi", [P, KD, 2 * INNER], F32R)
        wkv_lo = sb("wkv_lo", [P, KD, 2 * INNER], F32R)
        wq_sb = sb("wq_sb", [P, KD, INNER])
        wout_sb = sb("wout_sb", [P, PAIRS, D])
        rows = sb("rows", [P, CT, D])
        lat = sb("lat", [P, D])
        kvin_hi = sb("kvin_hi", [P, KD, KEYS], F32R)
        kvin_lo = sb("kvin_lo", [P, KD, KEYS], F32R)
        lat_t = sb("lat_t", [P, KD, M])
        k_two = sb("k_two", [P, 2, 2, KEYS], F32R)
        v_sb = sb("v_sb", [P, KT, HALF])
        q_hi = sb("q_hi", [P, PAIRS, 2, M], F32R)
        q_lo = sb("q_lo", [P, PAIRS, 2, M], F32R)
        probs = sb("probs", [P, 2, KT * P])
        probs_t = sb("probs_t", [P, 2, KT * M])
        out_t = sb("out_t", [P, PAIRS, M])
        mask_u8 = sb("mask_u8", [P, N], U8)
        mask_add = sb("mask_add", [P, KEYS])
        res = sb("res", [P, D])
        tail = sb("tail", [P, D])
        gain_o = sb("gain_o", [P, D])
        bias_o = sb("bias_o", [P, D])
        gain_x, bias_x, gain_l, bias_l = (sb(n, [P, D]) for n in ("gain_x", "bias_x", "gain_l", "bias_l"))
        tanh_g = sb("tanh_g", [P, 1])
        eps = sb("eps", [P, 1])
        ident = sb("ident", [P, P])
        stats = sb("stats", [P, NT, 6])
        mean_var = sb("mean_var", [P, NT, 2])
        std = sb("std", [P, NT])
        rstd = sb("rstd", [P, NT])
        neg_max = sb("neg_max", [P, 2])
        row_sum = sb("row_sum", [P, 2])
        row_inv = sb("row_inv", [P, 2])
        SW = INNER
        stage = [wout_sb[:, :, :].rearrange("p k n -> p (k n)")[:, SW * n:SW * n + SW] for n in range(PAIRS * D // SW)]
        stage += [v_sb[:, :, :].rearrange("p t n -> p (t n)")[:, SW * n:SW * n + SW] for n in range(KT * HALF // SW)]
        STAGE = len(stage)

        kv_ps = ps("kv_ps", [P, 2 * BANK])
        s_ps = ps("s_ps", [P, 2 * BANK])
        t_ps = ps("t_ps", [P, 2 * BANK])
        o_ps = ps("o_ps", [P, BANK])
        w_ps = ps("w_ps", [P, BANK])

        c_loaded = sem("c_loaded")
        w_loaded = [sem(f"w_loaded{n}") for n in range(STAGE)]
        w_hi_done = sem("w_hi_done")
        w_lo_done = sem("w_lo_done")
        pq_loaded = sem("pq_loaded")
        wout_loaded = sem("wout_loaded")
        rows_loaded = sem("rows_loaded")
        mask_loaded = sem("mask_loaded")
        res_loaded = sem("res_loaded")
        x_stored = sem("x_stored")
        const_done = sem("const_done")
        tanh_done = sem("tanh_done")
        mask_done = sem("mask_done")
        var_done = sem("var_done")
        std_done = sem("std_done")
        norm_done = sem("norm_done")
        tr_done = sem("tr_done")
        scaled_done = sem("scaled_done")
        in_hi_done = sem("in_hi_done")
        in_lo_done = sem("in_lo_done")
        q_ready = sem("q_ready")
        q_hi_done = sem("q_hi_done")
        q_lo_done = sem("q_lo_done")
        v_ready = sem("v_ready")
        v_done = sem("v_done")
        k_ready = sem("k_ready")
        k_hi_done = sem("k_hi_done")
        k_lo_done = sem("k_lo_done")
        s_ready = sem("s_ready")
        max_done = sem("max_done")
        exp_done = sem("exp_done")
        p_done = sem("p_done")
        t_ready = sem("t_ready")
        ta_done = sem("ta_done")
        tb_done = sem("tb_done")
        o_ready = sem("o_ready")
        o_done = sem("o_done")
        y_ready = sem("y_ready")
        y_read = sem("y_read")
        x_done = sem("x_done")
        held = sem("held")
        chain = sem("chain")
        pool_chain = sem("pool_chain")

        halves = (slice(0, HD), slice(HD, P))

        block = ctx.enter_context(nc.Block())


        @block.sync
        def _(sp):
            for s in (x_stored, rows_loaded, mask_loaded, res_loaded):
                sp.sem_inc(s, 1)

            def load_rows(b):
                full = P * (CT - 1)
                sp.dma_start(rows[:, 0:CT - 1, :], ctx_rows[b, 0:full, :].rearrange("(t p) d -> p t d", p=P)).then_inc(rows_loaded, 16)
                sp.dma_start(rows[0:CROWS[-1], CT - 1, :], ctx_rows[b, full:N, :]).then_inc(rows_loaded, 16)
                sp.dma_start(lat[0:M, :], x_in[b, :, :]).then_inc(rows_loaded, 16)

            def load_mask(b):
                sp.dma_start(mask_u8[0:M, :], keep_mask[b, :].rearrange("(a n) -> a n", a=1).to_broadcast([M, N])).then_inc(mask_loaded, 16)

            def load_res(b):
                sp.dma_start(res[0:M, :], x_in[b, :, :]).then_inc(res_loaded, 16)

            load_rows(0)
            for t, src in ((gain_x, ln_x_g), (bias_x, ln_x_b), (gain_l, ln_l_g), (bias_l, ln_l_b)):
                sp.dma_start(t[:, :], src.rearrange("(a n) -> a n", a=1).to_broadcast([P, D])).then_inc(c_loaded, 16)
            sp.dma_start(gain_o[0:M, :], ln_o_g.rearrange("(a n) -> a n", a=1).to_broadcast([M, D])).then_inc(c_loaded, 16)
            sp.dma_start(bias_o[0:M, :], ln_o_b.rearrange("(a n) -> a n", a=1).to_broadcast([M, D])).then_inc(c_loaded, 16)
            sp.dma_start(tanh_g[:, :], gate.to_broadcast([P, 1])).then_inc(c_loaded, 16)
            for n in range(2 * KD):
                if n >= STAGE:
                    sp.wait_ge(w_lo_done, 1 + n - STAGE + 1)
                sp.dma_start(stage[n % STAGE], wkv[P * (n // 2):P * (n // 2 + 1), SW * (n % 2):SW * (n % 2 + 1)]).then_inc(w_loaded[n % STAGE], 16)
                if n == STAGE - 1:
                    sp.dma_start(wq_sb[:, :, :], wq.rearrange("(k p) n -> p k n", p=P)).then_inc(pq_loaded, 16)
            sp.wait_ge(w_lo_done, 1 + 2 * KD)
            sp.dma_start(wout_sb[:, :, :], wout.rearrange("(k p) n -> p k n", p=P)).then_inc(wout_loaded, 16)
            load_mask(0)
            load_res(0)

            def turn(i, last):
                if not last:
                    sp.wait_ge(tr_done, 1 + NT * i + NT)
                    sp.sem_inc(held, 1)
                    load_rows(i + 1)
                    sp.wait_ge(mask_done, 1 + i + 1)
                    sp.sem_inc(held, 1)
                    load_mask(i + 1)
                sp.wait_ge(x_done, 1 + i + 1)
                sp.sem_inc(held, 1)
                sp.dma_start(x_out[i, :, :], tail[0:M, :]).then_inc(x_stored, 16)
                if not last:
                    load_res(i + 1)

            with sp.Fori(0, B - 1) as i:
                turn(i, False)
            turn(B - 1, True)
            sp.wait_ge(x_stored, 1 + 16 * B)

        @block.gpsimd
        def _(pool):
            for s in (const_done, scaled_done, pool_chain):
                pool.sem_inc(s, 1)
            own = Chain(pool, pool_chain)
            nc.gpsimd.memset(ident[:, :], 0.0).then_inc(const_done, 1)
            nc.gpsimd.memset(probs[:, :, :], 0.0).then_inc(const_done, 1)
            nc.gpsimd.memset(mask_add[:, :], 0.0).then_inc(const_done, 1)
            nc.gpsimd.memset(mean_var[:, :, :], 1.0).then_inc(const_done, 1)
            nc.gpsimd.memset(eps[:, :], EPS).then_inc(const_done, 1)
            pool.wait_ge(const_done, 2)
            nc.gpsimd.affine_select(out=ident[:, :], in_=ident[:, :], compare_op=ALU.not_equal, fill=1.0, base=0,
                                    pattern=[[-1, P]], channel_multiplier=1).then_inc(const_done, 1)

            def scale(p):
                for t in range(NT):
                    n = TILE_ROWS[t]
                    pool.wait_ge(norm_done, 1 + NT * p + t + 1)
                    row = lat[0:M, :] if t == LAT else rows[0:n, t, :]
                    g, b = (gain_l, bias_l) if t == LAT else (gain_x, bias_x)
                    pool.sem_inc(held, 1)
                    own.link(nc.gpsimd.tensor_tensor(row, row, g[0:n, :], ALU.mult))
                    nc.gpsimd.tensor_tensor(row, row, b[0:n, :], ALU.add).then_inc(scaled_done, 1)

            pool.wait_ge(c_loaded, 16 * 7)
            scale(0)
            pool.wait_ge(w_lo_done, 1 + 2 * KD)
            nc.gpsimd.memset(v_sb[:, KT - 1, :], 0.0).then_inc(const_done, 1)
            with own.loop(B - 1, NT) as i:
                scale(i + 1)

        @block.scalar
        def _(act):
            for s in (tanh_done, in_hi_done, q_hi_done, v_done, k_hi_done, exp_done, ta_done, w_hi_done):
                act.sem_inc(s, 1)
            act.wait_ge(c_loaded, 16 * 7)
            nc.scalar.activation(tanh_g[:, :], tanh_g[:, :], ACT.Tanh).then_inc(tanh_done, 1)

            def deviations(p, first=False):
                act.wait_ge(var_done, 1 if first else 3 * p)
                nc.scalar.activation(std[:, 0:NT], mean_var[:, 0:NT, 1], ACT.Sqrt, bias=eps[:, :]).then_inc(std_done, 1)

            def deviation_lat(p, first=False):
                act.wait_ge(var_done, 2 if first else 3 * p + 1)
                nc.scalar.activation(std[0:M, LAT:NT], mean_var[0:M, LAT:NT, 1], ACT.Sqrt, bias=eps[0:M, :]).then_inc(std_done, 1)

            def prepare(p, t):
                n, c = TILE_ROWS[t], TILE_COL[t]
                act.wait_ge(tr_done, 1 + NT * p + t + 1)
                src = kv_ps[:, BANK * (t % 2):BANK * (t % 2) + BANK].rearrange("p (k q) -> p k q", q=P)[:, :, 0:n]
                if t == LAT:
                    act.wait_ge(q_ready, 1 + p)
                    nc.scalar.activation(lat_t[:, :, :], src, ACT.Copy)
                nc.scalar.activation(kvin_hi[:, :, c:c + n], src, ACT.Copy).then_inc(in_hi_done, 1)

            def queries(i):
                act.wait_ge(q_ready, 1 + i + 1)
                for x in range(2):
                    for m in range(2):
                        n = PAIRS // 2
                        src = s_ps[HD * x:HD * x + HD, BANK * m:BANK * m + n * M].rearrange("p (h q) -> p h q", q=M)
                        for at in halves:
                            ins = nc.scalar.activation(q_hi[at, n * m:n * m + n, x, :], src, ACT.Copy, scale=SCALE)
                ins.then_inc(q_hi_done, 1)

            def values(i, half, t):
                act.wait_ge(v_ready, 1 + 2 * KT * i + KT * half + t + 1)
                act.wait_ge(o_ready, 1 + PAIRS * i + PAIRS // 2 * half)
                n = KROWS[t]
                nc.scalar.activation(v_sb[0:n, t, :], kv_ps[0:n, BANK * (t % 2):BANK * (t % 2) + HALF], ACT.Copy).then_inc(v_done, 1)

            def keys(i, hp, part):
                c, n = PART[part]
                act.wait_ge(k_ready, 1 + 2 * PAIRS * i + 2 * hp + part + 1)
                act.wait_ge(s_ready, 1 + 2 * PAIRS * i + (2 * hp - 2 if hp >= 2 else 0))
                for x in range(2):
                    nc.scalar.activation(k_two[halves[x], hp % 2, x, c:c + n], kv_ps[halves[x], c:c + n], ACT.Copy).then_inc(k_hi_done, 1)

            def move_t(i, hp, r):
                act.wait_ge(t_ready, 1 + 4 * PAIRS * i + 4 * hp + r + 1)
                act.wait_ge(o_ready, 1 + PAIRS * i + hp)
                c, n = (0, FIRST_T * M) if r == 0 else (FIRST_T * M, (KT - FIRST_T) * M)
                nc.scalar.activation(probs_t[:, 0, c:c + n], t_ps[:, BANK * r:BANK * r + n], ACT.Copy).then_inc(ta_done, 1)

            def exponent(i, hp, x):
                act.wait_ge(max_done, 1 + 2 * PAIRS * i + 2 * hp + x + 1)
                nc.scalar.activation(probs[0:M, x, 0:KEYS], probs[0:M, x, 0:KEYS], ACT.Exp, scale=-1.0,
                                     bias=neg_max[0:M, x:x + 1], accum_out=row_sum[0:M, x:x + 1]).then_inc(exp_done, 1)

            act.wait_ge(const_done, 7)
            deviations(0, True)
            for n in range(2 * KD):
                act.wait_ge(w_loaded[n % STAGE], 16 * (n // STAGE + 1))
                nc.scalar.activation(wkv_hi[:, n // 2, SW * (n % 2):SW * (n % 2 + 1)], stage[n % STAGE],
                                     ACT.Copy).then_inc(w_hi_done, 1)
                if n == 1:
                    deviation_lat(0, True)
                if n >= 3:
                    prepare(0, n - 3)
            for t in range(2 * KD - 3, NT):
                prepare(0, t)
            queries(0)
            keys(0, 0, 0)
            keys(0, 0, 1)

            def turn(i, last):
                for t in range(KT):
                    values(i, 0, t)
                    if t in (2, 4):
                        exponent(i, 0, (t - 2) // 2)
                move_t(i, 0, 0)
                move_t(i, 0, 1)
                keys(i, 1, 0)
                keys(i, 1, 1)
                for hp in range(1, PAIRS):
                    if hp >= 2:
                        move_t(i, hp - 1, 0)
                        move_t(i, hp - 1, 1)
                    for x in range(2):
                        if hp == PAIRS - 1 and not last:
                            prepare(i + 1, 2 * x)
                            prepare(i + 1, 2 * x + 1)
                        if hp + 1 < PAIRS and x == 1:
                            keys(i, hp + 1, x)
                        exponent(i, hp, x)
                        if hp + 1 < PAIRS and x == 0:
                            keys(i, hp + 1, x)
                    if hp == PAIRS // 2:
                        for t in range(KT):
                            values(i, 1, t)
                            if not last and t == 2:
                                deviations(i + 1)
                            if not last and t == 4:
                                deviation_lat(i + 1)
                if not last:
                    prepare(i + 1, 4)
                move_t(i, PAIRS - 1, 0)
                move_t(i, PAIRS - 1, 1)
                if not last:
                    prepare(i + 1, 5)
                    prepare(i + 1, 6)
                    queries(i + 1)
                    keys(i + 1, 0, 0)
                    keys(i + 1, 0, 1)
                act.wait_ge(var_done, 3 * i + (3 if last else 5))
                nc.scalar.activation(std[0:M, 0:1], mean_var[0:M, 0:1, 1], ACT.Sqrt, bias=eps[0:M, :]).then_inc(std_done, 1)

            with act.Fori(0, B - 1) as i:
                turn(i, False)
            turn(B - 1, True)

        @block.tensor
        def _(pe):
            for s in (tr_done, q_ready, v_ready, k_ready, s_ready, t_ready, o_ready, y_ready):
                pe.sem_inc(s, 1)

            def three(out, hi_l, lo_l, hi_r, lo_r, first, last):
                nc.tensor.matmul(out, hi_l, hi_r, start=first, stop=False)
                nc.tensor.matmul(out, hi_l, lo_r, start=False, stop=False)
                return nc.tensor.matmul(out, lo_l, hi_r, start=False, stop=last)

            def prepare(p, t):
                n = TILE_ROWS[t]
                pe.wait_ge(scaled_done, 1 + NT * p + t + 1)
                if t < 2:
                    pe.wait_ge(k_lo_done, 1 + 2 * PAIRS * p)
                else:
                    pe.wait_ge(in_lo_done, 1 + NT * p + t - 1)
                for k in range(KD):
                    src = lat[0:M, P * k:P * k + P] if t == LAT else rows[0:n, t, P * k:P * k + P]
                    ins = nc.tensor.transpose(kv_ps[:, BANK * (t % 2) + P * k:BANK * (t % 2) + P * k + n], src, ident[0:n, 0:n])
                ins.then_inc(tr_done, 1)

            def queries(i):
                pe.wait_ge(in_hi_done, 1 + NT * i + NT)
                pe.wait_ge(max_done, 1 + 2 * PAIRS * i)
                for m in range(PAIRS):
                    c = BANK * (m // (PAIRS // 2)) + M * (m % (PAIRS // 2))
                    for k in range(KD):
                        ins = nc.tensor.matmul(s_ps[:, c:c + M], wq_sb[:, k, P * m:P * m + P], lat_t[:, k, :], start=(k == 0), stop=(k == KD - 1))
                ins.then_inc(q_ready, 1)

            def values(i, half, t):
                n = KROWS[t]
                if t >= 2:
                    pe.wait_ge(v_done, 1 + 2 * KT * i + KT * half + t - 1)
                elif half:
                    pe.wait_ge(k_lo_done, 1 + 2 * PAIRS * i + 2 * (PAIRS // 2 + 1) + t + 1)
                else:
                    pe.wait_ge(k_lo_done, 1 + 2 * PAIRS * i + t + 1)
                out = kv_ps[0:n, BANK * (t % 2):BANK * (t % 2) + HALF]
                for k in range(KD):
                    r = slice(P * t, P * t + n)
                    c = slice(INNER + HALF * half, INNER + HALF * half + HALF)
                    ins = three(out, kvin_hi[:, k, r], kvin_lo[:, k, r], wkv_hi[:, k, c], wkv_lo[:, k, c], k == 0, k == KD - 1)
                ins.then_inc(v_ready, 1)

            def keys(i, hp, part):
                if hp == 0:
                    pe.wait_ge(in_lo_done, 1 + NT * i + NT)
                elif hp == 1:
                    pe.wait_ge(v_done, 1 + 2 * KT * i + KT)
                elif hp == PAIRS // 2 + 2:
                    pe.wait_ge(v_done, 1 + 2 * KT * i + 2 * KT)
                else:
                    pe.wait_ge(k_lo_done, 1 + 2 * PAIRS * i + 2 * (hp - 1) + part + 1)
                c, n = PART[part]
                m = slice(P * hp, P * hp + P)
                for k in range(KD):
                    ins = three(kv_ps[:, c:c + n], wkv_hi[:, k, m], wkv_lo[:, k, m], kvin_hi[:, k, c:c + n], kvin_lo[:, k, c:c + n],
                                k == 0, k == KD - 1)
                ins.then_inc(k_ready, 1)

            def scores(i, hp, x):
                pe.wait_ge(k_lo_done, 1 + 2 * PAIRS * i + 2 * hp + 2)
                pe.wait_ge(q_lo_done, 1 + i + 1)
                pe.wait_ge(max_done, 1 + 2 * PAIRS * i + 2 * hp + x)
                for c, n in PART:
                    k = k_two[:, hp % 2, x, c:c + n]
                    nc.tensor.matmul(s_ps[0:M, c:c + n], q_hi[:, hp, x, :], k, start=True, stop=False)
                    ins = nc.tensor.matmul(s_ps[0:M, c:c + n], q_lo[:, hp, x, :], k, start=False, stop=True)
                ins.then_inc(s_ready, 1)

            def transposes(i, hp, x):
                pe.wait_ge(p_done, 1 + 2 * PAIRS * i + 2 * hp + x + 1)
                for r in range(2):
                    if x:
                        pe.wait_ge(ta_done, 1 + 2 * PAIRS * i + 2 * hp + r + 1)
                    else:
                        pe.wait_ge(tb_done, 1 + 2 * PAIRS * i + (2 * hp + r - 1 if hp else 0))
                    for t in (range(FIRST_T) if r == 0 else range(FIRST_T, KT)):
                        c = BANK * r + M * (t - FIRST_T * r)
                        ins = nc.tensor.transpose(t_ps[:, c:c + M], probs[0:M, x, P * t:P * t + P], ident[0:M, 0:M])
                    ins.then_inc(t_ready, 1)

            def attend(i, hp):
                pe.wait_ge(ta_done, 1 + 2 * PAIRS * i + 2 * hp + 2)
                pe.wait_ge(tb_done, 1 + 2 * PAIRS * i + 2 * hp + 2)
                pe.wait_ge(v_done, 1 + 2 * KT * i + KT * (1 + hp // (PAIRS // 2)))
                pe.wait_ge(o_done, 1 + PAIRS * i + hp)
                for t in range(KT):
                    for x in range(2):
                        c = HD * (2 * (hp % (PAIRS // 2)) + x)
                        ins = nc.tensor.matmul(o_ps[HD * x:HD * x + HD, 0:M], v_sb[:, t, c:c + HD], probs_t[:, x, M * t:M * t + M],
                                               start=(t == 0), stop=(t == KT - 1))
                ins.then_inc(o_ready, 1)

            def finish(i):
                pe.wait_ge(wout_loaded, 16)
                pe.wait_ge(o_done, 1 + PAIRS * i + PAIRS)
                pe.wait_ge(y_read, 1 + i)
                for k in range(PAIRS):
                    ins = nc.tensor.matmul(w_ps[0:M, :], out_t[:, k, :], wout_sb[:, k, :], start=(k == 0), stop=(k == PAIRS - 1))
                ins.then_inc(y_ready, 1)

            pe.wait_ge(const_done, 7)
            for t in range(NT):
                prepare(0, t)
            pe.wait_ge(pq_loaded, 16)
            queries(0)
            pe.wait_ge(w_lo_done, 1 + 2 * KD)
            keys(0, 0, 0)
            keys(0, 0, 1)
            pe.wait_ge(const_done, 8)

            def turn(i, last):
                for t in range(KT):
                    values(i, 0, t)
                    if t in (1, 3):
                        scores(i, 0, t // 2)
                for x in range(2):
                    transposes(i, 0, x)
                    keys(i, 1, x)
                attend(i, 0)
                for hp in range(1, PAIRS):
                    for x in range(2):
                        if hp >= 2:
                            transposes(i, hp - 1, x)
                        scores(i, hp, x)
                        if hp + 1 < PAIRS:
                            keys(i, hp + 1, x)
                        elif not last:
                            prepare(i + 1, 2 * x)
                            prepare(i + 1, 2 * x + 1)
                    if hp >= 2:
                        attend(i, hp - 1)
                    if hp == PAIRS // 2:
                        for t in range(KT):
                            values(i, 1, t)
                for x in range(2):
                    if not last:
                        prepare(i + 1, 4 + x)
                    transposes(i, PAIRS - 1, x)
                if not last:
                    prepare(i + 1, 6)
                attend(i, PAIRS - 1)
                if not last:
                    queries(i + 1)
                finish(i)
                if not last:
                    keys(i + 1, 0, 0)
                    keys(i + 1, 0, 1)

            with pe.Fori(0, B - 1) as i:
                turn(i, False)
            turn(B - 1, True)

        @block.vector
        def _(dve):
            for s in (mask_done, norm_done, in_lo_done, q_lo_done, k_lo_done, max_done, p_done, tb_done, o_done, y_read,
                      x_done, w_lo_done, chain):
                dve.sem_inc(s, 1)
            own = Chain(dve, chain)

            def moments(p):
                dve.wait_ge(rows_loaded, 1 + 48 * (p + 1))
                for t in range(NT):
                    n = TILE_ROWS[t]
                    ins = nc.vector.bn_stats(stats[0:n, t, :], lat[0:M, :] if t == LAT else rows[0:n, t, :])
                own.link(ins)
                dve.sem_inc(held, 1)
                for t in range(NT):
                    n = TILE_ROWS[t]
                    ins = nc.vector.bn_aggr(mean_var[0:n, t, :], stats[0:n, t, :])
                ins.then_inc(var_done, 1)

            def normalise(p, first=False):
                dve.wait_ge(std_done, 1 if first else 3 * p)
                own.link(nc.vector.reciprocal(rstd[:, 0:NT], std[:, 0:NT]))
                own.link(nc.vector.tensor_scalar(lat[0:M, :], lat[0:M, :], mean_var[0:M, LAT, 0:1], rstd[0:M, LAT:NT], ALU.subtract, ALU.mult))
                own.link(nc.vector.bn_stats(stats[0:M, LAT, :], lat[0:M, :]))
                dve.sem_inc(held, 1)
                nc.vector.bn_aggr(mean_var[0:M, LAT, :], stats[0:M, LAT, :]).then_inc(var_done, 1)
                for t in range(CT):
                    n = TILE_ROWS[t]
                    nc.vector.tensor_scalar(rows[0:n, t, :], rows[0:n, t, :], mean_var[0:n, t, 0:1], rstd[0:n, t:t + 1],
                                            ALU.subtract, ALU.mult).then_inc(norm_done, 1)
                dve.wait_ge(std_done, 2 if first else 3 * p + 1)
                own.link(nc.vector.reciprocal(rstd[0:M, LAT:NT], std[0:M, LAT:NT]))
                nc.vector.tensor_scalar(lat[0:M, :], lat[0:M, :], mean_var[0:M, LAT, 0:1], rstd[0:M, LAT:NT],
                                        ALU.subtract, ALU.mult).then_inc(norm_done, 1)

            def prepare(p, t):
                n, c = TILE_ROWS[t], TILE_COL[t]
                dve.wait_ge(in_hi_done, 1 + NT * p + t + 1)
                src = kv_ps[:, BANK * (t % 2):BANK * (t % 2) + BANK].rearrange("p (k q) -> p k q", q=P)[:, :, 0:n]
                nc.vector.tensor_tensor(kvin_lo[:, :, c:c + n], src, kvin_hi[:, :, c:c + n].bitcast(F32), ALU.subtract).then_inc(in_lo_done, 1)

            def mask(i):
                dve.wait_ge(mask_loaded, 1 + 16 * (i + 1))
                nc.vector.tensor_scalar(mask_add[0:M, 0:N], mask_u8[0:M, :], 1.0, FAR, ALU.subtract, ALU.mult).then_inc(mask_done, 1)
                dve.wait_ge(mask_done, 1 + i + 1)

            def queries(i):
                dve.wait_ge(q_hi_done, 1 + i + 1)
                for x in range(2):
                    for m in range(2):
                        n = PAIRS // 2
                        src = s_ps[HD * x:HD * x + HD, BANK * m:BANK * m + n * M].rearrange("p (h q) -> p h q", q=M)
                        hi = q_hi[halves[x], n * m:n * m + n, x, :].bitcast(F32)
                        for at in halves:
                            ins = nc.vector.scalar_tensor_tensor(q_lo[at, n * m:n * m + n, x, :], src, SCALE, hi, ALU.mult, ALU.subtract)
                ins.then_inc(q_lo_done, 1)

            def keys(i, hp, part):
                c, n = PART[part]
                for x in range(2):
                    dve.wait_ge(k_hi_done, 1 + 4 * PAIRS * i + 4 * hp + 2 * part + x + 1)
                    ins = nc.vector.tensor_tensor(k_two[halves[1 - x], hp % 2, x, c:c + n], kv_ps[halves[x], c:c + n],
                                                  k_two[halves[x], hp % 2, x, c:c + n].bitcast(F32), ALU.subtract)
                ins.then_inc(k_lo_done, 1)

            def maximum(i, hp, x):
                dve.wait_ge(s_ready, 1 + 2 * PAIRS * i + 2 * hp + x + 1)
                dve.wait_ge(t_ready, 1 + 4 * PAIRS * i + (4 * hp - 2 + 2 * x if hp else 0))
                dve.sem_inc(held, 1)
                nc.vector.tensor_tensor_reduce(out=probs[0:M, x, 0:KEYS], in0=s_ps[0:M, 0:KEYS], in1=mask_add[0:M, :], scale=-1.0,
                                               scalar=3.0e38, op0=ALU.add, op1=ALU.min, accum_out=neg_max[0:M, x:x + 1]).then_inc(max_done, 1)

            def divide(i, hp, x):
                dve.wait_ge(exp_done, 1 + 2 * PAIRS * i + 2 * hp + x + 1)
                own.link(nc.vector.reciprocal(row_inv[0:M, x:x + 1], row_sum[0:M, x:x + 1]))
                nc.vector.tensor_scalar(probs[0:M, x, 0:KEYS], probs[0:M, x, 0:KEYS], row_inv[0:M, x:x + 1], None, ALU.mult).then_inc(p_done, 1)

            def move_t(i, hp, r):
                dve.wait_ge(t_ready, 1 + 4 * PAIRS * i + 4 * hp + 2 + r + 1)
                dve.wait_ge(o_ready, 1 + PAIRS * i + hp)
                c, n = (0, FIRST_T * M) if r == 0 else (FIRST_T * M, (KT - FIRST_T) * M)
                nc.vector.tensor_copy(probs_t[:, 1, c:c + n], t_ps[:, BANK * r:BANK * r + n]).then_inc(tb_done, 1)

            def move_o(i, hp):
                dve.wait_ge(o_ready, 1 + PAIRS * i + hp + 1)
                dve.wait_ge(y_ready, 1 + i)
                nc.vector.tensor_copy(out_t[:, hp, :], o_ps[:, 0:M]).then_inc(o_done, 1)

            def finish(i, last):
                dve.wait_ge(y_ready, 1 + i + 1)
                own.link(nc.vector.bn_stats(stats[0:M, 0, :], w_ps[0:M, :]))
                dve.sem_inc(held, 1)
                nc.vector.bn_aggr(mean_var[0:M, 0, :], stats[0:M, 0, :]).then_inc(var_done, 1)
                dve.wait_ge(std_done, 3 * i + (3 if last else 5))
                own.link(nc.vector.reciprocal(rstd[0:M, 0:1], std[0:M, 0:1]))
                dve.wait_ge(x_stored, 1 + 16 * i)
                nc.vector.tensor_scalar(tail[0:M, :], w_ps[0:M, :], mean_var[0:M, 0, 0:1], rstd[0:M, 0:1], ALU.subtract, ALU.mult).then_inc(y_read, 1)
                dve.wait_ge(y_read, 1 + i + 1)
                own.link(nc.vector.tensor_tensor(tail[0:M, :], tail[0:M, :], gain_o[0:M, :], ALU.mult))
                own.link(nc.vector.tensor_tensor(tail[0:M, :], tail[0:M, :], bias_o[0:M, :], ALU.add))
                dve.wait_ge(res_loaded, 1 + 16 * (i + 1))
                nc.vector.scalar_tensor_tensor(tail[0:M, :], tail[0:M, :], tanh_g[0:M, 0:1], res[0:M, :], ALU.mult, ALU.add).then_inc(x_done, 1)

            dve.wait_ge(const_done, 7)
            moments(0)
            normalise(0, True)
            for n in range(2 * KD):
                dve.wait_ge(w_hi_done, 1 + n + 1)
                at = (slice(0, P), n // 2, slice(SW * (n % 2), SW * (n % 2 + 1)))
                nc.vector.tensor_tensor(wkv_lo[at], stage[n % STAGE], wkv_hi[at].bitcast(F32), ALU.subtract).then_inc(w_lo_done, 1)
                if n >= 3:
                    prepare(0, n - 3)
            for t in range(2 * KD - 3, NT):
                prepare(0, t)
            queries(0)
            keys(0, 0, 0)
            keys(0, 0, 1)
            dve.wait_ge(tanh_done, 2)
            dve.wait_ge(c_loaded, 16 * 7)

            def turn(i, last):
                mask(i)
                for x in range(2):
                    maximum(i, 0, x)
                    divide(i, 0, x)
                for x in range(2):
                    if x == 1:
                        move_t(i, 0, 0)
                        move_t(i, 0, 1)
                    keys(i, 1, x)
                move_o(i, 0)
                for hp in range(1, PAIRS):
                    for x in range(2):
                        maximum(i, hp, x)
                        if hp == PAIRS - 1 and not last:
                            prepare(i + 1, 2 * x)
                            prepare(i + 1, 2 * x + 1)
                        if hp + 1 < PAIRS and x == 1:
                            keys(i, hp + 1, x)
                        divide(i, hp, x)
                        if hp >= 2 and x == 0:
                            move_t(i, hp - 1, 0)
                            move_t(i, hp - 1, 1)
                        if hp + 1 < PAIRS and x == 0:
                            keys(i, hp + 1, x)
                    if hp >= 2:
                        move_o(i, hp - 1)
                    if hp == PAIRS // 2 and not last:
                        moments(i + 1)
                        normalise(i + 1)
                if not last:
                    prepare(i + 1, 4)
                move_t(i, PAIRS - 1, 0)
                move_t(i, PAIRS - 1, 1)
                if not last:
                    prepare(i + 1, 5)
                    prepare(i + 1, 6)
                move_o(i, PAIRS - 1)
                if not last:
                    queries(i + 1)
                    keys(i + 1, 0, 0)
                    keys(i + 1, 0, 1)
                finish(i, last)

            with own.loop(B - 1, 2 * PAIRS + 9) as i:
                turn(i, False)
            turn(B - 1, True)


def three(nc, out, left_hi, left_lo, right_hi, right_lo, start, stop):
    nc.tensor.matmul(out, left_hi, right_hi, start=start, stop=False)
    nc.tensor.matmul(out, left_hi, right_lo, start=False, stop=False)
    return nc.tensor.matmul(out, left_lo, right_hi, start=False, stop=stop)


TOP = 2


def slots(tokens, experts):
    n = (TOP * tokens - experts) // 128 + experts
    return n + n % 2


def gated_experts(nc, name, x_in, router, router_bias, w_a, w_b, w_y, out_major, gate, place, gates, y_dram, x_out):
    B, M, D = x_in.shape
    P = 128
    T = B * M
    HT = T // 2
    HB = B // 2
    KD = D // P
    if out_major:
        E, F = w_a.shape[0], w_a.shape[1]
    else:
        E, F = w_a.shape[0], w_a.shape[2]
    G = F // P
    TILES = (T + P - 1) // P
    SLOTS = slots(T, E)
    RESIDENT = not out_major
    STAGED = SLOTS if RESIDENT else 3
    RING = 3 * E if RESIDENT else 4
    BANK = 512
    EPS = 1e-5
    U32 = mybir.dt.uint32

    tokens_dram = nc.dram_tensor(f"{name}_tokens", [SLOTS * P, D], F32, kind="Internal").ap()

    with ExitStack() as ctx:
        def sb(n, shape, dt=F32):
            return ctx.enter_context(nc.sbuf_tensor(f"{name}_{n}", shape, dt))

        def sem(n):
            return nc.alloc_semaphore(f"{name}_{n}")

        wab_hi = sb("wab_hi", [P, E, KD, 2 * P], F32R)
        wab_lo = sb("wab_lo", [P, E, KD, 2 * P], F32R)
        wy_hi = sb("wy_hi", [P, E, D], F32R)
        wy_lo = sb("wy_lo", [P, E, D], F32R)
        xs = sb("xs", [P, SLOTS, KD, P])
        x_hi = sb("x_hi", [P, STAGED, KD, P], F32R)
        x_lo = sb("x_lo", [P, STAGED, KD, P], F32R)
        y_acc = sb("y_acc", [P, SLOTS, D])
        ht_hi = sb("ht_hi", [P, SLOTS, P], F32R)
        ht_lo = sb("ht_lo", [P, SLOTS, P], F32R)
        raw = sb("raw", [P, RING, KD, P])
        s_sb = sb("s_sb", [P, 2, P])
        h_sb = sb("h_sb", [P, 2, P])
        ident = sb("ident", [P, P])
        expert = sb("expert", [1, SLOTS], U32)
        tanh_g = sb("tanh_g", [P, 1])
        table = sb("table", [1, 2])

        x_tok = y_acc[:, 0:B, :]
        zeros = y_acc[:, B, :]
        slot_rows = y_acc
        y_got = xs[:, 0:TOP * B, :, :].rearrange("p s k q -> p s (k q)")
        free = [xs[:, :, :, :].rearrange("p s k q -> p (s k q)")]

        def cut(*dims):
            n = 1
            for d in dims:
                n *= d
            piece, free[0] = free[0][:, 0:n], free[0][:, n:]
            if len(dims) == 2:
                return piece.rearrange("p (a b) -> p a b", b=dims[1])
            if len(dims) == 3:
                return piece.rearrange("p (a b c) -> p a b c", b=dims[1], c=dims[2])
            return piece

        xn_t = cut(KD, T)
        logit_t = cut(T)
        r_raw = cut(D) if out_major else None
        r_t = cut(KD, E)
        r_bias = cut(1)
        logits, p_exp, rank, chosen, pos, work = (cut(B, E) for _ in range(6))
        batches_before = cut(B + 1, E)
        above, equal = (cut(B, E, E) for _ in range(2))
        before, starts_of = (cut(E, E) for _ in range(2))
        l_max, p_sum, pos_f = cut(B), cut(B), cut(B)
        earlier = cut(P)
        ones = cut(P)
        threshold = cut(TILES)
        filled = cut(E, TILES)
        count, start, end = cut(E), cut(E), cut(E)
        slot_no = cut(SLOTS)
        passed = cut(SLOTS, E)
        expert_f = cut(SLOTS)
        eps = cut(1)
        stats, mean_var = cut(B, 6), cut(B, 2)
        std, rstd = cut(B), cut(B)

        banks = ctx.enter_context(nc.psum_tensor(f"{name}_banks", [P, 8, BANK], F32))
        H, HT_T, W = 0, 2, 6
        Y = (4, 5, 2, 3)

        x_loaded = [sem(f"x_loaded{n}") for n in range(2)]
        c_loaded = sem("c_loaded")
        raw_loaded = [sem(f"raw_loaded{n}") for n in range(RING)]
        zeroed = sem("zeroed")
        scattered = sem("scattered")
        rows_loaded = [sem(f"rows_loaded{n}") for n in range(SLOTS // 4)]
        y_stored = sem("y_stored")
        y_gathered = [sem(f"y_gathered{b}") for b in range(B)]
        x_again = sem("x_again")
        x_stored = sem("x_stored")
        const_done = sem("const_done")
        zero_tile = sem("zero_tile")
        acc_zeroed = sem("acc_zeroed")
        tanh_done = sem("tanh_done")
        var_done = sem("var_done")
        std_done = sem("std_done")
        norm_done = sem("norm_done")
        tr_done = sem("tr_done")
        xn_done = sem("xn_done")
        rt_ready = sem("rt_ready")
        rt_done = sem("rt_done")
        logit_ready = sem("logit_ready")
        logit_done = sem("logit_done")
        back_ready = sem("back_ready")
        shift_done = sem("shift_done")
        exp_done = sem("exp_done")
        chosen_done = sem("chosen_done")
        count_ready = sem("count_ready")
        expert_done = sem("expert_done")
        gates_done = sem("gates_done")
        place_done = sem("place_done")
        st_ready = sem("st_ready")
        xs_a = sem("xs_a")
        xs_b = sem("xs_b")
        tw_ready = sem("tw_ready")
        whi_done = sem("whi_done")
        wlo_done = sem("wlo_done")
        xhi_a = sem("xhi_a")
        xhi_b = sem("xhi_b")
        xlo_done = sem("xlo_done")
        h_ready = sem("h_ready")
        s_done = sem("s_done")
        h_done = sem("h_done")
        t_ready = sem("t_ready")
        hi_done = sem("hi_done")
        lo_done = sem("lo_done")
        y_ready = sem("y_ready")
        add_done = sem("add_done")
        x_done = sem("x_done")
        held = sem("held")
        chain = sem("chain")

        block = ctx.enter_context(nc.Block())


        def since(g, s, back):
            return 1 + SLOTS * g + max(s - back + 1, 0)

        PIECES = 3 * E
        LAST = 2 * E

        def last_pieces(s):
            n = SLOTS - 4
            return range(min(LAST + E * s // n, PIECES), min(LAST + E * (s + 1) // n, PIECES))

        def first_pieces(s):
            n = SLOTS - 4
            return range(min(LAST * s // n, LAST), min(LAST * (s + 1) // n, LAST))

        def number(g, c):
            return PIECES * g + c

        def loads(g, c):
            return PIECES // RING * g + c // RING + 1

        @block.sync
        def _(sp):
            for q in range(4):
                sp.dma_start(x_tok[0:M, 2 * q:2 * q + 2, :], x_in[2 * q:2 * q + 2].rearrange("b p d -> p b d")).then_inc(x_loaded[q // 2], 16)
            if out_major:
                sp.dma_start(r_raw[0:E, :], router[:, :]).then_inc(c_loaded, 16)
            else:
                sp.dma_start(r_t[:, :, :], router.rearrange("(k p) e -> p k e", p=P), allow_slow_non_contiguous=True).then_inc(c_loaded, 16)
                sp.dma_start(r_bias[0:E, :], router_bias.rearrange("(e a) -> e a", a=1), allow_slow_non_contiguous=True).then_inc(c_loaded, 16)
            sp.dma_start(tanh_g[:, :], gate.to_broadcast([P, 1])).then_inc(c_loaded, 16)

            def load(g, c):
                w, e = (w_y, c - LAST) if c >= LAST else ((w_a, w_b)[c % 2], c // 2)
                if (c >= LAST) == out_major:
                    dst, src = raw[:, c % RING, :, :], w[e, :, bass.ds(P * g, P)].rearrange("(k p) f -> p k f", p=P)
                else:
                    dst, src = raw[:, c % RING, :, :].rearrange("p k q -> p (k q)"), w[e, bass.ds(P * g, P), :]
                sp.dma_start(dst, src).then_inc(raw_loaded[c % RING], 16)

            def reload(g, c):
                sp.wait_ge(tw_ready if out_major else wlo_done, 1 + number(g, c) - RING + 1)
                sp.sem_inc(held, 1)
                load(g, c)

            for c in range(RING):
                load(0, c)
            sp.wait_ge(zero_tile, 1)
            sp.dma_start(tokens_dram.rearrange("(s p) d -> p s d", p=P), zeros.unsqueeze(1).to_broadcast([P, SLOTS, D])).then_inc(zeroed, 16)
            for c in range(RING, LAST):
                reload(0, c)
            sp.wait_ge(scattered, 16 * TOP * B)
            for q in range(SLOTS // 4):
                sp.dma_start(slot_rows[:, 4 * q:4 * q + 4, :],
                             tokens_dram[4 * P * q:4 * P * q + 4 * P, :].rearrange("(s p) d -> p s d", p=P)).then_inc(rows_loaded[q], 16)
            with sp.Fori(0, G - 1) as g:
                for c in range(max(LAST, RING), PIECES):
                    reload(g, c)
                for c in range(max(LAST, RING)):
                    reload(g + 1, c)
            for c in range(max(LAST, RING), PIECES):
                reload(G - 1, c)
            for q in range(SLOTS // 4):
                sp.wait_ge(add_done, 1 + SLOTS * (G - 1) + 4 * q + 4)
                sp.dma_start(y_dram[4 * P * q:4 * P * q + 4 * P, :].rearrange("(s p) d -> p s d", p=P),
                             y_acc[:, 4 * q:4 * q + 4, :]).then_inc(y_stored, 16)
            sp.wait_ge(y_stored, 16 * (SLOTS // 4))
            if x_out is None:
                return
            sp.dma_start(x_tok[0:M, :, :], x_in.rearrange("b p d -> p b d")).then_inc(x_again, 16)
            for b in range(B):
                sp.wait_ge(x_done, b + 1)
                sp.dma_start(x_out[b, :, :], x_tok[0:M, b, :]).then_inc(x_stored, 16)
            sp.wait_ge(x_stored, 16 * B)

        def split_dst(ab, y, c):
            if c >= LAST:
                return y[:, c - LAST, :].rearrange("p (k q) -> p k q", q=P)
            return ab[:, c // 2, :, P * (c % 2):P * (c % 2) + P]

        def split_src(c):
            if out_major:
                return banks[:, W + c % 2, :].rearrange("p (k q) -> p k q", q=P)
            return raw[:, c % RING, :, :]

        @block.gpsimd
        def _(pool):
            pool.sem_inc(xlo_done, 1)

            def split(g, c):
                pool.wait_ge(whi_done, 1 + number(g, c) + 1)
                pool.sem_inc(held, 1)
                nc.gpsimd.tensor_tensor(split_dst(wab_lo, wy_lo, c), split_src(c), split_dst(wab_hi, wy_hi, c).bitcast(F32),
                                        ALU.subtract).then_inc(wlo_done, 1)

            nc.gpsimd.memset(zeros, 0.0).then_inc(zero_tile, 1)
            nc.gpsimd.memset(ident[:, :], 0.0).then_inc(const_done, 1)
            nc.gpsimd.memset(before, 1.0).then_inc(const_done, 1)
            nc.gpsimd.memset(earlier, 1.0).then_inc(const_done, 1)
            nc.gpsimd.memset(table[:, :], 0.0).then_inc(const_done, 1)
            nc.gpsimd.memset(eps, EPS).then_inc(const_done, 1)
            pool.wait_ge(const_done, 5)
            nc.gpsimd.affine_select(out=ident[:, :], in_=ident[:, :], compare_op=ALU.not_equal, fill=1.0, base=0,
                                    pattern=[[-1, P]], channel_multiplier=1).then_inc(const_done, 1)
            nc.gpsimd.affine_select(out=before, in_=before, compare_op=ALU.is_gt, fill=0.0, base=0,
                                    pattern=[[1, E], [-1, E]], channel_multiplier=0).then_inc(const_done, 1)
            nc.gpsimd.affine_select(out=earlier, in_=earlier, compare_op=ALU.is_gt, fill=0.0, base=0,
                                    pattern=[[1, P]], channel_multiplier=-1).then_inc(const_done, 1)
            nc.gpsimd.memset(ones, 1.0).then_inc(const_done, 1)
            nc.gpsimd.memset(batches_before[:, 0, :], 0.0).then_inc(const_done, 1)
            for n in range(TILES):
                nc.gpsimd.memset(threshold[:, n:n + 1], float(P * n)).then_inc(const_done, 1)
            for n in range(SLOTS):
                nc.gpsimd.memset(slot_no[:, n:n + 1], float(n)).then_inc(const_done, 1)
            pool.wait_ge(zeroed, 16)
            pool.wait_ge(place_done, 1)
            for b in range(B):
                for k in range(TOP):
                    nc.gpsimd.indirect_dma_start(tokens_dram[:, :], bass.IndirectOffsetOnAxis(ap=place[0:M, b, k:k + 1], axis=0),
                                                 x_tok[0:M, b, :], None).then_inc(scattered, 16)
            for s in range(SLOTS):
                pool.wait_ge(st_ready, s + 1)
                nc.gpsimd.memset(y_acc[:, s, :], 0.0).then_inc(acc_zeroed, 1)

            def low_part(g, s):
                pool.wait_ge((xhi_a, xhi_b)[s % 2], 1 + SLOTS // 2 * g + s // 2 + 1)
                pool.sem_inc(held, 1)
                nc.gpsimd.tensor_tensor(x_lo[:, s % STAGED, :, :], xs[:, s, :, :], x_hi[:, s % STAGED, :, :].bitcast(F32), ALU.subtract).then_inc(xlo_done, 1)

            pool.wait_ge(xs_a, SLOTS // 2)
            pool.wait_ge(xs_b, SLOTS // 2)
            if RESIDENT:
                for s in range(SLOTS):
                    low_part(0, s)
                with pool.Fori(0, G - 1) as g:
                    for c in range(LAST, PIECES):
                        split(g, c)
                    for c in range(LAST):
                        split(g + 1, c)
                for c in range(LAST, PIECES):
                    split(G - 1, c)
            else:
                with pool.Fori(0, G) as g:
                    for s in range(SLOTS):
                        low_part(g, s)
            if x_out is None:
                return
            pool.wait_ge(y_stored, 16 * (SLOTS // 4))
            pool.wait_ge(h_ready, 1 + SLOTS * G)
            for b in range(B):
                for k in range(TOP):
                    nc.gpsimd.indirect_dma_start(y_got[0:M, TOP * b + k, :], None, y_dram[:, :],
                                                 bass.IndirectOffsetOnAxis(ap=place[0:M, b, k:k + 1], axis=0)).then_inc(y_gathered[b], 16)

        @block.scalar
        def _(act):
            for s in (whi_done, xhi_a, s_done, hi_done):
                act.sem_inc(s, 1)
            act.wait_ge(c_loaded, 16 * (2 if out_major else 3))
            nc.scalar.activation(tanh_g[:, :], tanh_g[:, :], ACT.Tanh).then_inc(tanh_done, 1)
            act.wait_ge(const_done, 5)
            act.wait_ge(var_done, 1)
            nc.scalar.activation(std[0:M, :], mean_var[0:M, :, 1], ACT.Sqrt, bias=eps[0:M, :]).then_inc(std_done, 1)
            if out_major:
                act.wait_ge(rt_ready, 1)
                nc.scalar.activation(r_t, banks[:, 0, 0:KD * E].rearrange("p (k e) -> p k e", e=E), ACT.Copy).then_inc(rt_done, 1)
            for b in range(B):
                act.wait_ge(tr_done, b + 1)
                nc.scalar.activation(xn_t[:, :, M * b:M * b + M], banks[:, 2 + b % 4, :].rearrange("p (k q) -> p k q", q=P)[:, :, 0:M],
                                     ACT.Copy).then_inc(xn_done, 1)
            for half in range(2):
                act.wait_ge(logit_ready, half + 1)
                src = banks[0:E, half, 0:HT]
                dst = logit_t[0:E, HT * half:HT * half + HT]
                if out_major:
                    nc.scalar.activation(dst, src, ACT.Copy).then_inc(logit_done, 1)
                else:
                    nc.scalar.activation(dst, src, ACT.Identity, bias=r_bias[0:E, :]).then_inc(logit_done, 1)
            act.wait_ge(shift_done, 1)
            nc.scalar.activation(p_exp[0:M, :, :], p_exp[0:M, :, :], ACT.Exp).then_inc(exp_done, 1)

            def split(g, c):
                if out_major:
                    act.wait_ge(tw_ready, 1 + number(g, c) + 1)
                else:
                    act.wait_ge(raw_loaded[c % RING], 16 * loads(g, c))
                nc.scalar.activation(split_dst(wab_hi, wy_hi, c), split_src(c), ACT.Copy).then_inc(whi_done, 1)

            def move_tokens(s):
                act.wait_ge(rows_loaded[s // 4], 16)
                act.wait_ge(st_ready, s + 1)
                nc.scalar.activation(xs[:, s, :, :], banks[:, s % 4, :].rearrange("p (k q) -> p k q", q=P), ACT.Copy).then_inc(xs_a, 1)

            def high_part(g, s):
                if s % 2 == 0:
                    act.wait_ge(h_ready, since(g, s, STAGED))
                    nc.scalar.activation(x_hi[:, s % STAGED, :, :], xs[:, s, :, :], ACT.Copy).then_inc(xhi_a, 1)

            def stage_a(g):
                nc.scalar.activation(table[0:1, 1:2], table[0:1, 0:1], ACT.Silu)
                for s in range(SLOTS):
                    n = SLOTS * g + s
                    act.wait_ge(h_ready, 1 + n + 1)
                    act.wait_ge(h_done, since(g, s, 2))
                    nc.scalar.activation(s_sb[:, s % 2, :], banks[:, H + s % 2, 0:P], ACT.Silu).then_inc(s_done, 1)
                    if s + STAGED < SLOTS:
                        high_part(g, s + STAGED)
                    if s:
                        high_hidden(g, s - 1)
                    for c in last_pieces(s):
                        act.wait_ge(y_ready, 1 + SLOTS * g)
                        split(g, c)
                high_hidden(g, SLOTS - 1)

            def high_hidden(g, s):
                act.wait_ge(t_ready, 1 + SLOTS * g + s + 1)
                nc.scalar.activation(ht_hi[:, s, :], banks[:, HT_T + s % 2, 0:P], ACT.Copy).then_inc(hi_done, 1)

            def stage_b(g):
                if not RESIDENT:
                    for s in range(STAGED):
                        high_part(g + 1, s)
                for s in range(SLOTS):
                    for c in first_pieces(s):
                        act.wait_ge(h_ready, 1 + SLOTS * (g + 1))
                        split(g + 1, c)

            for c in range(LAST):
                split(0, c)
            act.wait_ge(gates_done, 1)
            for s in range(0, SLOTS, 2):
                move_tokens(s)
            act.wait_ge(xs_a, SLOTS // 2)
            for s in range(STAGED):
                high_part(0, s)
            with act.Fori(0, G - 1) as g:
                stage_a(g)
                stage_b(g)
            stage_a(G - 1)

        @block.tensor
        def _(pe):
            for s in (tw_ready, h_ready, t_ready, y_ready):
                pe.sem_inc(s, 1)
            pe.wait_ge(const_done, 8)
            if out_major:
                pe.wait_ge(c_loaded, 32)
                for k in range(KD):
                    ins = nc.tensor.transpose(banks[:, 0, E * k:E * k + E], r_raw[0:E, P * k:P * k + P], ident[0:E, 0:E])
                ins.then_inc(rt_ready, 1)
            for b in range(B):
                pe.wait_ge(norm_done, b + 1)
                if b >= 4:
                    pe.wait_ge(xn_done, b - 3)
                for k in range(KD):
                    ins = nc.tensor.transpose(banks[:, 2 + b % 4, P * k:P * k + M], x_tok[0:M, b, P * k:P * k + P], ident[0:M, 0:M])
                ins.then_inc(tr_done, 1)
            if out_major:
                pe.wait_ge(rt_done, 1)
            else:
                pe.wait_ge(c_loaded, 48)
            for half in range(2):
                pe.wait_ge(xn_done, HB * (half + 1))
                for k in range(KD):
                    ins = nc.tensor.matmul(banks[0:E, half, 0:HT], r_t[:, k, :], xn_t[:, k, HT * half:HT * half + HT], start=(k == 0), stop=(k == KD - 1))
                ins.then_inc(logit_ready, 1)
            pe.wait_ge(logit_done, 2)
            for b in range(B):
                ins = nc.tensor.transpose(banks[0:M, 2, E * b:E * b + E], logit_t[0:E, M * b:M * b + M], ident[0:E, 0:E])
            ins.then_inc(back_ready, 1)

            def turn_piece(g, c):
                pe.wait_ge(raw_loaded[c % RING], 16 * loads(g, c))
                pe.wait_ge(wlo_done, number(g, max(c, 1)))
                for k in range(KD):
                    ins = nc.tensor.transpose(banks[:, W + c % 2, P * k:P * k + P], raw[:, c % RING, k, :], ident[:, :])
                ins.then_inc(tw_ready, 1)

            pe.wait_ge(chosen_done, 1)
            flat = "p b e -> p (b e)"
            nc.tensor.matmul(banks[0:M, 0, 0:B * E], earlier[0:M, 0:M], chosen[0:M, :, :].rearrange(flat), start=True, stop=False)
            nc.tensor.matmul(banks[0:M, 0, 0:B * E], ones[0:M, 0:M], batches_before[0:M, 0:B, :].rearrange(flat), start=False, stop=True)
            ins = nc.tensor.matmul(banks[:, 1, 0:E], ones[0:M, :], batches_before[0:M, B, :], start=True, stop=True)
            ins.then_inc(count_ready, 1)
            experts = []

            def load_expert():
                experts.append(pe.value_load(expert[0:1, len(experts):len(experts) + 1], min_val=0, max_val=E - 1))

            if out_major:
                for c in range(LAST):
                    turn_piece(0, c)
                    if c == 3:
                        pe.wait_ge(expert_done, 1)
                    if c >= 3:
                        load_expert()
            else:
                pe.wait_ge(expert_done, 1)
            while len(experts) < SLOTS:
                load_expert()
            for s in range(SLOTS):
                pe.wait_ge(rows_loaded[s // 4], 16)
                if s >= 4:
                    pe.wait_ge((xs_a, xs_b)[s % 2], (s - 4) // 2 + 1)
                for k in range(KD):
                    ins = nc.tensor.transpose(banks[:, s % 4, P * k:P * k + P], slot_rows[:, s, P * k:P * k + P], ident[:, :])
                ins.then_inc(st_ready, 1)
            pe.wait_ge(xs_a, SLOTS // 2)
            pe.wait_ge(xs_b, SLOTS // 2)

            def hidden(g, s):
                if s == 0:
                    pe.wait_ge(wlo_done, 1 + number(g, LAST))
                pe.wait_ge(xlo_done, 1 + (s if RESIDENT else SLOTS * g + s) + 1)
                pe.wait_ge(h_done, since(g, s, 2))
                e = experts[s]
                for k in range(KD):
                    ins = three(nc, banks[:, H + s % 2, 0:2 * P], x_hi[:, s % STAGED, k, :], x_lo[:, s % STAGED, k, :], wab_hi[:, e, k, :], wab_lo[:, e, k, :],
                                k == 0, k == KD - 1)
                ins.then_inc(h_ready, 1)

            def turn_hidden(g, s):
                pe.wait_ge(h_done, 1 + SLOTS * g + s + 1)
                pe.wait_ge(lo_done, since(g, s, 2))
                if s < 2:
                    pe.wait_ge(add_done, 1 + SLOTS * g)
                nc.tensor.transpose(banks[:, HT_T + s % 2, 0:P], h_sb[:, s % 2, :], ident[:, :]).then_inc(t_ready, 1)

            def project(g, s):
                if s == 0:
                    pe.wait_ge(wlo_done, 1 + number(g, PIECES))
                pe.wait_ge(lo_done, 1 + SLOTS * g + s + 1)
                pe.wait_ge(add_done, since(g, s, 4))
                if s in (2, 3):
                    pe.wait_ge(lo_done, 1 + SLOTS * g + SLOTS - 3 + s)
                e = experts[s]
                three(nc, banks[:, Y[s % 4], :], ht_hi[:, s, :], ht_lo[:, s, :], wy_hi[:, e, :], wy_lo[:, e, :], True, True).then_inc(y_ready, 1)

            def stage_a(g):
                for s in range(SLOTS):
                    hidden(g, s)
                    if s:
                        turn_hidden(g, s - 1)
                    if out_major:
                        for c in last_pieces(s):
                            turn_piece(g, c)

            def stage_b(g, last):
                for s in range(SLOTS):
                    project(g, s)
                    if s == 0:
                        turn_hidden(g, SLOTS - 1)
                    if out_major and not last:
                        for c in first_pieces(s):
                            turn_piece(g + 1, c)

            with pe.Fori(0, G - 1) as g:
                stage_a(g)
                stage_b(g, False)
            stage_a(G - 1)
            stage_b(G - 1, True)

        @block.vector
        def _(dve):
            for s in (xhi_b, h_done, lo_done, add_done, chain):
                dve.sem_inc(s, 1)
            dve.sem_inc(wlo_done, 1)
            own = Chain(dve, chain)
            for b in range(B):
                if b % HB == 0:
                    dve.wait_ge(x_loaded[b // HB], 32)
                ins = nc.vector.bn_stats(stats[0:M, b, :], x_tok[0:M, b, :])
            own.link(ins)
            for b in range(B):
                ins = nc.vector.bn_aggr(mean_var[0:M, b, :], stats[0:M, b, :])
            ins.then_inc(var_done, 1)
            dve.wait_ge(std_done, 1)
            own.link(nc.vector.reciprocal(rstd[0:M, :], std[0:M, :]))
            for b in range(B):
                nc.vector.tensor_scalar(x_tok[0:M, b, :], x_tok[0:M, b, :], mean_var[0:M, b, 0:1], rstd[0:M, b:b + 1],
                                        ALU.subtract, ALU.mult).then_inc(norm_done, 1)
            dve.wait_ge(back_ready, 1)
            dve.wait_ge(const_done, 10 + TILES + SLOTS)
            own.link(nc.vector.tensor_copy(logits[0:M, :, :], banks[0:M, 2, 0:B * E].rearrange("p (b e) -> p b e", e=E)))
            own.link(nc.vector.tensor_reduce(l_max[0:M, :], logits[0:M, :, :], axis=AX.X, op=ALU.max))
            nc.vector.tensor_tensor(p_exp[0:M, :, :], logits[0:M, :, :], l_max[0:M, :].unsqueeze(2).to_broadcast([M, B, E]), ALU.subtract).then_inc(shift_done, 1)
            other = logits[0:M, :, :].unsqueeze(2).to_broadcast([M, B, E, E])
            this = logits[0:M, :, :].unsqueeze(3).to_broadcast([M, B, E, E])
            nc.vector.tensor_tensor(above[0:M, :, :, :], other, this, ALU.is_gt)
            own.link(nc.vector.tensor_tensor(equal[0:M, :, :, :], other, this, ALU.is_equal))
            own.link(nc.vector.tensor_tensor(equal[0:M, :, :, :], equal[0:M, :, :, :], before[0:M, :, :].unsqueeze(1).to_broadcast([M, B, E, E]), ALU.mult))
            own.link(nc.vector.tensor_tensor(above[0:M, :, :, :], above[0:M, :, :, :], equal[0:M, :, :, :], ALU.add))
            own.link(nc.vector.tensor_reduce(rank[0:M, :, :], above[0:M, :, :, :], axis=AX.X, op=ALU.add))
            own.link(nc.vector.tensor_scalar(chosen[0:M, :, :], rank[0:M, :, :], TOP - 0.5, None, ALU.is_lt))
            own.link(nc.vector.tensor_copy(batches_before[0:M, 1, :], chosen[0:M, 0, :]))
            for b in range(1, B):
                own.link(nc.vector.tensor_tensor(batches_before[0:M, b + 1, :], batches_before[0:M, b, :], chosen[0:M, b, :], ALU.add))
            dve.sem_inc(chosen_done, 1)
            dve.wait_ge(count_ready, 1)
            own.link(nc.vector.tensor_copy(count, banks[:, 1, 0:E]))
            own.link(nc.vector.tensor_tensor(filled, count.unsqueeze(2).to_broadcast([P, E, TILES]), threshold.unsqueeze(1).to_broadcast([P, E, TILES]), ALU.is_gt))
            own.link(nc.vector.tensor_reduce(count, filled, axis=AX.X, op=ALU.add))
            own.link(nc.vector.tensor_tensor(starts_of, before, count.unsqueeze(1).to_broadcast([P, E, E]), ALU.mult))
            own.link(nc.vector.tensor_reduce(start, starts_of, axis=AX.X, op=ALU.add))
            own.link(nc.vector.tensor_tensor(end, start, count, ALU.add))
            own.link(nc.vector.tensor_tensor(passed, slot_no.unsqueeze(2).to_broadcast([P, SLOTS, E]), end.unsqueeze(1).to_broadcast([P, SLOTS, E]), ALU.is_ge))
            own.link(nc.vector.tensor_reduce(expert_f, passed, axis=AX.X, op=ALU.add))
            own.link(nc.vector.tensor_scalar(expert_f, expert_f, float(E - 1), None, ALU.min))
            nc.vector.tensor_copy(expert[:, :], expert_f[0:1, :]).then_inc(expert_done, 1)
            own.link(nc.vector.tensor_scalar(start, start, float(P), None, ALU.mult))
            own.link(nc.vector.tensor_tensor(pos[0:M, :, :], banks[0:M, 0, 0:B * E].rearrange("p (b e) -> p b e", e=E),
                                             start[0:M, :].unsqueeze(1).to_broadcast([M, B, E]), ALU.add))
            for k in range(TOP):
                own.link(nc.vector.scalar_tensor_tensor(work[0:M, :, :], rank[0:M, :, :], float(k), pos[0:M, :, :], ALU.is_equal, ALU.mult))
                own.link(nc.vector.tensor_reduce(pos_f[0:M, :], work[0:M, :, :], axis=AX.X, op=ALU.add))
                own.link(nc.vector.tensor_copy(place[0:M, :, k], pos_f[0:M, :]))
            dve.sem_inc(place_done, 1)
            dve.wait_ge(exp_done, 1)
            for k in range(TOP):
                own.link(nc.vector.scalar_tensor_tensor(work[0:M, :, :], rank[0:M, :, :], float(k), p_exp[0:M, :, :], ALU.is_equal, ALU.mult))
                own.link(nc.vector.tensor_reduce(gates[0:M, :, k], work[0:M, :, :], axis=AX.X, op=ALU.add))
            own.link(nc.vector.tensor_reduce(p_sum[0:M, :], gates[0:M, :, :], axis=AX.X, op=ALU.add))
            own.link(nc.vector.reciprocal(p_sum[0:M, :], p_sum[0:M, :]))
            dve.wait_ge(tanh_done, 1)
            own.link(nc.vector.tensor_scalar(p_sum[0:M, :], p_sum[0:M, :], tanh_g[0:M, 0:1], None, ALU.mult))
            own.link(nc.vector.tensor_tensor(gates[0:M, :, :], gates[0:M, :, :], p_sum[0:M, :].unsqueeze(2).to_broadcast([M, B, TOP]), ALU.mult))
            dve.sem_inc(gates_done, 1)

            def split(g, c):
                dve.wait_ge(whi_done, 1 + number(g, c) + 1)
                nc.vector.tensor_tensor(split_dst(wab_lo, wy_lo, c), split_src(c), split_dst(wab_hi, wy_hi, c).bitcast(F32),
                                        ALU.subtract).then_inc(wlo_done, 1)

            def move_tokens(s):
                dve.wait_ge(st_ready, s + 1)
                nc.vector.tensor_copy(xs[:, s, :, :], banks[:, s % 4, :].rearrange("p (k q) -> p k q", q=P)).then_inc(xs_b, 1)

            def high_part(g, s):
                if s % 2:
                    dve.wait_ge(h_ready, since(g, s, STAGED))
                    nc.vector.tensor_copy(x_hi[:, s % STAGED, :, :], xs[:, s, :, :]).then_inc(xhi_b, 1)

            def low_hidden(g, s):
                dve.wait_ge(hi_done, 1 + SLOTS * g + s + 1)
                nc.vector.tensor_tensor(ht_lo[:, s, :], banks[:, HT_T + s % 2, 0:P], ht_hi[:, s, :].bitcast(F32), ALU.subtract).then_inc(lo_done, 1)

            def stage_a(g):
                for s in range(SLOTS):
                    n = SLOTS * g + s
                    dve.wait_ge(h_ready, 1 + n + 1)
                    dve.wait_ge(s_done, 1 + n + 1)
                    dve.wait_ge(t_ready, since(g, s, 2))
                    nc.vector.tensor_tensor(h_sb[:, s % 2, :], s_sb[:, s % 2, :], banks[:, H + s % 2, P:2 * P], ALU.mult).then_inc(h_done, 1)
                    if s + STAGED < SLOTS:
                        high_part(g, s + STAGED)
                    if s:
                        low_hidden(g, s - 1)
                    if out_major:
                        for c in last_pieces(s):
                            split(g, c)
                low_hidden(g, SLOTS - 1)

            def stage_b(g, last):
                if not last and not RESIDENT:
                    for s in range(STAGED):
                        high_part(g + 1, s)
                for s in range(SLOTS):
                    n = SLOTS * g + s
                    dve.wait_ge(y_ready, 1 + n + 1)
                    dve.wait_ge(add_done, 1 + SLOTS * g)
                    nc.vector.tensor_tensor(y_acc[:, s, :], y_acc[:, s, :], banks[:, Y[s % 4], :], ALU.add).then_inc(add_done, 1)
                    if out_major and not last:
                        for c in first_pieces(s):
                            split(g + 1, c)

            for c in range(LAST):
                split(0, c)
            for s in range(1, SLOTS, 2):
                move_tokens(s)
            dve.wait_ge(xs_b, SLOTS // 2)
            for s in range(STAGED):
                high_part(0, s)
            dve.wait_ge(acc_zeroed, SLOTS)
            with dve.Fori(0, G - 1) as g:
                stage_a(g)
                stage_b(g, False)
            stage_a(G - 1)
            stage_b(G - 1, True)
            if x_out is None:
                return
            dve.wait_ge(x_again, 16)
            for b in range(B):
                dve.wait_ge(y_gathered[b], 16 * TOP)
                for k in range(TOP):
                    ins = nc.vector.scalar_tensor_tensor(x_tok[0:M, b, :], y_got[0:M, TOP * b + k, :], gates[0:M, b, k:k + 1], x_tok[0:M, b, :],
                                                         ALU.mult, ALU.add)
                    if k == 0:
                        own.link(ins)
                ins.then_inc(x_done, 1)


def strided_attention(nc, x_in, y_pairs, place, gates, x_mid, ctx_rows, wq, bq, wk, bk, wv, bv, wo, bo, gate, x_out):
    B, M, D = x_in.shape
    P = 128
    H = 16
    HD = D // H
    J = ctx_rows.shape[1] // H
    KD = D // P
    QH = P // HD
    HH = H // 2
    T = B * M
    HT = T // 2
    HB = B // 2
    BJ = HB * J
    ROWS = H * J
    CT = (ROWS + P - 1) // P
    CROWS = [min(P, ROWS - P * t) for t in range(CT)]
    FILLS = HB * CT
    BANK = 512
    EPS = 1e-5
    SCALE = HD ** -0.5

    with ExitStack() as ctx:
        def sb(n, shape, dt=F32):
            return ctx.enter_context(nc.sbuf_tensor("g_" + n, shape, dt))

        def sem(n):
            return nc.alloc_semaphore("g_" + n)

        ctx_t = sb("ctx_t", [P, KD, H, BJ])
        rows = sb("rows", [P, 2, CT, D])
        raw = sb("raw", [P, 2, KD, D])
        wq_hi, wq_lo, wo_hi, wo_lo = (sb(n, [P, KD, D], F32R) for n in ("wq_hi", "wq_lo", "wo_hi", "wo_lo"))
        wk_t, wv_t = (sb(n, [P, KD, D]) for n in ("wk_t", "wv_t"))
        xn_hi = sb("xn_hi", [P, KD, T], F32R)
        xn_lo = sb("xn_lo", [P, KD, T], F32R)
        shared = sb("shared", [P, B * D])
        k_t = sb("k_t", [P, KD, B * J])
        v_t = sb("v_t", [P, KD, B * J])
        q_b = sb("q_b", [P, 2, KD, M])
        k_b = sb("k_b", [P, 2, KD, QH * J])
        v_tb = sb("v_tb", [P, 2, KD, J])
        v_b = sb("v_b", [P, 2, D])
        probs = sb("probs", [P, 2, H * J])
        probs_t = sb("probs_t", [P, H * M])
        s_max = sb("s_max", [P, 2, HH])
        s_sum = sb("s_sum", [P, 2, HH])
        bias = {n: sb("b" + n, [P, KD]) for n in "qkvo"}
        tanh_g = sb("tanh_g", [P, 1])
        eps = sb("eps", [P, 1])
        ident = sb("ident", [P, P])
        stats = sb("stats", [P, B, 6])
        mean_var = sb("mean_var", [P, B, 2])
        std = sb("std", [P, B])
        rstd = sb("rstd", [P, B])
        y_got = [t[0:M, 0:TOP * D].rearrange("p (k d) -> p k d", d=D)
                 for t in (probs[:, :, :].rearrange("p u n -> p (u n)"), probs_t)]
        x_tok = shared[:, :].rearrange("p (b d) -> p b d", d=D)
        q_t = shared[:, 0:KD * T].rearrange("p (k t) -> p k t", t=T)
        y_t = q_t
        x_res = rows[:, :, :, :].rearrange("p s t d -> p (s t) d")[:, 0:B, :]

        banks = ctx.enter_context(nc.psum_tensor("g_banks", [P, 8, BANK], F32))
        S, TP, V, O = 0, 4, 6, 7

        x_loaded = [sem(f"x_loaded{n}") for n in range(2)]
        c_loaded = sem("c_loaded")
        w_loaded = [sem(f"w_loaded{n}") for n in range(4)]
        rows_loaded = [sem(f"rows_loaded{n}") for n in range(2)]
        y_gathered = [sem(f"y_gathered{n}") for n in range(2)]
        mid_done = sem("mid_done")
        mid_stored = sem("mid_stored")
        x_again = sem("x_again")
        x_stored = sem("x_stored")
        const_done = sem("const_done")
        tanh_done = sem("tanh_done")
        var_done = sem("var_done")
        std_done = sem("std_done")
        norm_done = sem("norm_done")
        piece_done = sem("piece_done")
        fill_ready = sem("fill_ready")
        fill_hi = sem("fill_hi")
        fill_done = sem("fill_done")
        q_ready = sem("q_ready")
        q_done = sem("q_done")
        ctx_ready = sem("ctx_ready")
        ctx_done = sem("ctx_done")
        kv_ready = sem("kv_ready")
        kv_done = sem("kv_done")
        qb_done = sem("qb_done")
        kb_done = sem("kb_done")
        vt_done = sem("vt_done")
        s_ready = sem("s_ready")
        sub_done = sem("sub_done")
        exp_done = sem("exp_done")
        p_done = sem("p_done")
        v_ready = sem("v_ready")
        v_done = sem("v_done")
        t_ready = sem("t_ready")
        ta_done = sem("ta_done")
        tb_done = sem("tb_done")
        o_ready = sem("o_ready")
        ohi_done = sem("ohi_done")
        olo_done = sem("olo_done")
        y_ready = sem("y_ready")
        y_done = sem("y_done")
        out_ready = sem("out_ready")
        x_done = sem("x_done")
        held = sem("held")
        chain = sem("chain")
        pool_chain = sem("pool_chain")

        block = ctx.enter_context(nc.Block())

        CTX0, KV0, S0, SUB0, V0, T0, O0 = 4, 4, 2, 2, 2, 5, 2

        PLAIN = 2 * KD
        SPLIT = 2 * KD + B

        @block.sync
        def _(sp):
            def load_weights(n, w):
                sp.dma_start(raw[:, n % 2, :, :], w.rearrange("(c p) d -> p c d", p=P)).then_inc(w_loaded[n], 16)

            def load_rows(b, slot):
                full = P * (CT - 1)
                sp.dma_start(rows[:, slot, 0:CT - 1, :], ctx_rows[b, 0:full, :].rearrange("(t p) d -> p t d", p=P)).then_inc(rows_loaded[slot], 16)
                sp.dma_start(rows[0:CROWS[-1], slot, CT - 1, :], ctx_rows[b, full:ROWS, :]).then_inc(rows_loaded[slot], 16)

            load_weights(0, wk)
            load_rows(0, 0)
            load_weights(1, wv)
            load_rows(1, 1)
            for n, src in zip("qkvo", (bq, bk, bv, bo)):
                sp.dma_start(bias[n][:, :], src.rearrange("(c p) -> p c", p=P), allow_slow_non_contiguous=True).then_inc(c_loaded, 16)
            sp.dma_start(tanh_g[:, :], gate.to_broadcast([P, 1])).then_inc(c_loaded, 16)

            def reload(i):
                for slot in range(2):
                    sp.wait_ge(ctx_ready, 1 + CT * (2 * i + slot + 1))
                    load_rows(2 * i + 2 + slot, slot)

            reload(0)
            for q in range(4):
                sp.dma_start(x_tok[0:M, 2 * q:2 * q + 2, :], x_in[2 * q:2 * q + 2].rearrange("b p d -> p b d")).then_inc(x_loaded[q // 2], 16)
            for i in range(1, B // 2 - 1):
                reload(i)
            for n, w in ((2, wq), (3, wo)):
                sp.wait_ge(piece_done, KD * (n - 1))
                load_weights(n, w)
            sp.wait_ge(ctx_ready, 1 + CT * B)
            sp.wait_ge(mid_stored, 16)
            sp.dma_start(x_res[0:M, :, :], x_mid.rearrange("b p d -> p b d")).then_inc(x_again, 16)
            for b in range(B):
                sp.wait_ge(x_done, b + 1)
                sp.dma_start(x_out[b, :, :], x_res[0:M, b, :]).then_inc(x_stored, 16)
            sp.wait_ge(x_stored, 16 * B)

        def move_context(f):
            t, b = f % CT, f // CT
            n = CROWS[t] // H
            j = J * b + P // H * t
            src = banks[:, f % 4, :].rearrange("p (k q) -> p k q", q=P)[:, :, 0:CROWS[t]].rearrange("p k (j h) -> p k h j", h=H)
            return nc.scalar.copy(ctx_t[:, :, :, j:j + n], src)

        def split_places(n, q, o, x):
            bank = banks[:, n % 4, :]
            if n < KD:
                return q[:, n, :], bank
            if n < KD + B:
                b = n - KD
                return x[:, :, M * b:M * b + M], bank.rearrange("p (k q) -> p k q", q=P)[:, :, 0:M]
            return o[:, n - KD - B, :], bank

        @block.gpsimd
        def _(pool):
            pool.sem_inc(qb_done, 1)
            pool.sem_inc(vt_done, 1)
            nc.gpsimd.memset(ident[:, :], 0.0).then_inc(const_done, 1)
            nc.gpsimd.memset(eps[:, :], EPS).then_inc(const_done, 1)
            nc.gpsimd.memset(k_b[:, :, :, :], 0.0).then_inc(const_done, 1)
            pool.wait_ge(const_done, 3)
            nc.gpsimd.affine_select(out=ident[:, :], in_=ident[:, :], compare_op=ALU.not_equal, fill=1.0, base=0,
                                    pattern=[[-1, P]], channel_multiplier=1).then_inc(const_done, 1)
            for b in range(B):
                if b >= 2:
                    pool.wait_ge(mid_done, b - 1)
                for k in range(TOP):
                    nc.gpsimd.indirect_dma_start(y_got[b % 2][:, k, :], None, y_pairs[:, :],
                                                 bass.IndirectOffsetOnAxis(ap=place[0:M, b, k:k + 1], axis=0)).then_inc(y_gathered[b % 2], 16)
            pool.sem_inc(pool_chain, 1)
            pool.wait_ge(q_done, 2 * KD)
            pool.wait_ge(kv_done, KV0 + 4 * KD)
            pool.sem_inc(held, 1)
            own = Chain(pool, pool_chain)
            with own.loop(B // 2, 4) as i:
                for u in range(2):
                    n = 2 * i + u
                    pool.wait_ge(s_ready, S0 + n - 1)
                    pool.sem_inc(held, 1)
                    own.link(nc.gpsimd.tensor_copy(q_b[:, u, :, :], q_t[:, :, bass.ds(M * n, M)]))
                    pool.sem_inc(qb_done, 1)
                    pool.wait_ge(v_ready, V0 + n - 1)
                    pool.sem_inc(held, 1)
                    own.link(nc.gpsimd.tensor_copy(v_tb[:, u, :, :], v_t[:, :, bass.ds(J * n, J)]))
                    pool.sem_inc(vt_done, 1)

        @block.scalar
        def _(act):
            for s, start in ((ctx_done, CTX0), (kv_done, KV0), (kb_done, 1), (exp_done, 1), (v_done, 1), (ta_done, 1), (ohi_done, 1)):
                act.sem_inc(s, start)
            for n in range(PLAIN):
                act.wait_ge(fill_ready, n + 1)
                nc.scalar.activation((wk_t, wv_t)[n // KD][:, n % KD, :], banks[:, n % 4, :], ACT.Copy).then_inc(piece_done, 1)
            act.wait_ge(c_loaded, 80)
            for half in range(2):
                for f in range(FILLS):
                    act.wait_ge(ctx_ready, 1 + FILLS * half + f + 1)
                    move_context(f).then_inc(ctx_done, 1)
                if half == 1:
                    act.wait_ge(const_done, 3)
                    act.wait_ge(mid_done, B)
                    act.dma_start(x_mid.rearrange("b p d -> p b d"), x_tok[0:M, :, :]).then_inc(mid_stored, 16)
                    act.wait_ge(var_done, 1)
                    nc.scalar.activation(std[0:M, :], mean_var[0:M, :, 1], ACT.Sqrt, bias=eps[0:M, :]).then_inc(std_done, 1)
                    nc.scalar.activation(tanh_g[:, :], tanh_g[:, :], ACT.Tanh).then_inc(tanh_done, 1)
                for n in range(2 * KD):
                    act.wait_ge(kv_ready, 1 + 2 * KD * half + n + 1)
                    dst, b = ((k_t, "k"), (v_t, "v"))[n % 2]
                    nc.scalar.activation(dst[:, n // 2, BJ * half:BJ * half + BJ], banks[:, TP + n % 4, 0:BJ], ACT.Identity,
                                         bias=bias[b][:, n // 2:n // 2 + 1]).then_inc(kv_done, 1)

            for n in range(SPLIT):
                act.wait_ge(fill_ready, PLAIN + n + 1)
                dst, src = split_places(n, wq_hi, wo_hi, xn_hi)
                nc.scalar.activation(dst, src, ACT.Copy).then_inc(fill_hi, 1)

            def spread_keys(n, u):
                act.wait_ge(s_ready, S0 + n - 1)
                for r in range(QH):
                    p = slice(HD * r, HD * r + HD)
                    ins = nc.scalar.copy(k_b[p, u, :, J * r:J * r + J], k_t[p, :, bass.ds(J * n, J)])
                ins.then_inc(kb_done, 1)

            def exponent(n, u):
                act.wait_ge(sub_done, SUB0 + n + 1)
                nc.scalar.activation(probs[0:M, u, :], probs[0:M, u, :], ACT.Exp).then_inc(exp_done, 1)

            def element(n, u, last, ending):
                act.wait_ge(v_ready, V0 + n + 1)
                act.wait_ge(o_ready, O0 + n - 1)
                nc.scalar.activation(v_b[0:J, u, :], banks[0:J, V, :], ACT.Copy).then_inc(v_done, 1)
                for r in (0, 2):
                    act.wait_ge(t_ready, T0 + 4 * n + r + 1)
                    act.wait_ge(o_ready, O0 + n)
                    nc.scalar.activation(probs_t[0:J, 4 * M * r:4 * M * r + 4 * M], banks[0:J, TP, 0:4 * M], ACT.Copy).then_inc(ta_done, 1)
                if not last:
                    exponent(n + 1, (u + 1) % 2)
                if not ending:
                    spread_keys(n + 2, u)
                act.wait_ge(o_ready, O0 + n + 1)
                nc.scalar.activation(xn_hi[:, :, bass.ds(M * n, M)], banks[:, O, 0:KD * M].rearrange("p (k q) -> p k q", q=M),
                                     ACT.Copy).then_inc(ohi_done, 1)

            act.wait_ge(const_done, 3)
            spread_keys(0, 0)
            spread_keys(1, 1)
            exponent(0, 0)
            with act.Fori(0, B // 2 - 1) as i:
                element(2 * i, 0, False, False)
                element(2 * i + 1, 1, False, False)
            element(B - 2, 0, False, True)
            element(B - 1, 1, True, True)
            for n in range(2 * KD):
                half, d = n // KD, n % KD
                act.wait_ge(y_ready, n + 1)
                nc.scalar.activation(y_t[:, d, HT * half:HT * half + HT], banks[:, n % 4, 0:HT], ACT.Identity,
                                     bias=bias["o"][:, d:d + 1]).then_inc(y_done, 1)

        @block.tensor
        def _(pe):
            for s, start in ((ctx_ready, 1), (kv_ready, 1), (s_ready, S0), (v_ready, V0), (t_ready, T0), (o_ready, O0)):
                pe.sem_inc(s, start)
            pe.wait_ge(const_done, 4)

            def turn_weights(n, w, k):
                pe.wait_ge(w_loaded[w], 16)
                for c in range(KD):
                    ins = nc.tensor.transpose(banks[:, n % 4, P * c:P * c + P], raw[:, w % 2, c, P * k:P * k + P], ident[:, :])
                ins.then_inc(fill_ready, 1)

            for n in range(PLAIN):
                if n >= 4:
                    pe.wait_ge(piece_done, n - 3)
                turn_weights(n, n // KD, n % KD)
            pe.wait_ge(piece_done, PLAIN)

            with pe.Fori(0, 2) as half:
                for f in range(FILLS):
                    t, b = f % CT, f // CT
                    pe.wait_ge(rows_loaded[b % 2], 16 * (HB * half + 2 * (b // 2) + 2))
                    pe.wait_ge(ctx_done, CTX0 + FILLS * half + f - 3)
                    pe.sem_inc(held, 1)
                    c = CROWS[t]
                    for k in range(KD):
                        ins = nc.tensor.transpose(banks[:, f % 4, P * k:P * k + c], rows[0:c, b % 2, t, P * k:P * k + P], ident[0:c, 0:c])
                    ins.then_inc(ctx_ready, 1)
                pe.wait_ge(ctx_done, CTX0 + FILLS * (half + 1))
                for n in range(2 * KD):
                    w = (wk_t, wv_t)[n % 2]
                    pe.wait_ge(kv_done, KV0 + 2 * KD * half + n - 3)
                    for k in range(KD):
                        for r in range(QH):
                            h = QH * (n // 2) + r
                            ins = nc.tensor.matmul(banks[HD * r:HD * r + HD, TP + n % 4, 0:BJ], w[:, k, HD * h:HD * h + HD], ctx_t[:, k, h, :],
                                                   start=(k == 0), stop=(k == KD - 1))
                    ins.then_inc(kv_ready, 1)

            pe.wait_ge(kv_done, KV0 + 4 * KD)
            for n in range(SPLIT):
                if n >= 4:
                    pe.wait_ge(fill_done, n - 3)
                if n < KD:
                    turn_weights(n, 2, n)
                elif n < KD + B:
                    b = n - KD
                    pe.wait_ge(norm_done, b + 1)
                    for k in range(KD):
                        ins = nc.tensor.transpose(banks[:, n % 4, P * k:P * k + M], x_tok[0:M, b, P * k:P * k + P], ident[0:M, 0:M])
                    ins.then_inc(fill_ready, 1)
                else:
                    turn_weights(n, 3, n - KD - B)
            pe.wait_ge(fill_done, SPLIT)
            for n in range(2 * KD):
                half, m = n // KD, n % KD
                if n >= 4:
                    pe.wait_ge(q_done, n - 3)
                t = slice(HT * half, HT * half + HT)
                c = slice(P * m, P * m + P)
                for k in range(KD):
                    ins = three(nc, banks[:, TP + n % 4, 0:HT], wq_hi[:, k, c], wq_lo[:, k, c], xn_hi[:, k, t], xn_lo[:, k, t], k == 0, k == KD - 1)
                ins.then_inc(q_ready, 1)
            pe.wait_ge(q_done, 2 * KD)

            def scores(n, u):
                pe.wait_ge(qb_done, 1 + n + 1)
                pe.wait_ge(kb_done, 1 + n + 1)
                pe.wait_ge(sub_done, SUB0 + n - 1)
                for c in range(KD):
                    at = QH * J * (c % 2)
                    ins = nc.tensor.matmul(banks[0:M, S + 2 * u + c // 2, at:at + QH * J], q_b[:, u, c, :], k_b[:, u, c, :], start=True, stop=True)
                ins.then_inc(s_ready, 1)

            def element(n, u, last):
                if not last:
                    scores(n + 1, (u + 1) % 2)
                pe.wait_ge(vt_done, 1 + n + 1)
                pe.wait_ge(v_done, 1 + n)
                pe.sem_inc(held, 1)
                for c in range(KD):
                    ins = nc.tensor.transpose(banks[0:J, V, P * c:P * c + P], v_tb[:, u, c, :], ident[:, :])
                ins.then_inc(v_ready, 1)
                pe.wait_ge(p_done, 1 + n + 1)
                for r in range(4):
                    pe.wait_ge((ta_done, tb_done)[r % 2], 1 + 2 * n + r // 2)
                    pe.sem_inc(held, 1)
                    for x in range(4):
                        h = 4 * r + x
                        ins = nc.tensor.transpose(banks[0:J, TP + r % 2, M * x:M * x + M], probs[0:M, u, J * h:J * h + J], ident[0:M, 0:M])
                    ins.then_inc(t_ready, 1)
                pe.wait_ge(ta_done, 1 + 2 * n + 2)
                pe.wait_ge(tb_done, 1 + 2 * n + 2)
                pe.wait_ge(v_done, 1 + n + 1)
                pe.wait_ge(olo_done, 1 + n)
                pe.sem_inc(held, 1)
                for h in range(H):
                    p, c = HD * (h % QH), M * (h // QH)
                    ins = nc.tensor.matmul(banks[p:p + HD, O, c:c + M], v_b[0:J, u, HD * h:HD * h + HD], probs_t[0:J, M * h:M * h + M],
                                           start=True, stop=True)
                ins.then_inc(o_ready, 1)

            scores(0, 0)
            with pe.Fori(0, B // 2 - 1) as i:
                element(2 * i, 0, False)
                element(2 * i + 1, 1, False)
            element(B - 2, 0, False)
            element(B - 1, 1, True)
            pe.wait_ge(olo_done, 1 + B)
            for n in range(2 * KD):
                half, d = n // KD, n % KD
                if n >= 4:
                    pe.wait_ge(y_done, n - 3)
                t = slice(HT * half, HT * half + HT)
                c = slice(P * d, P * d + P)
                for k in range(KD):
                    ins = three(nc, banks[:, n % 4, 0:HT], wo_hi[:, k, c], wo_lo[:, k, c], xn_hi[:, k, t], xn_lo[:, k, t], k == 0, k == KD - 1)
                ins.then_inc(y_ready, 1)
            for b in range(B):
                pe.wait_ge(y_done, KD * (1 + b // HB))
                if b >= 4:
                    pe.wait_ge(x_done, b - 3)
                for k in range(KD):
                    ins = nc.tensor.transpose(banks[0:M, 4 + b % 4, P * k:P * k + P], y_t[:, k, M * b:M * b + M], ident[:, :])
                ins.then_inc(out_ready, 1)

        @block.vector
        def _(dve):
            for s, start in ((sub_done, SUB0), (p_done, 1), (tb_done, 1), (olo_done, 1), (chain, 1)):
                dve.sem_inc(s, start)
            own = Chain(dve, chain)
            for b in range(B):
                if b % HB == 0:
                    dve.wait_ge(x_loaded[b // HB], 32)
                dve.wait_ge(y_gathered[b % 2], 16 * TOP * (b // 2 + 1))
                for k in range(TOP):
                    own.link(nc.vector.scalar_tensor_tensor(x_tok[0:M, b, :], y_got[b % 2][:, k, :], gates[0:M, b, k:k + 1], x_tok[0:M, b, :],
                                                            ALU.mult, ALU.add))
                dve.sem_inc(mid_done, 1)
                ins = nc.vector.bn_stats(stats[0:M, b, :], x_tok[0:M, b, :])
            own.link(ins)
            for b in range(B):
                ins = nc.vector.bn_aggr(mean_var[0:M, b, :], stats[0:M, b, :])
            ins.then_inc(var_done, 1)
            dve.wait_ge(std_done, 1)
            own.link(nc.vector.reciprocal(rstd[0:M, :], std[0:M, :]))
            dve.wait_ge(mid_stored, 16)
            for b in range(B):
                nc.vector.tensor_scalar(x_tok[0:M, b, :], x_tok[0:M, b, :], mean_var[0:M, b, 0:1], rstd[0:M, b:b + 1],
                                        ALU.subtract, ALU.mult).then_inc(norm_done, 1)
            for n in range(SPLIT):
                dve.wait_ge(fill_hi, n + 1)
                dst, src = split_places(n, wq_lo, wo_lo, xn_lo)
                hi, _ = split_places(n, wq_hi, wo_hi, xn_hi)
                nc.vector.tensor_tensor(dst, src, hi.bitcast(F32), ALU.subtract).then_inc(fill_done, 1)
            dve.wait_ge(c_loaded, 80)
            for n in range(2 * KD):
                half, m = n // KD, n % KD
                dve.wait_ge(q_ready, n + 1)
                nc.vector.tensor_scalar(q_t[:, m, HT * half:HT * half + HT], banks[:, TP + n % 4, 0:HT], bias["q"][:, m:m + 1], SCALE,
                                        ALU.add, ALU.mult).then_inc(q_done, 1)

            def rowwise(t):
                return t[0:M, :, :].unsqueeze(3).to_broadcast([M, 2, HH, J])

            def lower(n, u):
                s = banks[0:M, S + 2 * u:S + 2 * u + 2, 0:HH * J].rearrange("p r (h j) -> p r h j", j=J)
                dve.wait_ge(s_ready, S0 + n + 1)
                own.link(nc.vector.tensor_reduce(s_max[0:M, :, :], s, axis=AX.X, op=ALU.max))
                dve.wait_ge(t_ready, T0 + 4 * (n - 1))
                nc.vector.tensor_tensor(probs[0:M, u, :].rearrange("p (r h j) -> p r h j", h=HH, j=J), s, rowwise(s_max), ALU.subtract).then_inc(sub_done, 1)

            def element(n, u, last):
                p = probs[0:M, u, :].rearrange("p (r h j) -> p r h j", h=HH, j=J)
                dve.wait_ge(exp_done, 1 + n + 1)
                own.link(nc.vector.tensor_reduce(s_sum[0:M, :, :], p, axis=AX.X, op=ALU.add))
                own.link(nc.vector.reciprocal(s_sum[0:M, :, :], s_sum[0:M, :, :]))
                nc.vector.tensor_tensor(p, p, rowwise(s_sum), ALU.mult).then_inc(p_done, 1)
                if not last:
                    lower(n + 1, (u + 1) % 2)
                for r in (1, 3):
                    dve.wait_ge(t_ready, T0 + 4 * n + r + 1)
                    dve.wait_ge(o_ready, O0 + n)
                    nc.vector.tensor_copy(probs_t[0:J, 4 * M * r:4 * M * r + 4 * M], banks[0:J, TP + 1, 0:4 * M]).then_inc(tb_done, 1)
                dve.wait_ge(ohi_done, 1 + n + 1)
                t = bass.ds(M * n, M)
                nc.vector.tensor_tensor(xn_lo[:, :, t], banks[:, O, 0:KD * M].rearrange("p (k q) -> p k q", q=M), xn_hi[:, :, t].bitcast(F32),
                                        ALU.subtract).then_inc(olo_done, 1)

            lower(0, 0)
            with own.loop(B // 2 - 1, 6) as i:
                element(2 * i, 0, False)
                element(2 * i + 1, 1, False)
            element(B - 2, 0, False)
            element(B - 1, 1, True)
            dve.wait_ge(tanh_done, 1)
            dve.wait_ge(x_again, 16)
            for b in range(B):
                dve.wait_ge(out_ready, b + 1)
                nc.vector.scalar_tensor_tensor(x_res[0:M, b, :], banks[0:M, 4 + b % 4, :], tanh_g[0:M, 0:1], x_res[0:M, b, :],
                                               ALU.mult, ALU.add).then_inc(x_done, 1)


def flamingo_layers(nc, x, ctx_1024, mask_BxS2_bk0, g_xattn, g_ffn,
                    a_ln_x_g, a_ln_x_b, a_ln_l_g, a_ln_l_b, a_wq, a_wkv, a_wout, a_ln_o_g, a_ln_o_b,
                    f_router_w, f_router_b, f_w1, f_w3, f_w2,
                    g_wq, g_bq, g_wk, g_bk, g_wv, g_bv, g_wo, g_bo,
                    m_wg, m_w1, m_w2, m_w3, out):
    B, M, D = x.shape
    P = 128
    x1, x2, x3 = (nc.dram_tensor(f"x_after_{n}", x.shape, F32, kind="Internal").ap() for n in range(1, 4))
    y1, y2 = (nc.dram_tensor(f"y_{n}", [slots(B * M, w.shape[0]) * P, D], F32, kind="Internal").ap() for n, w in enumerate((f_w1, m_w1)))
    with nc.cleanup_on_exit():
        perceiver_attention(nc, ctx_1024, x, mask_BxS2_bk0, a_ln_x_g, a_ln_x_b, a_ln_l_g, a_ln_l_b, a_wq, a_wkv, a_wout,
                            a_ln_o_g, a_ln_o_b, g_xattn[0:1], x1)
    with ExitStack() as ctx:
        place = ctx.enter_context(nc.sbuf_tensor("place", [P, B, TOP], mybir.dt.uint32))
        gates = ctx.enter_context(nc.sbuf_tensor("gates", [P, B, TOP], F32))
        with nc.cleanup_on_exit():
            gated_experts(nc, "f", x1, f_router_w, f_router_b, f_w1, f_w3, f_w2, False, g_ffn[0:1], place, gates, y1, None)
        with nc.cleanup_on_exit():
            strided_attention(nc, x1, y1, place, gates, x2, ctx_1024, g_wq, g_bq, g_wk, g_bk, g_wv, g_bv, g_wo, g_bo, g_xattn[1:2], x3)
        with nc.cleanup_on_exit():
            gated_experts(nc, "m", x3, m_wg, None, m_w1, m_w2, m_w3, True, g_ffn[1:2], place, gates, y2, out)


_INS = ["x", "ctx_1024", "mask_BxS2_bk0", "g_xattn", "g_ffn",
        "L0_xattn_ln_x_g", "L0_xattn_ln_x_b", "L0_xattn_ln_l_g", "L0_xattn_ln_l_b", "L0_xattn_Wq", "L0_xattn_Wkv",
        "L0_xattn_Wout", "L0_xattn_ln_o_g", "L0_xattn_ln_o_b",
        "L0_ffn_router_w", "L0_ffn_router_b", "L0_ffn_w1", "L0_ffn_w3", "L0_ffn_w2",
        "L1_xattn_Wq", "L1_xattn_bq", "L1_xattn_Wk", "L1_xattn_bk", "L1_xattn_Wv", "L1_xattn_bv", "L1_xattn_Wo", "L1_xattn_bo",
        "L1_ffn_Wg", "L1_ffn_W1", "L1_ffn_W2", "L1_ffn_W3"]


def kernel(**inputs):
    import numpy as _np
    import concourse.bacc as _bacc
    from concourse import mybir as _mybir
    from concourse.bass_utils import run_bass_kernel_spmd as _run

    nc = _bacc.Bacc("TRN2", target_bir_lowering=False, num_devices=1, dynamic_dma_scratch_size=4096)
    arrays, args = {}, []
    for name in _INS:
        a = _np.ascontiguousarray(inputs[name])
        arrays[name] = a
        args.append(nc.dram_tensor(name, a.shape, _mybir.dt.from_np(a.dtype), kind="ExternalInput").ap())
    args.append(nc.dram_tensor("out", inputs["x"].shape, F32, kind="ExternalOutput").ap())
    flamingo_layers(nc, *args)
    r = _run(nc, [arrays], core_ids=[0])
    return r.results[0]["out"]
```
